# Optimizing a Trainium2 kernel written in Bass

```python
import numpy as np
import jax
import jax.numpy as jnp

def _softmax(x, axis=-1):
    return jax.nn.softmax(x, axis=axis)

def _gelu(x):
    return jax.nn.gelu(x, approximate=True)

def _silu(x):
    return jax.nn.silu(x)

def _sigmoid(x):
    return jax.nn.sigmoid(x)

def _layernorm(x, axis=-1, eps=1e-05):
    m = jnp.mean(x, axis=axis, keepdims=True)
    v = jnp.var(x, axis=axis, keepdims=True)
    return (x - m) / jnp.sqrt(v + eps)

def _scatter_add(tgt, idx, src, axis=0):
    return tgt.at[idx].add(src)

def _segment_sum(src, seg, n):
    return jax.ops.segment_sum(src, seg, n)
kernel_name = 'mk_xattn_ffn_d2_seqx_r8_82a95c'

def setup_inputs(seed: int=0):
    np.random.seed(seed)
    _w = jnp.asarray

    def _rec_inputs():
        import jax
        import jax.numpy as jnp
        _rk = jax.random.key(seed)
        x = 0.5 + 0.2887 * jax.random.normal(jax.random.fold_in(_rk, 1), (4, 256, 256), jnp.float32)
        _lenS = 256 - jax.random.randint(jax.random.fold_in(_rk, 7), (4,), 0, max(1, 256 // 4) + 1, jnp.int32)
        _lenS2 = 256 - jax.random.randint(jax.random.fold_in(_rk, 8), (4,), 0, max(1, 256 // 4) + 1, jnp.int32)
        _ctx_512P = jax.random.normal(jax.random.fold_in(_rk, 11), (4, 16, 64), jnp.float32)
        _ctx_512c = jax.random.dirichlet(jax.random.fold_in(_rk, 511), 0.3 * jnp.ones((16,), jnp.float32), (4, 256))
        _ctx_512t = jnp.einsum('bsk,bkd->bsd', _ctx_512c, _ctx_512P)
        _ctx_512t = _ctx_512t * jax.lax.rsqrt(jnp.mean(jnp.square(_ctx_512t)) + 1e-12) * 0.953939
        ctx_512 = -0.000392918 + 0.999932 * (_ctx_512t + 0.3 * jax.random.normal(jax.random.fold_in(_rk, 611), (4, 256, 64), jnp.float32))
        return (x, ctx_512)
    x, ctx_512 = _rec_inputs()

    def _L0_xattn_setup():
        import jax, jax.numpy as jnp
        import numpy as np
        B, N, D = (16, 256, 64)
        H = 4
        TOP_K_RATIO = 0.3
        key = jax.random.key(seed)
        k1, k2, k3, k4 = jax.random.split(key, 4)
        h = jax.random.normal(k1, (B, N, D), dtype=jnp.float32)
        adj_raw = jax.random.uniform(k2, (B, N, N), dtype=jnp.float32)
        lim = 1.0 / np.sqrt(D)
        Wq = jax.random.uniform(k3, (D, D), minval=-lim, maxval=lim, dtype=jnp.float32)
        Wk = jax.random.uniform(k4, (D, D), minval=-lim, maxval=lim, dtype=jnp.float32)
        gamma_raw = jnp.float32(-0.85)
        return {'h': h, 'adj_raw': adj_raw, 'Wq': Wq, 'Wk': Wk, 'gamma_raw': gamma_raw}
    _L0_xattn_all = _L0_xattn_setup()
    _L0_xattn_in = {k: v for k, v in _L0_xattn_all.items() if k in ('Wq', 'Wk', 'gamma_raw')}
    del _L0_xattn_all

    def _L0_ffn_setup():
        import jax, jax.numpy as jnp
        import numpy as np
        ALPHA = 1.702
        LIMIT = 7.0
        TOP_K = 4
        B, S, H = (1, 128, 256)
        E, D = (16, 256)
        key = jax.random.key(seed)
        ks = jax.random.split(key, 7)
        s = 0.02
        return {'hidden_states': jax.random.normal(ks[0], (B, S, H), dtype=jnp.float32), 'router_weight': jax.random.normal(ks[1], (E, H), dtype=jnp.float32) * s, 'router_bias': jax.random.normal(ks[2], (E,), dtype=jnp.float32) * s, 'gate_up_proj': jax.random.normal(ks[3], (E, H, 2 * D), dtype=jnp.float32) * s, 'gate_up_proj_bias': jax.random.normal(ks[4], (E, 2 * D), dtype=jnp.float32) * s, 'down_proj': jax.random.normal(ks[5], (E, D, H), dtype=jnp.float32) * s, 'down_proj_bias': jax.random.normal(ks[6], (E, H), dtype=jnp.float32) * s}
    _L0_ffn_all = _L0_ffn_setup()
    _L0_ffn_in = {k: v for k, v in _L0_ffn_all.items() if k in ('router_weight', 'router_bias', 'gate_up_proj', 'gate_up_proj_bias', 'down_proj', 'down_proj_bias')}
    del _L0_ffn_all

    def _L1_xattn_setup():
        import jax, jax.numpy as jnp
        import numpy as np
        B, S, H, NH, L = (2, 256, 256, 16, 64)
        HD = H // NH
        key = jax.random.key(seed)
        k1, k2, k3, k4, k5 = jax.random.split(key, 5)
        scale = 0.02
        return {'q': jax.random.normal(k1, (B, S, H), dtype=jnp.float32), 'latent_kv': jax.random.normal(k2, (B, S, L), dtype=jnp.float32), 'Wq': jax.random.normal(k3, (H, H), dtype=jnp.float32) * scale, 'Wkv_expand': jax.random.normal(k4, (2 * H, L), dtype=jnp.float32) * scale, 'Wout': jax.random.normal(k5, (H, H), dtype=jnp.float32) * scale}
    _L1_xattn_all = _L1_xattn_setup()
    _L1_xattn_in = {k: v for k, v in _L1_xattn_all.items() if k in ('Wq', 'Wkv_expand', 'Wout')}
    del _L1_xattn_all

    def _L1_ffn_setup():
        import jax, jax.numpy as jnp
        import numpy as np
        EPS = 1e-06
        K_STEPS = 4
        USE_GATING = True

        def layer_norm(x, gamma, beta):
            mu = jnp.mean(x, axis=-1, keepdims=True)
            var = jnp.mean(jnp.square(x - mu), axis=-1, keepdims=True)
            return (x - mu) * jax.lax.rsqrt(var + EPS) * gamma + beta
        key = jax.random.key(seed)
        B, L, D, H = (4, 512, 256, 1024)
        ks = jax.random.split(key, 16)
        s = 0.02
        return {'x': jax.random.normal(ks[0], (B, L, D), dtype=jnp.float32), 'in_gamma': jnp.ones((D,), jnp.float32), 'in_beta': jnp.zeros((D,), jnp.float32), 'agg_w': jax.random.normal(ks[1], (D, D), jnp.float32) * s, 'agg_b': jnp.zeros((D,), jnp.float32), 'pn_gamma': jnp.ones((D,), jnp.float32), 'pn_beta': jnp.zeros((D,), jnp.float32), 'd1_w': jax.random.normal(ks[2], (D, H), jnp.float32) * s, 'd1_b': jnp.zeros((H,), jnp.float32), 'd2_w': jax.random.normal(ks[3], (H, D), jnp.float32) * s, 'd2_b': jnp.zeros((D,), jnp.float32), 'bc_w': jax.random.normal(ks[4], (D, D), jnp.float32) * s, 'bc_b': jnp.zeros((D,), jnp.float32), 'gate_w': jax.random.normal(ks[5], (D, D), jnp.float32) * s, 'gate_b': jnp.zeros((D,), jnp.float32), 'out_gamma': jnp.ones((D,), jnp.float32), 'out_beta': jnp.zeros((D,), jnp.float32)}
    _L1_ffn_all = _L1_ffn_setup()
    _L1_ffn_in = {k: v for k, v in _L1_ffn_all.items() if k in ('in_gamma', 'in_beta', 'agg_w', 'agg_b', 'pn_gamma', 'pn_beta', 'd1_w', 'd1_b', 'd2_w', 'd2_b', 'bc_w', 'bc_b', 'gate_w', 'gate_b', 'out_gamma', 'out_beta')}
    del _L1_ffn_all
    return {'x': x, 'ctx_512': ctx_512, 'L0_xattn_Wq': _L0_xattn_in['Wq'], 'L0_xattn_Wk': _L0_xattn_in['Wk'], 'L0_xattn_gamma_raw': _L0_xattn_in['gamma_raw'], 'L0_ffn_router_weight': _L0_ffn_in['router_weight'], 'L0_ffn_router_bias': _L0_ffn_in['router_bias'], 'L0_ffn_gate_up_proj': _L0_ffn_in['gate_up_proj'], 'L0_ffn_gate_up_proj_bias': _L0_ffn_in['gate_up_proj_bias'], 'L0_ffn_down_proj': _L0_ffn_in['down_proj'], 'L0_ffn_down_proj_bias': _L0_ffn_in['down_proj_bias'], 'L1_xattn_Wq': _L1_xattn_in['Wq'], 'L1_xattn_Wkv_expand': _L1_xattn_in['Wkv_expand'], 'L1_xattn_Wout': _L1_xattn_in['Wout'], 'L1_ffn_in_gamma': _L1_ffn_in['in_gamma'], 'L1_ffn_in_beta': _L1_ffn_in['in_beta'], 'L1_ffn_agg_w': _L1_ffn_in['agg_w'], 'L1_ffn_agg_b': _L1_ffn_in['agg_b'], 'L1_ffn_pn_gamma': _L1_ffn_in['pn_gamma'], 'L1_ffn_pn_beta': _L1_ffn_in['pn_beta'], 'L1_ffn_d1_w': _L1_ffn_in['d1_w'], 'L1_ffn_d1_b': _L1_ffn_in['d1_b'], 'L1_ffn_d2_w': _L1_ffn_in['d2_w'], 'L1_ffn_d2_b': _L1_ffn_in['d2_b'], 'L1_ffn_bc_w': _L1_ffn_in['bc_w'], 'L1_ffn_bc_b': _L1_ffn_in['bc_b'], 'L1_ffn_gate_w': _L1_ffn_in['gate_w'], 'L1_ffn_gate_b': _L1_ffn_in['gate_b'], 'L1_ffn_out_gamma': _L1_ffn_in['out_gamma'], 'L1_ffn_out_beta': _L1_ffn_in['out_beta']}

def reference(x, ctx_512, L0_xattn_Wq, L0_xattn_Wk, L0_xattn_gamma_raw, L0_ffn_router_weight, L0_ffn_router_bias, L0_ffn_gate_up_proj, L0_ffn_gate_up_proj_bias, L0_ffn_down_proj, L0_ffn_down_proj_bias, L1_xattn_Wq, L1_xattn_Wkv_expand, L1_xattn_Wout, L1_ffn_in_gamma, L1_ffn_in_beta, L1_ffn_agg_w, L1_ffn_agg_b, L1_ffn_pn_gamma, L1_ffn_pn_beta, L1_ffn_d1_w, L1_ffn_d1_b, L1_ffn_d2_w, L1_ffn_d2_b, L1_ffn_bc_w, L1_ffn_bc_b, L1_ffn_gate_w, L1_ffn_gate_b, L1_ffn_out_gamma, L1_ffn_out_beta):
    import jax
    import jax.numpy as jnp

    def _L0_xattn_ref(h, adj_raw, Wq, Wk, gamma_raw):
        import jax, jax.numpy as jnp
        import numpy as np
        B, N, D = (16, 256, 64)
        H = 4
        TOP_K_RATIO = 0.3
        b, n, dm = h.shape
        d = dm // H
        Q = (h @ Wq.T).reshape(b, n, H, d).transpose(0, 2, 1, 3)
        K = (h @ Wk.T).reshape(b, n, H, d).transpose(0, 2, 1, 3)
        sim = jnp.einsum('bhnd,bhmd->bnm', Q, K) / (jnp.sqrt(jnp.float32(d)) * H)
        k = max(1, int(n * TOP_K_RATIO))
        topk_vals = jax.lax.top_k(sim, k)[0]
        threshold = topk_vals[:, :, -1:]
        sparse_mask = (sim >= threshold).astype(sim.dtype)
        A_learned = jax.nn.sigmoid(sim) * sparse_mask
        A_learned = (A_learned + jnp.swapaxes(A_learned, -1, -2)) * 0.5
        gamma = jax.nn.sigmoid(gamma_raw)
        return (1.0 - gamma) * adj_raw + gamma * A_learned

    def _L0_ffn_ref(hidden_states, router_weight, router_bias, gate_up_proj, gate_up_proj_bias, down_proj, down_proj_bias):
        import jax, jax.numpy as jnp
        import numpy as np
        ALPHA = 1.702
        LIMIT = 7.0
        TOP_K = 4
        B, S, H = (1, 128, 256)
        E, D = (16, 256)
        batch, seq, hdim = hidden_states.shape
        x = hidden_states.reshape(-1, hdim)
        T = x.shape[0]
        logits = x @ router_weight.T + router_bias
        top_val, top_idx = jax.lax.top_k(logits, TOP_K)
        top_val = jax.nn.softmax(top_val, axis=-1)
        router_scores = jnp.zeros_like(logits).at[jnp.arange(T)[:, None], top_idx].set(top_val)
        gate_up = jnp.einsum('th,ehd->etd', x, gate_up_proj) + gate_up_proj_bias[:, None, :]
        gate = gate_up[..., ::2]
        up = gate_up[..., 1::2]
        gate = jnp.minimum(gate, LIMIT)
        up = jnp.clip(up, -LIMIT, LIMIT)
        glu = gate * jax.nn.sigmoid(gate * ALPHA)
        out = jnp.einsum('etd,edh->eth', (up + 1.0) * glu, down_proj) + down_proj_bias[:, None, :]
        out = out * router_scores.T[:, :, None]
        out = out.sum(axis=0)
        return out.reshape(batch, seq, hdim)

    def _L1_xattn_ref(q, latent_kv, Wq, Wkv_expand, Wout):
        import jax, jax.numpy as jnp
        import numpy as np
        B, S, H, NH, L = (2, 256, 256, 16, 64)
        HD = H // NH
        b, sq, _ = q.shape
        sk = latent_kv.shape[1]
        qp = q @ Wq.T
        kv = latent_kv @ Wkv_expand.T
        k, v = jnp.split(kv, 2, axis=-1)
        qh = qp.reshape(b, sq, NH, HD).transpose(0, 2, 1, 3)
        kh = k.reshape(b, sk, NH, HD).transpose(0, 2, 1, 3)
        vh = v.reshape(b, sk, NH, HD).transpose(0, 2, 1, 3)
        inv_sqrt_d = 1.0 / jnp.sqrt(jnp.float32(HD))
        scores = jnp.einsum('bhqd,bhkd->bhqk', qh, kh) * inv_sqrt_d
        causal = jnp.tril(jnp.ones((sq, sk), dtype=bool))
        scores = jnp.where(causal, scores, jnp.finfo(scores.dtype).min)
        attn = jax.nn.softmax(scores, axis=-1)
        out = jnp.einsum('bhqk,bhkd->bhqd', attn, vh)
        out = out.transpose(0, 2, 1, 3).reshape(b, sq, H)
        return out @ Wout.T

    def _L1_ffn_ref(x, in_gamma, in_beta, agg_w, agg_b, pn_gamma, pn_beta, d1_w, d1_b, d2_w, d2_b, bc_w, bc_b, gate_w, gate_b, out_gamma, out_beta):
        import jax, jax.numpy as jnp
        import numpy as np
        EPS = 1e-06
        K_STEPS = 4
        USE_GATING = True

        def layer_norm(x, gamma, beta):
            mu = jnp.mean(x, axis=-1, keepdims=True)
            var = jnp.mean(jnp.square(x - mu), axis=-1, keepdims=True)
            return (x - mu) * jax.lax.rsqrt(var + EPS) * gamma + beta
        x_norm = layer_norm(x, in_gamma, in_beta)
        thought = x_norm[:, -1, :] @ agg_w + agg_b
        for _ in range(K_STEPS):
            t = layer_norm(thought, pn_gamma, pn_beta)
            t = jax.nn.gelu(t @ d1_w + d1_b, approximate=False)
            thought = thought + (t @ d2_w + d2_b)
        broadcast = (thought @ bc_w + bc_b)[:, None, :]
        if USE_GATING:
            gate = jax.nn.sigmoid(x @ gate_w + gate_b)
            out = x + gate * broadcast
        else:
            out = x + broadcast
        return layer_norm(out, out_gamma, out_beta)
    x = x + _L0_xattn_ref(ctx_512, _layernorm(x, axis=-1), L0_xattn_Wq, L0_xattn_Wk, L0_xattn_gamma_raw)
    x = x + _L0_ffn_ref(_layernorm(x, axis=-1), L0_ffn_router_weight, L0_ffn_router_bias, L0_ffn_gate_up_proj, L0_ffn_gate_up_proj_bias, L0_ffn_down_proj, L0_ffn_down_proj_bias)
    x = x + _L1_xattn_ref(_layernorm(x, axis=-1), ctx_512, L1_xattn_Wq, L1_xattn_Wkv_expand, L1_xattn_Wout)
    x = x + _L1_ffn_ref(_layernorm(x, axis=-1), L1_ffn_in_gamma, L1_ffn_in_beta, L1_ffn_agg_w, L1_ffn_agg_b, L1_ffn_pn_gamma, L1_ffn_pn_beta, L1_ffn_d1_w, L1_ffn_d1_b, L1_ffn_d2_w, L1_ffn_d2_b, L1_ffn_bc_w, L1_ffn_bc_b, L1_ffn_gate_w, L1_ffn_gate_b, L1_ffn_out_gamma, L1_ffn_out_beta)
    return x

_drawn_inputs = setup_inputs


def setup_inputs(seed=0):
    import zlib

    import numpy as np

    out = dict(_drawn_inputs(seed))
    spreads = {'L1_ffn_in_gamma': (1.0, 0.6),
     'L1_ffn_in_beta': (0.0, 0.8),
     'L1_ffn_agg_b': (0.0, 0.525),
     'L1_ffn_pn_gamma': (1.0, 0.6),
     'L1_ffn_pn_beta': (0.0, 0.8),
     'L1_ffn_d1_b': (0.0, 0.612),
     'L1_ffn_d2_b': (0.0, 0.1),
     'L1_ffn_bc_b': (0.0, 0.32),
     'L1_ffn_gate_b': (0.0, 0.8),
     'L1_ffn_out_gamma': (1.0, 0.2),
     'L1_ffn_out_beta': (0.0, 0.1)}
    factors = {'L0_ffn_router_bias': 8.0,
     'L0_ffn_gate_up_proj_bias': 27.735,
     'L0_ffn_down_proj_bias': 5.694,
     'L1_xattn_Wq': 64.0,
     'L1_ffn_gate_w': 6.193}
    for name, (base, spread) in spreads.items():
        noise = np.random.default_rng([zlib.crc32(name.encode()), seed]).standard_normal(out[name].shape)
        drawn = base * np.exp(spread * noise) if base else spread * noise
        out[name] = jnp.asarray(drawn.astype(out[name].dtype))
    for name, factor in factors.items():
        out[name] = (out[name] * factor).astype(out[name].dtype)
    return out
```

```python
from contextlib import ExitStack

import concourse.bass as bass
from concourse import mybir

F32 = mybir.dt.float32
F16 = mybir.dt.float16
BF16 = mybir.dt.bfloat16
ALU = mybir.AluOpType
ACT = mybir.ActivationFunctionType
AXX = mybir.AxisListType.X

P = 128
NB = 4
SEQ = 256
D = 256
KT = D // P
NT = NB * SEQ // P
HT = NT // 2
HC = HT * P
CD = 64
TOPK = max(1, int(SEQ * 0.3))
NE = 16
NTOP = 4
NH = 16
HD = D // NH
VW = HD + 1
WC = KT * 2 * D + KT * D
WS = 64.0
GLIM = 7.0
ALPHA = 1.702
KS = 16.0
HID = 4 * D
STEPS = 4
NEG = -1e30


def chip_program(nc, a):
    with ExitStack() as ctx:
        def sb(name, shape, dt=F32):
            return ctx.enter_context(nc.sbuf_tensor(name, shape, dt))

        def sem(name):
            return ctx.enter_context(nc.semaphore(name))

        psum = [ctx.enter_context(nc.psum_tensor(f"bank{i}", [P, 512], F32)) for i in range(8)]

        x = sb("x", [P, NT, D])
        xn = sb("xn", [P, HT, D])
        ctx3 = sb("ctx3", [P, 3, NB * SEQ])
        ctxT, qT0, kT0 = (ctx3[0:CD, i] for i in range(3))
        wqk0 = sb("wqk0", [CD, 2 * CD])
        simwork = sb("simwork", [P, 2, NT, SEQ])
        sim, work = simwork[:, 0], simwork[:, 1]
        sig = sb("sig", [P, NT, SEQ])
        top = sb("top", [P, NT, 8])
        bn = sb("bn", [P, NT, 6])
        mv = sb("mv", [P, NT, 2])
        vare = sb("vare", [P, NT])
        rstd = sb("rstd", [P, NT])
        mhalf = sb("mhalf", [P, NT])
        gam = sb("gam", [P, 4])
        lna = sb("lna", [P, NT])
        lnc = sb("lnc", [P, NT])
        ident = sb("ident", [P, P])
        identb = sb("identb", [P, P], BF16)
        maskb = sb("maskb", [P, 2, P], BF16)
        neg = sb("neg", [P, 2, P], F16)
        pick = sb("pick", [P, NH], F16)
        rbias = sb("rbias", [P, NE])
        gub = sb("gub", [P, NE, 4])
        gub64 = sb("gub64", [P, NE, 2])
        ub1 = sb("ub1", [P, NE, 2])
        tri = sb("tri", [P, NE * NE])
        rw = sb("rw", [P, KT, NE])
        bdown = sb("bdown", [NE, D])
        stage2 = sb("stage2", [P, 2, WC])
        stage = [stage2[:, i] for i in range(2)]
        w16 = sb("w16", [P, NE, 2 * WC], F16)
        xhi = sb("xhi", [P, KT, HC], F16)
        xlo = sb("xlo", [P, KT, HC], F16)
        lg = sb("lg", [P, HT, NE])
        rank = sb("rank", [P, HT, NE])
        rex = sb("rex", [P, HT, NE])
        rmx = sb("rmx", [P, HT])
        rsm = sb("rsm", [P, HT])
        sc = sb("sc", [P, HT, NE])
        sc64 = sb("sc64", [P, HT, NE])
        gbuf = sb("gbuf", [P, 2, HC])
        tbuf = sb("tbuf", [P, 2, HC])
        ubuf = sb("ubuf", [P, 2, HC])
        hhi = sb("hhi", [P, 2, HC], F16)
        hlo = sb("hlo", [P, 2, HC], F16)
        kst = sb("kst", [P, NH // 2, NB * SEQ], F16)
        vals = sb("vals", [P, 2 * NB, NH * VW])
        mx = sb("mx", [P, NB, NH])
        rs = sb("rs", [P, 2, NB])
        consts = gbuf[:, 0, :]
        maskf = gbuf[:, 0, 0:2 * P].rearrange("p (a c) -> p a c", a=2)
        negf = gbuf[:, 0, 2 * P:4 * P].rearrange("p (a c) -> p a c", a=2)
        pickf = gbuf[:, 1, 0:NH]
        wk_rep = tbuf[0:CD].rearrange("p a c -> p (a c)")
        wv = ubuf[0:CD, 0, 0:D]
        khi = hhi
        xT = ubuf
        cmp1 = gbuf[:, :, :].rearrange("p a c -> p (a c)").rearrange("p (t e f) -> p t e f", t=HT, e=NE)
        cmp2 = tbuf[:, :, :].rearrange("p a c -> p (a c)").rearrange("p (t e f) -> p t e f", t=HT, e=NE)
        scT = tbuf[0:NE, 0, :]
        qst = simwork[:, :, :, :].rearrange("p a t c -> p (a t c)").bitcast(F16).rearrange("p (h q) -> p h q", h=NH)
        sigf = sig[:, :, :].rearrange("p t c -> p (t c)")
        pT = sigf[:, 0:2 * HC].rearrange("p (k q) -> p k q", k=2)
        xTa = sigf[:, 2 * HC:4 * HC].rearrange("p (k q) -> p k q", k=2)
        wq_rep = stage2[:, :, :].rearrange("p a c -> p (a c)")[:, 0:KT * 4 * D].rearrange("p (k c) -> p k c", k=KT)
        qhi = stage2[:, :, :].rearrange("p a c -> p (a c)")[:, KT * 4 * D:KT * 4 * D + HC].bitcast(F16).rearrange("p (k c) -> p k c", k=2)
        nmx = stage2[:, :, :].rearrange("p a c -> p (a c)")[0:NH, KT * 4 * D + HC:KT * 4 * D + 2 * HC]
        g = [gbuf[:, i] for i in range(2)]
        tt = [tbuf[:, i] for i in range(2)]
        u = [ubuf[:, i] for i in range(2)]
        ao = ctx3[:, 0].rearrange("p (b c) -> p b c", b=NB)
        aoT = ctx3[:, 1].rearrange("p (k q) -> p k q", k=KT)
        nm = ctx3[:, 2, KT * D:KT * D + HC // 2].bitcast(F16)
        wout = ctx3[:, 2, 0:KT * D].rearrange("p (k c) -> p k c", k=KT)
        w32 = w16[:, :, :].rearrange("p e c -> p (e c)").bitcast(F32)
        place = [0]

        def carve(*shape):
            n = 1
            for v in shape:
                n *= v
            out = w32[:, place[0]:place[0] + n]
            place[0] += n
            if len(shape) == 2:
                return out.rearrange("p (a c) -> p a c", a=shape[0])
            return out

        d1, d2, aggw, bcw, gatew = carve(KT, HID), carve(HID // P, D), carve(KT, D), carve(KT, D), carve(KT, D)
        rows, cols = carve(4, D), carve(32)
        brow, gsum, zt, tbr = carve(NB, D), carve(HT, D), carve(HT, D), carve(KT, NB * P)
        yl, cen, sq, nrm, th, act8 = carve(KT, NB), carve(KT, NB), carve(KT, NB), carve(KT, NB), carve(KT, NB), carve(HID // P, NB)
        cvar, crs, chalf, mean4 = carve(NB), carve(NB), carve(NB), carve(P)

        in_ctx, in_x, in_const = sem("in_ctx"), sem("in_x"), sem("in_const")
        in_w = [sem("in_w0"), sem("in_w1")]
        const_ready = sem("const_ready")
        l0_proj, l0_qk, sim_ready, sim_copied, sig_ready = (sem(n) for n in ("l0_proj", "l0_qk", "sim_ready", "sim_copied", "sig_ready"))
        top_ready, top_removed, masked, mask_t, sym_done, x1_done = (sem(n) for n in ("top_ready", "top_removed", "masked", "mask_t", "sym_done", "x1_done"))
        ln_x0 = sem("ln_x0")
        dve_step = sem("dve_step")
        vare_ready, rstd_ready, xn_ready = sem("vare_ready"), sem("rstd_ready"), sem("xn_ready")
        w_scaled, w_hi, w_lo = sem("w_scaled"), sem("w_hi"), sem("w_lo")
        t_ready, xhi_ready, xlo_ready, xT_ready = (sem(n) for n in ("t_ready", "xhi_ready", "xlo_ready", "xT_ready"))
        logit_ready, rdiff_ready, rexp_ready, sc_ready, scT_mm, scT_ready, bias_mm = (sem(n) for n in (
            "logit_ready", "rdiff_ready", "rexp_ready", "sc_ready", "scT_mm", "scT_ready", "bias_mm"))
        gu_ready, g_done, u_raw, u_done, tanh_done, glu_done, h_done, hhi_done, hlo_done, dn_ready, acc_done = (sem(n) for n in (
            "gu_ready", "g_done", "u_raw", "u_done", "tanh_done", "glu_done", "h_done", "hhi_done", "hlo_done", "dn_ready", "acc_done"))
        kwt_ready, kpsum, khi_ready, kcorr, kst_ready, vpsum, v_ready = (sem(n) for n in (
            "kwt_ready", "kpsum", "khi_ready", "kcorr", "kst_ready", "vpsum", "v_ready"))
        zero_ready, in_attn, xTa_ready, qpsum, qhi_ready, qcorr, q_ready = (sem(n) for n in (
            "zero_ready", "in_attn", "xTa_ready", "qpsum", "qhi_ready", "qcorr", "q_ready"))
        s_ready, mx_done, mxT_ready, nmx_ready, nm_ready, st_ready, exp_done, pv_done, rs_done, o_done = (sem(n) for n in (
            "s_ready", "mx_done", "mxT_ready", "nmx_ready", "nm_ready", "st_ready", "exp_done", "pv_done", "rs_done", "o_done"))
        aoT_psum, aoT_ready, wo_ready, x3_done = sem("aoT_psum"), sem("aoT_ready"), sem("wo_ready"), sem("x3_done")
        in_ffn, c_mm, c_v, c_var, c_rstd, c_gelu = (sem(n) for n in ("in_ffn", "c_mm", "c_v", "c_var", "c_rstd", "c_gelu"))
        brow_ready, gate_mm, z_ready, gate_ready, fin_ready = (sem(n) for n in ("brow_ready", "gate_mm", "z_ready", "gate_ready", "fin_ready"))
        out_done = sem("out_done")

        dstep = [0]

        def link(dve, ins):
            dstep[0] += 1
            ins.then_inc(dve_step, 1)
            dve.wait_ge(dve_step, dstep[0])

        block = ctx.enter_context(nc.Block())
        NCONST = 13
        FFN = ((d1, "d1"), (d2, "d2"), (aggw, "aggw"), (bcw, "bcw"), (gatew, "gatew"), (rows, "rows"), (cols, "cols"))
        NFFN = 16 * len(FFN)
        ADDS = HT * (NE + 1)

        @block.sync
        def _(sp):
            sp.dma_start(ctxT[:, :], a["ctxT"]).then_inc(in_ctx, 16)
            sp.dma_start(wqk0[:, :], a["wqk0"]).then_inc(in_ctx, 16)
            sp.dma_start(x[:, :, :], a["x"]).then_inc(in_x, 16)
            for dst, n in ((gam[:, 0:1], "gamma"), (mhalf[:, :], "mhalf"), (ident[:, :], "ident"), (maskf, "masks"), (negf, "neg"),
                           (pickf, "pick"), (wk_rep, "wk_rep"), (wv, "wv"),
                           (rbias[:, :], "rbias"), (gub[:, :, :], "gub"), (tri[:, :], "tri"), (rw[:, :, :], "rw"),
                           (bdown[:, :], "bdown")):
                sp.dma_start(dst, a[n]).then_inc(in_const, 16)
            for s in range(2):
                sp.dma_start(stage[s][:, :], a["w_exp"][s]).then_inc(in_w[s], 16)
            with sp.Fori(1, NE // 2) as i:
                for s in range(2):
                    sp.wait_ge(w_lo, 2 * i + s - 1)
                    sp.dma_start(stage[s][:, :], a["w_exp"][bass.ds(2 * i + s, 1)].rearrange("e p c -> p (e c)")).then_inc(in_w[s], 16)
            sp.wait_ge(w_lo, NE)
            sp.dma_start(wq_rep, a["wq_rep"]).then_inc(in_attn, 16)
            sp.wait_ge(sim_ready, NT)
            sp.dma_start(wout, a["wout"]).then_inc(in_attn, 16)
            sp.wait_ge(dn_ready, 2 * 2 * NE)
            for dst, n in FFN:
                sp.dma_start(dst, a[n]).then_inc(in_ffn, 16)
            sp.wait_ge(fin_ready, 2 * HT)
            sp.dma_start(a["out"], x[:, :, :]).then_inc(out_done, 16)
            sp.wait_ge(out_done, 16)

        @block.tensor
        def _(pe):
            pe.wait_ge(in_ctx, 32)
            for j in range(2):
                for w in range(2):
                    pe.matmul(psum[2 * w + j][0:CD, :], wqk0[:, w * CD:(w + 1) * CD], ctxT[:, j * 512:(j + 1) * 512],
                              start=True, stop=True).then_inc(l0_proj, 1)
            for b in range(NB):
                pe.wait_ge(l0_qk, 4 * (b // 2) // 2 + 2)
                for half in range(2):
                    t, r = half * HT + b, 1 - half
                    pe.matmul(psum[4 + t // 2][:, (t % 2) * SEQ:(t % 2 + 1) * SEQ],
                              qT0[:, b * SEQ + r * P:b * SEQ + (r + 1) * P], kT0[:, b * SEQ:(b + 1) * SEQ],
                              start=True, stop=True).then_inc(sim_ready, 1)
            pe.wait_ge(kwt_ready, 1)
            pe.wait_ge(in_const, 16 * NCONST)
            for n in range(NH):
                i, j = n // 2, n % 2
                if n >= 2:
                    pe.wait_ge(kst_ready, n - 1)
                else:
                    pe.wait_ge(l0_qk, 4)
                pe.matmul(psum[n % 2][:, :], wk_rep[:, i * P:(i + 1) * P], ctxT[:, j * 512:(j + 1) * 512],
                          start=True, stop=True).then_inc(kpsum, 1)
                pe.wait_ge(khi_ready, n + 1)
                pe.matmul(psum[n % 2][:, :], neg[:, 1, :], khi[:, n % 2, :], start=False, stop=True,
                          skip_group_check=True).then_inc(kcorr, 1)
            for m in range(4):
                if m >= 2:
                    pe.wait_ge(v_ready, m - 1)
                for c in range(2):
                    t = 2 * m + c
                    mm = pe.matmul(psum[2 + m % 2][:, c * D:(c + 1) * D], ctxT[:, t * P:(t + 1) * P], wv, start=True, stop=True)
                mm.then_inc(vpsum, 1)
            pe.wait_ge(masked, NT)
            pe.wait_ge(kst_ready, NH)
            pe.wait_ge(v_ready, 4)
            for m in range(NT // 2):
                for t in (2 * m, 2 * m + 1):
                    b, r = t % HT, 1 - t // HT
                    for kc in range(2):
                        src = (1 - kc) * HT + b
                        mm = pe.transpose(psum[m][:, (t % 2) * SEQ + kc * P:(t % 2) * SEQ + (kc + 1) * P],
                                          work[:, src, r * P:(r + 1) * P], ident[:, :])
                mm.then_inc(mask_t, 1)

            def turn_xn(n):
                pe.wait_ge(xn_ready, HT * (n + 1))
                for kt in range(KT):
                    for j in range(HT):
                        mm = pe.transpose(psum[6 + kt][:, j * P:(j + 1) * P], xn[:, j, kt * P:(kt + 1) * P], ident[:, :])
                    mm.then_inc(t_ready, 1)

            def logits(half):
                pe.wait_ge(xT_ready, KT * (half + 1))
                if half:
                    pe.wait_ge(acc_done, ADDS)
                for j in range(HT):
                    for kt in range(KT):
                        mm = pe.matmul(psum[4][:, j * NE:(j + 1) * NE], xT[:, kt, j * P:(j + 1) * P], rw[:, kt, :],
                                       start=(kt == 0), stop=(kt == KT - 1))
                mm.then_inc(logit_ready, 1)

            def gate_up(half, e, first=False):
                gi = half * NE + e
                for d in range(2):
                    for which, bank, read in ((0, psum[d], g_done), (1, psum[2 + d], u_raw)):
                        if not first or half:
                            pe.wait_ge(read, 2 * gi + d - 1)
                        col = which * D + d * P
                        n = 0
                        for kt in range(KT):
                            for wpart, xpart in ((0, xhi), (0, xlo), (1, xhi)):
                                c0 = wpart * WC + kt * 2 * D + col
                                mm = pe.matmul(bank[:, :], w16[:, bass.ds(e, 1), c0:c0 + P].rearrange("p a c -> p (a c)"),
                                               xpart[:, kt, :], start=(n == 0), stop=(n == 5))
                                n += 1
                        mm.then_inc(gu_ready, 1)

            def down(half, e):
                gi = half * NE + e
                pe.wait_ge(hlo_done, 2 * gi + 2)
                for j in range(HT):
                    if j % 2 == 0:
                        pe.wait_ge(acc_done, ADDS * half + 4 * e + j + 2)
                    n = 0
                    for d in range(2):
                        for hpart, wpart in ((hhi, 0), (hhi, 1), (hlo, 0)):
                            c0 = wpart * WC + KT * 2 * D + d * D
                            mm = pe.matmul(psum[4 + j // 2][:, (j % 2) * D:(j % 2 + 1) * D], hpart[:, d, j * P:(j + 1) * P],
                                           w16[:, bass.ds(e, 1), c0:c0 + D].rearrange("p a c -> p (a c)"),
                                           start=(n == 0), stop=(n == 5))
                            n += 1
                    if j % 2:
                        mm.then_inc(dn_ready, 1)

            for half in range(2):
                turn_xn(half)
                logits(half)
                pe.wait_ge(xhi_ready, KT * (half + 1))
                pe.wait_ge(xlo_ready, KT * (half + 1))
                pe.wait_ge(w_lo, NE if half else 1)
                pe.wait_ge(w_hi, NE if half else 1)
                gate_up(half, 0, first=True)
                pe.wait_ge(sc_ready, half + 1)
                for j in range(HT):
                    mm = pe.transpose(psum[5][0:NE, j * P:(j + 1) * P], sc[:, j, :], ident[:, :])
                mm.then_inc(scT_mm, 1)
                pe.wait_ge(scT_ready, half + 1)
                for j in range(HT):
                    mm = pe.matmul(psum[6 + j // 2][:, (j % 2) * D:(j % 2 + 1) * D], scT[:, j * P:(j + 1) * P], bdown[:, :],
                                   start=True, stop=True)
                    if j % 2:
                        mm.then_inc(bias_mm, 1)
                with pe.Fori(1, NE) as e:
                    if not half:
                        pe.wait_ge(w_lo, e + 1)
                        pe.wait_ge(w_hi, e + 1)
                    gate_up(half, e)
                    down(half, e - 1)
                down(half, NE - 1)

            def project_q(half):
                pe.wait_ge(in_attn, 32)
                pe.wait_ge(xTa_ready, KT * (half + 1))
                for i in range(NH // 2):
                    n = 8 * half + i
                    if i >= 2:
                        pe.wait_ge(q_ready, 2 * (n - 1))
                    for kt in range(KT):
                        mm = pe.matmul(psum[6 + i % 2][:, :], wq_rep[:, kt, i * P:(i + 1) * P], xTa[:, kt, :],
                                       start=(kt == 0), stop=(kt == KT - 1))
                    mm.then_inc(qpsum, 1)
                    pe.wait_ge(qhi_ready, n + 1)
                    pe.matmul(psum[6 + i % 2][:, :], neg[:, 0, :], qhi[:, i % 2, :], start=False, stop=True,
                              skip_group_check=True).then_inc(qcorr, 1)

            def scores(half, i, hh):
                n = NH * half + 2 * i + hh
                width = SEQ if half == 0 else P
                for k in range(2):
                    pe.wait_ge(mx_done, 2 * n + k + 1)
                    for c in range(2):
                        b = 2 * k + c
                        pe.matmul(psum[6 + k][:, c * width:(c + 1) * width],
                                  qst[:, bass.ds(2 * i + hh, 1), b * P:(b + 1) * P].rearrange("p a c -> p (a c)"),
                                  kst[:, bass.ds(i, 1), b * SEQ:b * SEQ + width].rearrange("p a c -> p (a c)"), start=True, stop=False)
                        mm = pe.matmul(psum[6 + k][:, (c + 1) * width - P:(c + 1) * width], identb[:, :], maskb[:, 0, :],
                                       start=False, stop=True)
                    mm.then_inc(s_ready, 1)

            def turn_maxima(half):
                pe.wait_ge(mx_done, 2 * NH * (half + 1) + 2)
                for b in range(NB):
                    mm = pe.transpose(psum[6][0:NH, b * P:(b + 1) * P], mx[:, b, :], ident[:, :])
                mm.then_inc(mxT_ready, 1)

            def scores_t(half, i, hh, kt, bank):
                diagonal = kt == 1 or half == 1
                pe.matmul(bank[:, :], pick[:, bass.ds(2 * i + hh, 1)].broadcast_to([P, P]), nm, start=True, stop=False)
                if diagonal:
                    pe.matmul(bank[:, :], identb[:, :], maskb[:, 1, :].unsqueeze(1).broadcast_to([P, NB, P]), start=False, stop=False)
                for b in range(NB):
                    mm = pe.matmul(bank[:, b * P:(b + 1) * P],
                                   kst[:, bass.ds(i, 1), b * SEQ + kt * P:b * SEQ + (kt + 1) * P].rearrange("p a c -> p (a c)"),
                                   qst[:, bass.ds(2 * i + hh, 1), b * P:(b + 1) * P].rearrange("p a c -> p (a c)"),
                                   start=False, stop=(b == NB - 1))
                mm.then_inc(st_ready, 1)

            def weigh(i, hh, kts, slots, bank):
                for b in range(NB):
                    for kt, slot in zip(kts, slots):
                        mm = pe.matmul(bank[:, b * VW:(b + 1) * VW], pT[:, slot, b * P:(b + 1) * P],
                                       vals[:, 2 * b + kt, bass.ds((2 * i + hh) * VW, VW)],
                                       start=(kt == 0), stop=(kt == kts[-1]))
                mm.then_inc(pv_done, 1)

            def project_out(half):
                pe.wait_ge(o_done, NH * (half + 1) + 2)
                for kt in range(KT):
                    for b in range(NB):
                        mm = pe.transpose(psum[6 + kt][:, b * P:(b + 1) * P], ao[:, b, kt * P:(kt + 1) * P], ident[:, :])
                    mm.then_inc(aoT_psum, 1)
                pe.wait_ge(aoT_ready, 2 * (half + 1))
                for j in range(HT):
                    for kt in range(KT):
                        mm = pe.matmul(psum[6 + j // 2][:, (j % 2) * D:(j % 2 + 1) * D], aoT[:, kt, j * P:(j + 1) * P], wout[:, kt, :],
                                       start=(kt == 0), stop=(kt == KT - 1))
                    if j % 2:
                        mm.then_inc(wo_ready, 1)

            for half in range(2):
                turn_xn(2 + half)
                project_q(half)
                pe.wait_ge(q_ready, NH * (half + 1))
                with pe.Fori(0, NH // 2) as i:
                    for hh in range(2):
                        scores(half, i, hh)
                turn_maxima(half)
                pe.wait_ge(nm_ready, 2 * (half + 1))
                with pe.Fori(0, NH // 2) as i:
                    if half == 0:
                        for hh in range(2):
                            pe.wait_ge(o_done, 2 * i + hh + 2)
                            for kt in range(2):
                                scores_t(0, i, hh, kt, psum[6 + kt])
                            pe.wait_ge(exp_done, 4 * i + 2 * hh + 2)
                            weigh(i, hh, (0, 1), (0, 1), psum[6])
                    else:
                        for hh in range(2):
                            pe.wait_ge(o_done, NH + 2 * i + hh + 1)
                            scores_t(1, i, hh, 0, psum[6 + hh])
                        for hh in range(2):
                            pe.wait_ge(exp_done, 2 * NH + 2 * i + hh + 1)
                            weigh(i, hh, (0,), (hh,), psum[6 + hh])
                project_out(half)

            cbank = psum[5]
            pe.wait_ge(in_ffn, NFFN)
            count = [0, 0]

            def column_sum(src):
                count[1] += 1
                pe.wait_ge(c_v, count[1])
                for kt in range(KT):
                    mm = pe.matmul(cbank[:, 0:NB], mean4, src[:, kt, :], start=(kt == 0), stop=(kt == KT - 1))
                mm.then_inc(c_mm, 1)

            def column_mm(w, src, kts, ms):
                count[1] += 1
                pe.wait_ge(c_v, count[1])
                for m in range(ms):
                    for kt in range(kts):
                        mm = pe.matmul(cbank[:, m * NB:(m + 1) * NB], w[:, kt, m * P:(m + 1) * P], src[:, kt, :],
                                       start=(kt == 0), stop=(kt == kts - 1))
                mm.then_inc(c_mm, 1)

            turn_xn(4)
            column_sum(yl)
            column_sum(sq)
            column_mm(aggw, nrm, KT, KT)
            for _ in range(STEPS):
                column_sum(th)
                column_sum(sq)
                column_mm(d1, nrm, KT, HID // P)
                column_mm(d2, act8, HID // P, KT)
            count[1] += 1
            pe.wait_ge(c_v, count[1])
            for b in range(NB):
                for kt in range(KT):
                    mm = pe.matmul(psum[b // 2][:, (b % 2) * D:(b % 2 + 1) * D], th[:, kt, b:b + 1].broadcast_to([P, P]), bcw[:, kt, :],
                                   start=(kt == 0), stop=(kt == KT - 1))
            mm.then_inc(c_mm, 1)
            for half in range(2):
                if half:
                    turn_xn(5)
                    pe.wait_ge(z_ready, 2)
                pe.wait_ge(xTa_ready, KT * (3 + half))
                for j in range(HT):
                    for kt in range(KT):
                        mm = pe.matmul(psum[2 + j // 2][:, (j % 2) * D:(j % 2 + 1) * D], xTa[:, kt, j * P:(j + 1) * P], gatew[:, kt, :],
                                       start=(kt == 0), stop=(kt == KT - 1))
                    if j % 2:
                        mm.then_inc(gate_mm, 1)

        @block.scalar
        def _(act):
            for n in range(4):
                act.wait_ge(l0_proj, n + 1)
                j, w = n // 2, n % 2
                dst = (qT0, kT0)[w]
                act.activation(dst[:, j * 512:(j + 1) * 512], psum[2 * w + j][0:CD, :], ACT.Copy).then_inc(l0_qk, 1)
            for bank, need in ((0, 3), (2, 4), (1, 7), (3, 8)):
                act.wait_ge(sim_ready, need)
                for dst in (work, sim):
                    act.activation(dst[:, 2 * bank:2 * bank + 2, :], psum[4 + bank][:, :].rearrange("p (a c) -> p a c", a=2),
                                   ACT.Copy).then_inc(sim_copied, 1)
            act.wait_ge(in_const, 16 * NCONST)
            act.activation(wk_rep, wk_rep, ACT.Copy, scale=KS).then_inc(kwt_ready, 1)
            act.wait_ge(const_ready, 1)
            for n in range(NH):
                i, j = n // 2, n % 2
                act.wait_ge(kpsum, n + 1)
                act.activation(khi[:, n % 2, :], psum[n % 2][:, :], ACT.Copy).then_inc(khi_ready, 1)
                act.wait_ge(kcorr, n + 1)
                act.activation(kst[:, i, j * 512:(j + 1) * 512], psum[n % 2][:, :], ACT.Copy).then_inc(kst_ready, 1)
            for m in range(4):
                act.wait_ge(vpsum, m + 1)
                act.activation(vals[:, 2 * m:2 * m + 2, :].rearrange("p t (h v) -> p t h v", v=VW)[:, :, :, 0:HD],
                               psum[2 + m % 2][:, :].rearrange("p (t h v) -> p t h v", t=2, h=NH), ACT.Copy).then_inc(v_ready, 1)
            act.wait_ge(sim_copied, 8)
            for m in range(4):
                act.activation(sig[:, 2 * m:2 * m + 2, :], sim[:, 2 * m:2 * m + 2, :], ACT.Tanh, scale=1 / 32).then_inc(sig_ready, 1)
            for m in range(4):
                act.wait_ge(sig_ready, m + 1)
                act.activation(sig[:, 2 * m:2 * m + 2, :], sig[:, 2 * m:2 * m + 2, :], ACT.Copy, bias=1.0).then_inc(sig_ready, 1)
            act.activation(gam[:, 1:2], gam[:, 0:1], ACT.Tanh, scale=0.5).then_inc(const_ready, 1)
            act.wait_ge(ln_x0, 2)
            for t in range(NT):
                act.activation(x[:, t, :], x[:, t, :], ACT.Identity, bias=lnc[:, t:t + 1], scale=lna[:, t:t + 1]).then_inc(ln_x0, 1)
            with act.Fori(0, NE // 2) as i:
                for s in range(2):
                    act.wait_ge(in_w[s], 16 * i + 16)
                    act.activation(stage[s][:, :], stage[s][:, :], ACT.Copy, scale=WS).then_inc(w_scaled, 1)
                    act.wait_ge(w_scaled, 2 * i + s + 1)
                    act.activation(w16[:, bass.ds(2 * i + s, 1), 0:WC].rearrange("p a c -> p (a c)"), stage[s][:, :], ACT.Copy).then_inc(w_hi, 1)
            for half in range(2):
                for kt in range(KT):
                    act.wait_ge(t_ready, KT * half + kt + 1)
                    if half and kt == 0:
                        act.wait_ge(gu_ready, 4 * NE)
                        act.wait_ge(hlo_done, 2 * NE)
                    act.activation(xhi[:, kt, :], psum[6 + kt][:, :], ACT.Copy).then_inc(xhi_ready, 1)
                    act.activation(xT[:, kt, :], psum[6 + kt][:, :], ACT.Copy).then_inc(xT_ready, 1)
                act.wait_ge(rdiff_ready, half + 1)
                act.activation(rex[:, :, :], rex[:, :, :], ACT.Exp).then_inc(rexp_ready, 1)
                act.wait_ge(scT_mm, half + 1)
                act.activation(scT, psum[5][0:NE, :], ACT.Copy).then_inc(scT_ready, 1)

                def experts(e, first=False):
                    gi = half * NE + e
                    for d in range(2):
                        act.wait_ge(gu_ready, 4 * gi + 2 * d + 2)
                        if not (first and half == 0):
                            act.wait_ge(hlo_done, 2 * gi + d - 1)
                        act.activation(u[d], psum[2 + d][:, :], ACT.Identity, scale=1 / WS,
                                       bias=ub1[:, bass.ds(e, 1), d:d + 1].rearrange("p a c -> p (a c)")).then_inc(u_raw, 1)
                        act.wait_ge(g_done, 2 * gi + d + 1)
                        if first and d == 0:
                            act.wait_ge(bias_mm, 2 * half + 2)
                        act.activation(tt[d], g[d], ACT.Tanh, scale=ALPHA / 2 / WS).then_inc(tanh_done, 1)
                    for d in range(2):
                        if not (first and half == 0):
                            act.wait_ge(dn_ready, 2 * gi)
                        act.wait_ge(h_done, 2 * gi + d + 1)
                        act.activation(hhi[:, d, :], u[d], ACT.Copy).then_inc(hhi_done, 1)

                experts(0, first=True)
                with act.Fori(1, NE) as e:
                    experts(e)

            def copy_turned(n):
                for kt in range(KT):
                    act.wait_ge(t_ready, KT * n + kt + 1)
                    act.activation(xTa[:, kt, :], psum[6 + kt][:, :], ACT.Copy).then_inc(xTa_ready, 1)

            for half in range(2):
                copy_turned(2 + half)
                act.wait_ge(zero_ready, 3)
                for i in range(NH // 2):
                    n = 8 * half + i
                    act.wait_ge(qpsum, n + 1)
                    act.activation(qhi[:, i % 2, :], psum[6 + i % 2][:, :], ACT.Copy).then_inc(qhi_ready, 1)
                    act.wait_ge(qcorr, n + 1)
                    for hh in range(2):
                        r = slice(hh * 64, hh * 64 + 64)
                        act.activation(qst[r, 2 * i + hh, :], psum[6 + i % 2][r, :], ACT.Copy).then_inc(q_ready, 1)
                act.wait_ge(mxT_ready, half + 1)
                act.activation(nm[0:NH, :], psum[6][0:NH, :], ACT.Copy, scale=-1.0).then_inc(nm_ready, 1)
                act.activation(nmx, psum[6][0:NH, :], ACT.Copy, scale=-1.0).then_inc(nmx_ready, 1)
                with act.Fori(0, NH // 2) as i:
                    for hh in range(2):
                        for kt in range(2 - half):
                            n = (4 * i + 2 * hh + kt) if half == 0 else (2 * NH + 2 * i + hh)
                            slot = hh if half else kt
                            act.wait_ge(st_ready, n + 1)
                            act.activation(pT[:, slot, :], psum[6 + slot][:, :], ACT.Exp, scale=HD ** -0.5 / KS).then_inc(exp_done, 1)
                for kt in range(KT):
                    act.wait_ge(aoT_psum, 2 * half + kt + 1)
                    act.activation(aoT[:, kt, :], psum[6 + kt][:, :], ACT.Copy).then_inc(aoT_ready, 1)
            copy_turned(4)
            for k in range(STEPS):
                act.wait_ge(c_gelu, k + 1)
                act.activation(act8[:, :, :], act8[:, :, :], ACT.Gelu).then_inc(c_v, 1)
            for half in range(2):
                if half:
                    act.wait_ge(gate_mm, 2)
                    copy_turned(5)
                for m in range(2):
                    act.wait_ge(z_ready, 2 * half + m + 1)
                    act.activation(zt[:, 2 * m:2 * m + 2, :], zt[:, 2 * m:2 * m + 2, :], ACT.Tanh, scale=0.5).then_inc(gate_ready, 1)

        @block.gpsimd
        def _(pool):
            def power(n, sl):
                pool.wait_ge(vare_ready, n)
                pool.tensor_tensor(rstd[:, sl], vare[:, sl], mhalf[:, sl], ALU.pow).then_inc(rstd_ready, 1)

            pool.memset(vals[:, :, :].rearrange("p t (h v) -> p t h v", v=VW)[:, :, :, HD:VW], 1.0).then_inc(zero_ready, 1)
            pool.wait_ge(in_const, 16 * NCONST)
            power(1, slice(0, NT))
            with pool.Fori(0, NE // 2) as i:
                for s in range(2):
                    pool.wait_ge(w_hi, 2 * i + s + 1)
                    pool.tensor_tensor(w16[:, bass.ds(2 * i + s, 1), WC:2 * WC].rearrange("p a c -> p (a c)"), stage[s][:, :],
                                       w16[:, bass.ds(2 * i + s, 1), 0:WC].rearrange("p a c -> p (a c)"), ALU.subtract).then_inc(w_lo, 1)
            pool.wait_ge(x1_done, 4)
            pool.memset(ctx3[:, 2, KT * D:KT * D + HC // 2], 0.0).then_inc(zero_ready, 1)
            pool.memset(simwork[:, :, :, :].rearrange("p a t c -> p (a t c)"), 0.0).then_inc(zero_ready, 1)
            for half in range(2):
                power(2 + half, slice(0, HT))

                def experts(e, first=False):
                    gi = half * NE + e
                    for d in range(2):
                        pool.wait_ge(hhi_done, 2 * gi + d + 1)
                        pool.tensor_tensor(hlo[:, d, :], u[d], hhi[:, d, :], ALU.subtract).then_inc(hlo_done, 1)

                experts(0, first=True)
                with pool.Fori(1, NE) as e:
                    experts(e)
            power(4, slice(0, HT))
            power(5, slice(0, HT))
            power(6, slice(0, HT))
            for k in range(STEPS + 1):
                pool.wait_ge(c_var, k + 1)
                pool.tensor_tensor(crs, cvar, chalf, ALU.pow).then_inc(c_rstd, 1)
            power(7, slice(0, HT))
            power(8, slice(0, HT))
            power(9, slice(0, HT))

        @block.vector
        def _(dve):
            def stats(src, k, n, eps):
                for j in range(k):
                    ins = dve.bn_stats(bn[:, j, :], src[:, j, :])
                link(dve, ins)
                for j in range(k):
                    ins = dve.bn_aggr(mv[:, j, :], bn[:, j, :])
                link(dve, ins)
                dve.tensor_scalar(vare[:, 0:k], mv[:, 0:k, 1], eps, None, ALU.add).then_inc(vare_ready, 1)
                dve.wait_ge(rstd_ready, n)

            dve.wait_ge(in_x, 16)
            dve.sem_inc(mx_done, 2)
            dve.sem_inc(o_done, 2)
            stats(x, NT, 1, 1e-5)
            dve.wait_ge(in_const, 16 * NCONST)
            dve.tensor_copy(identb[:, :], ident[:, :])
            dve.tensor_copy(maskb[:, :, :], maskf)
            dve.tensor_copy(neg[:, :, :], negf)
            dve.tensor_copy(pick[:, :], pickf)
            dve.tensor_scalar(gub64[:, :, :], gub[:, :, 0:2], WS, None, ALU.mult)
            dve.tensor_scalar(ub1[:, :, :], gub[:, :, 2:4], 1.0, None, ALU.add).then_inc(const_ready, 1)
            dve.wait_ge(const_ready, 2)
            link(dve, dve.tensor_scalar(gam[:, 2:3], gam[:, 1:2], -0.5, 0.5, ALU.mult, ALU.add))
            dve.tensor_scalar(gam[:, 3:4], gam[:, 1:2], 0.125, 0.125, ALU.mult, ALU.add)
            dve.tensor_scalar(lna[:, :], rstd[:, :], gam[:, 2:3], 1.0, ALU.mult, ALU.add).then_inc(ln_x0, 1)
            link(dve, dve.scalar_tensor_tensor(lnc[:, :], mv[:, :, 0], gam[:, 2:3], rstd[:, :], ALU.mult, ALU.mult))
            dve.tensor_scalar(lnc[:, :], lnc[:, :], -1.0, None, ALU.mult).then_inc(ln_x0, 1)

            dve.wait_ge(sim_copied, 8)
            for t in range(NT):
                dve.max(top[:, t, :], work[:, t, :]).then_inc(top_ready, 1)
            for i in range(TOPK // 8):
                for t in range(NT):
                    dve.wait_ge(top_ready, NT * i + t + 1)
                    dve.match_replace(work[:, t, :], top[:, t, :], work[:, t, :], -3e38).then_inc(top_removed, 1)
                for t in range(NT):
                    dve.wait_ge(top_removed, NT * i + t + 1)
                    dve.max(top[:, t, :], work[:, t, :]).then_inc(top_ready, 1)
            kth = TOPK % 8 - 1
            dve.wait_ge(top_ready, NT * (TOPK // 8 + 1))
            dve.wait_ge(sig_ready, 8)
            for t in range(NT):
                dve.scalar_tensor_tensor(work[:, t, :], sim[:, t, :], top[:, t, kth:kth + 1], sig[:, t, :],
                                         ALU.is_ge, ALU.mult).then_inc(masked, 1)
            dve.wait_ge(masked, NT)
            dve.wait_ge(ln_x0, 2 + NT)
            for m in range(NT // 2):
                dve.wait_ge(mask_t, m + 1)
                dve.tensor_tensor(sim[:, 2 * m:2 * m + 2, :], work[:, 2 * m:2 * m + 2, :],
                                  psum[m][:, :].rearrange("p (a c) -> p a c", a=2), ALU.add).then_inc(sym_done, 1)
            for m in range(NT // 2):
                dve.wait_ge(sym_done, m + 1)
                dve.scalar_tensor_tensor(x[:, 2 * m:2 * m + 2, :], sim[:, 2 * m:2 * m + 2, :], gam[:, 3:4],
                                         x[:, 2 * m:2 * m + 2, :], ALU.mult, ALU.add).then_inc(x1_done, 1)
            def normalise(half, n):
                stats(x[:, half * HT:(half + 1) * HT], HT, len(rounds) + 2, 1e-5)
                rounds.append(n)
                if n:
                    dve.wait_ge(t_ready, KT * n)
                for j in range(HT):
                    dve.tensor_scalar(xn[:, j, :], x[:, half * HT + j, :], mv[:, j, 0:1], rstd[:, j:j + 1],
                                      ALU.subtract, ALU.mult).then_inc(xn_ready, 1)

            rounds = []
            for half in range(2):
                dve.wait_ge(x1_done, 4)
                normalise(half, half)
                if half:
                    dve.wait_ge(gu_ready, 4 * NE)
                for kt in range(KT):
                    dve.wait_ge(xT_ready, KT * half + kt + 1)
                    dve.tensor_tensor(xlo[:, kt, :], xT[:, kt, :], xhi[:, kt, :], ALU.subtract).then_inc(xlo_ready, 1)
                dve.wait_ge(logit_ready, half + 1)
                link(dve, dve.tensor_tensor(lg[:, :, :], psum[4][:, 0:HT * NE].rearrange("p (t e) -> p t e", t=HT),
                                            rbias[:, :].unsqueeze(1).broadcast_to([P, HT, NE]), ALU.add))
                link(dve, dve.tensor_reduce(rmx[:, :], lg[:, :, :], AXX, ALU.max))
                dve.tensor_tensor(rex[:, :, :], lg[:, :, :], rmx[:, :].unsqueeze(2).broadcast_to([P, HT, NE]),
                                  ALU.subtract).then_inc(rdiff_ready, 1)
                mine = lg[:, :, :].unsqueeze(3).broadcast_to([P, HT, NE, NE])
                other = lg[:, :, :].unsqueeze(2).broadcast_to([P, HT, NE, NE])
                dve.tensor_tensor(cmp1, other, mine, ALU.is_gt)
                link(dve, dve.tensor_tensor(cmp2, other, mine, ALU.is_equal))
                cmp2f = cmp2.rearrange("p t e f -> p t (e f)")
                link(dve, dve.tensor_tensor(cmp2f, cmp2f, tri[:, :].unsqueeze(1).broadcast_to([P, HT, NE * NE]), ALU.mult))
                link(dve, dve.tensor_tensor(cmp1, cmp1, cmp2, ALU.add))
                link(dve, dve.tensor_reduce(rank[:, :, :], cmp1, AXX, ALU.add))
                dve.wait_ge(rexp_ready, half + 1)
                link(dve, dve.scalar_tensor_tensor(rex[:, :, :], rank[:, :, :], float(NTOP), rex[:, :, :], ALU.is_lt, ALU.mult))
                link(dve, dve.tensor_reduce(rsm[:, :], rex[:, :, :], AXX, ALU.add))
                link(dve, dve.reciprocal(rsm[:, :], rsm[:, :]))
                dve.tensor_tensor(sc[:, :, :], rex[:, :, :], rsm[:, :].unsqueeze(2).broadcast_to([P, HT, NE]),
                                  ALU.mult).then_inc(sc_ready, 1)
                dve.wait_ge(sc_ready, half + 1)
                link(dve, dve.tensor_scalar(sc64[:, :, :], sc[:, :, :], 1 / WS, None, ALU.mult))

                def act_fn(e, first=False):
                    gi = half * NE + e
                    for d in range(2):
                        dve.wait_ge(gu_ready, 4 * gi + 2 * d + 1)
                        dve.tensor_scalar(g[d], psum[d][:, :], gub64[:, bass.ds(e, 1), d:d + 1].rearrange("p a c -> p (a c)"),
                                          GLIM * WS, ALU.add, ALU.min).then_inc(g_done, 1)
                        dve.wait_ge(tanh_done, 2 * gi + d + 1)
                        dve.scalar_tensor_tensor(tt[d], tt[d], 1.0, g[d], ALU.add, ALU.mult).then_inc(glu_done, 1)
                        dve.wait_ge(u_raw, 2 * gi + d + 1)
                        dve.tensor_scalar(u[d], u[d], GLIM + 1, 1 - GLIM, ALU.min, ALU.max).then_inc(u_done, 1)
                        dve.wait_ge(glu_done, 2 * gi + d + 1)
                        dve.wait_ge(u_done, 2 * gi + d + 1)
                        dve.scalar_tensor_tensor(u[d], tt[d], 0.5 / WS, u[d], ALU.mult, ALU.mult).then_inc(h_done, 1)

                def add_out(e):
                    gi = half * NE + e
                    for j in range(HT):
                        t = half * HT + j
                        dve.wait_ge(dn_ready, 2 * gi + j // 2 + 1)
                        dve.scalar_tensor_tensor(x[:, t, :], psum[4 + j // 2][:, (j % 2) * D:(j % 2 + 1) * D],
                                                 sc64[:, j, bass.ds(e, 1)], x[:, t, :], ALU.mult, ALU.add).then_inc(acc_done, 1)

                act_fn(0, first=True)
                for j in range(HT):
                    t = half * HT + j
                    dve.wait_ge(bias_mm, 2 * half + j // 2 + 1)
                    dve.tensor_tensor(x[:, t, :], x[:, t, :], psum[6 + j // 2][:, (j % 2) * D:(j % 2 + 1) * D], ALU.add).then_inc(acc_done, 1)
                dve.wait_ge(acc_done, ADDS * half + HT)
                with dve.Fori(1, NE) as e:
                    act_fn(e)
                    add_out(e - 1)
                add_out(NE - 1)

            for half in range(2):
                dve.wait_ge(acc_done, 2 * ADDS)
                normalise(half, 2 + half)
                width = SEQ if half == 0 else P
                with dve.Fori(0, NH // 2) as i:
                    for hh in range(2):
                        n = NH * half + 2 * i + hh
                        for k in range(2):
                            dve.wait_ge(s_ready, 2 * n + k + 1)
                            dve.tensor_reduce(mx[:, 2 * k:2 * k + 2, bass.ds(2 * i + hh, 1)],
                                              psum[6 + k][:, 0:2 * width].rearrange("p (b c) -> p b c", b=2), AXX, ALU.max).then_inc(mx_done, 1)
                dve.wait_ge(nmx_ready, half + 1)
                dve.tensor_tensor(nm[32:32 + NH, :], nmx, nm[0:NH, :], ALU.subtract).then_inc(nm_ready, 1)
                with dve.Fori(0, NH // 2) as i:
                    for hh in range(2):
                        n = NH * half + 2 * i + hh
                        o = psum[6 + (hh if half else 0)][:, 0:NB * VW].rearrange("p (b v) -> p b v", v=VW)
                        dve.wait_ge(pv_done, n + 1)
                        dve.reciprocal(rs[:, hh, :], o[:, :, HD]).then_inc(rs_done, 1)
                        dve.wait_ge(rs_done, n + 1)
                        dve.tensor_tensor(ao[:, :, bass.ds((2 * i + hh) * HD, HD)], o[:, :, 0:HD],
                                          rs[:, hh, :].unsqueeze(2).broadcast_to([P, NB, HD]), ALU.mult).then_inc(o_done, 1)
                for j in range(HT):
                    t = half * HT + j
                    dve.wait_ge(wo_ready, 2 * half + j // 2 + 1)
                    dve.tensor_tensor(x[:, t, :], x[:, t, :], psum[6 + j // 2][:, (j % 2) * D:(j % 2 + 1) * D], ALU.add).then_inc(x3_done, 1)

            dve.wait_ge(x3_done, 2 * HT)
            normalise(0, 4)
            dve.wait_ge(in_ffn, NFFN)
            dve.memset(mean4, 1.0 / D)
            dve.memset(chalf, -0.5)
            dve.wait_ge(xTa_ready, KT * 3)
            dve.tensor_copy(yl[:, :, :], xTa.rearrange("p k (b q) -> p k b q", b=NB)[:, :, :, P - 1]).then_inc(c_v, 1)
            mm_seen, ln_seen = [0], [0]

            def column(c, n=KT):
                return cols[:, c:c + n].unsqueeze(2).broadcast_to([P, n, NB])

            def from_mm(n=NB):
                mm_seen[0] += 1
                dve.wait_ge(c_mm, mm_seen[0])
                return psum[5][:, 0:n]

            def column_norm(src, eps, gcol, bcol):
                mean = from_mm().unsqueeze(1).broadcast_to([P, KT, NB])
                link(dve, dve.tensor_tensor(cen[:, :, :], src[:, :, :], mean, ALU.subtract))
                dve.tensor_tensor(sq[:, :, :], cen[:, :, :], cen[:, :, :], ALU.mult).then_inc(c_v, 1)
                dve.tensor_scalar(cvar, from_mm(), eps, None, ALU.add).then_inc(c_var, 1)
                ln_seen[0] += 1
                dve.wait_ge(c_rstd, ln_seen[0])
                link(dve, dve.tensor_tensor(nrm[:, :, :], cen[:, :, :], crs.unsqueeze(1).broadcast_to([P, KT, NB]), ALU.mult))
                link(dve, dve.tensor_tensor(nrm[:, :, :], nrm[:, :, :], column(gcol), ALU.mult))
                dve.tensor_tensor(nrm[:, :, :], nrm[:, :, :], column(bcol), ALU.add).then_inc(c_v, 1)

            def pairs(v):
                return v.rearrange("p (a c) -> p a c", c=NB)

            column_norm(yl, 1e-6, 0, 2)
            dve.tensor_tensor(th[:, :, :], pairs(from_mm(KT * NB)), column(4), ALU.add).then_inc(c_v, 1)
            for k in range(STEPS):
                column_norm(th, 1e-6, 6, 8)
                dve.tensor_tensor(act8[:, :, :], pairs(from_mm(HID // P * NB)), column(12, HID // P), ALU.add).then_inc(c_gelu, 1)
                link(dve, dve.tensor_tensor(th[:, :, :], th[:, :, :], column(10), ALU.add))
                dve.tensor_tensor(th[:, :, :], th[:, :, :], pairs(from_mm(KT * NB)), ALU.add).then_inc(c_v, 1)

            from_mm()
            for m in range(2):
                ins = dve.tensor_tensor(brow[:, 2 * m:2 * m + 2, :], psum[m][:, :].rearrange("p (b c) -> p b c", b=2),
                                        rows[:, 3:4, :].broadcast_to([P, 2, D]), ALU.add)
            link(dve, ins)
            for half in range(2):
                if half:
                    normalise(1, 5)
                for m in range(2):
                    dve.wait_ge(gate_mm, 2 * half + m + 1)
                    dve.tensor_tensor(zt[:, 2 * m:2 * m + 2, :], psum[2 + m][:, :].rearrange("p (b c) -> p b c", b=2),
                                      rows[:, 0:1, :].broadcast_to([P, 2, D]), ALU.add).then_inc(z_ready, 1)
                for m in range(2):
                    two = slice(2 * m, 2 * m + 2)
                    dve.wait_ge(gate_ready, 2 * half + m + 1)
                    link(dve, dve.scalar_tensor_tensor(gsum[:, two, :], zt[:, two, :], 1.0, brow[:, two, :], ALU.add, ALU.mult))
                    link(dve, dve.scalar_tensor_tensor(gsum[:, two, :], gsum[:, two, :], 0.5, xn[:, two, :], ALU.mult, ALU.add))
                stats(gsum, HT, len(rounds) + 2, 1e-6)
                rounds.append("out")
                for j in range(HT):
                    t = half * HT + j
                    link(dve, dve.tensor_scalar(gsum[:, j, :], gsum[:, j, :], mv[:, j, 0:1], rstd[:, j:j + 1], ALU.subtract, ALU.mult))
                    dve.tensor_tensor(x[:, t, :], x[:, t, :], rows[:, 2, :], ALU.add)
                    link(dve, dve.tensor_tensor(gsum[:, j, :], gsum[:, j, :], rows[:, 1, :], ALU.mult))
                    dve.tensor_tensor(x[:, t, :], x[:, t, :], gsum[:, j, :], ALU.add).then_inc(fin_ready, 1)


def kernel(**inputs):
    import numpy as np
    import concourse.bacc as bacc
    from concourse.bass_utils import run_bass_kernel_spmd as run

    I = {k: np.asarray(v) for k, v in inputs.items()}
    f = np.float32

    def tiles(w):
        return np.ascontiguousarray(w.reshape(-1, P, w.shape[-1]).transpose(1, 0, 2))

    def spread(v):
        return np.ascontiguousarray(np.broadcast_to(v.reshape(1, -1), (P, v.size)))

    def column(v):
        return v.reshape(-1, P).T

    xs = I["x"].reshape(NB, 2, P, D)[:, ::-1].transpose(2, 1, 0, 3).reshape(P, NT, D)
    gu = I["L0_ffn_gate_up_proj"].reshape(NE, KT, P, D, 2).transpose(0, 2, 1, 4, 3).reshape(NE, P, KT * 2 * D)
    dn = I["L0_ffn_down_proj"].reshape(NE, KT, P, D).transpose(0, 2, 1, 3).reshape(NE, P, KT * D)
    gb = I["L0_ffn_gate_up_proj_bias"].reshape(NE, 2, P, 2).transpose(2, 0, 3, 1).reshape(P, NE, 4)
    i = np.arange(P)
    up = np.where(i[None, :] > i[:, None], f(NEG), f(0))
    e = np.arange(NE)
    group = i // HD % 4
    neg = np.stack([-np.diag((group == c).astype(f)) for c in (1, 2)], 1).astype(f)
    pick = np.where(i[:, None] % 32 == e[None, :], f(1), f(0)) * (i[:, None] < 64)
    pick = pick.astype(f)

    def stacked(w, copies):
        w = w.reshape(-1, NH, 1, HD)
        none = np.zeros((w.shape[0], NH, 4 - copies, HD), f)
        return np.concatenate([w] * copies + [none], 2).reshape(w.shape[0], NH * 64)

    wk_rep = stacked(I["L1_xattn_Wkv_expand"][:D].T, 3)
    wq_rep = tiles(stacked(I["L1_xattn_Wq"].T, 3))
    arrays = {
        "x": xs, "ctxT": I["ctx_512"].reshape(-1, CD).T,
        "wqk0": np.concatenate([I["L0_xattn_Wq"].T, I["L0_xattn_Wk"].T], 1),
        "gamma": np.broadcast_to(I["L0_xattn_gamma_raw"].reshape(1, 1), (P, 1)),
        "ident": np.eye(P, dtype=f), "masks": np.stack([up, up.T], 1).astype(f),
        "mhalf": np.full((P, NT), -0.5, f),
        "neg": neg, "pick": pick, "wk_rep": wk_rep, "wq_rep": wq_rep,
        "wv": I["L1_xattn_Wkv_expand"][D:].T, "wout": tiles(I["L1_xattn_Wout"].T),
        "d1": tiles(I["L1_ffn_d1_w"]), "d2": tiles(I["L1_ffn_d2_w"]), "aggw": tiles(I["L1_ffn_agg_w"]),
        "bcw": tiles(I["L1_ffn_bc_w"]), "gatew": tiles(I["L1_ffn_gate_w"]),
        "rows": np.stack([spread(I[n]) for n in ("L1_ffn_gate_b", "L1_ffn_out_gamma", "L1_ffn_out_beta", "L1_ffn_bc_b")], 1),
        "cols": np.concatenate([column(I["L1_ffn_" + n]) for n in ("in_gamma", "in_beta", "agg_b", "pn_gamma", "pn_beta", "d2_b", "d1_b")]
                               + [np.zeros((P, 32 - 20), f)], 1),
        "rbias": spread(I["L0_ffn_router_bias"]), "gub": gb,
        "tri": spread((e[None, :] < e[:, None]).astype(f)),
        "rw": tiles(I["L0_ffn_router_weight"].T), "bdown": I["L0_ffn_down_proj_bias"],
        "w_exp": np.concatenate([gu, dn], 2),
    }
    arrays = {k: np.ascontiguousarray(v) for k, v in arrays.items()}
    nc = bacc.Bacc("TRN2", target_bir_lowering=False, num_devices=1)
    args = {k: nc.dram_tensor(f"in_{k}", v.shape, mybir.dt.from_np(v.dtype), kind="ExternalInput").ap() for k, v in arrays.items()}
    args["out"] = nc.dram_tensor("out_x", (P, NT, D), F32, kind="ExternalOutput").ap()
    chip_program(nc, args)
    r = run(nc, [{f"in_{k}": v for k, v in arrays.items()}], core_ids=[0])
    out = r.results[0]["out_x"]
    return np.ascontiguousarray(out.reshape(P, 2, NB, D).transpose(2, 1, 0, 3)[:, ::-1].reshape(NB, SEQ, D))
```

```python
from contextlib import ExitStack

import concourse.bass as bass
from concourse import mybir

F32 = mybir.dt.float32
F16 = mybir.dt.float16
BF16 = mybir.dt.bfloat16
ALU = mybir.AluOpType
ACT = mybir.ActivationFunctionType
AXX = mybir.AxisListType.X

P = 128
NB = 4
SEQ = 256
D = 256
KT = D // P
NT = NB * SEQ // P
HT = NT // 2
HC = HT * P
CD = 64
TOPK = max(1, int(SEQ * 0.3))
NE = 16
NTOP = 4
NH = 16
HD = D // NH
VW = HD + 1
WC = KT * 2 * D + KT * D
WP = WC // 2
WS = 64.0
GLIM = 7.0
ALPHA = 1.702
KS = 16.0
HID = 4 * D
STEPS = 4
NEG = -1e30


def chip_program(nc, a):
    with ExitStack() as ctx:
        def sb(name, shape, dt=F32):
            return ctx.enter_context(nc.sbuf_tensor(name, shape, dt))

        def sem(name):
            return ctx.enter_context(nc.semaphore(name))

        psum = [ctx.enter_context(nc.psum_tensor(f"bank{i}", [P, 512], F32)) for i in range(8)]

        x = sb("x", [P, NT, D])
        xn = sb("xn", [P, HT, D])
        ctx3 = sb("ctx3", [P, 3, NB * SEQ])
        ctxT, qT0, kT0 = (ctx3[0:CD, i] for i in range(3))
        wqk0 = sb("wqk0", [CD, 2 * CD])
        simwork = sb("simwork", [P, 2, NT, SEQ])
        sim, work = simwork[:, 0], simwork[:, 1]
        sig = sb("sig", [P, NT, SEQ])
        top = sb("top", [P, NT, 8])
        bn = sb("bn", [P, NT, 6])
        mv = sb("mv", [P, NT, 2])
        vare = sb("vare", [P, NT])
        rstd = sb("rstd", [P, NT])
        mhalf = sb("mhalf", [P, NT])
        gam = sb("gam", [P, 4])
        lna = sb("lna", [P, NT])
        lnc = sb("lnc", [P, NT])
        ident = sb("ident", [P, P])
        identb = sb("identb", [P, P], BF16)
        maskb = sb("maskb", [P, 2, P], BF16)
        neg = sb("neg", [P, 2, P], F16)
        pick = sb("pick", [P, NH], F16)
        rbias = sb("rbias", [P, NE])
        gub = sb("gub", [P, NE, 4])
        gub64 = sb("gub64", [P, NE, 2])
        ub1 = sb("ub1", [P, NE, 2])
        tri = sb("tri", [P, NE * NE])
        rw16 = sb("rw16", [P, 2, KT, NE], F16)
        bdown = sb("bdown", [NE, D])
        stage2 = sb("stage2", [P, 2, WC])
        stage = stage2[:, :, :].rearrange("p a c -> p (a c)").rearrange("p (q c) -> p q c", q=4)
        w16 = sb("w16", [P, NE, 2 * WC], F16)
        xh0 = sb("xh0", [P, 2 * KT, HC], F16)
        lg = sb("lg", [P, HT, NE])
        rank = sb("rank", [P, HT, NE])
        rex = sb("rex", [P, HT, NE])
        rmx = sb("rmx", [P, HT])
        rsm = sb("rsm", [P, HT])
        sc = sb("sc", [P, HT, NE])
        sc64 = sb("sc64", [P, HT, NE])
        gbuf = sb("gbuf", [P, 2, HC])
        tbuf = sb("tbuf", [P, 2, HC])
        ubuf = sb("ubuf", [P, 2, HC])
        hhi = sb("hhi", [P, 2, HC], F16)
        hlo = sb("hlo", [P, 2, HC], F16)
        kst = sb("kst", [P, NH // 2, NB * SEQ], F16)
        vals = sb("vals", [P, 2 * NB, NH * VW])
        mx = sb("mx", [P, NB, NH])
        rs = sb("rs", [P, 2, NB])
        consts = gbuf[:, 0, :]
        maskf = gbuf[:, 0, 0:2 * P].rearrange("p (a c) -> p a c", a=2)
        negf = gbuf[:, 0, 2 * P:4 * P].rearrange("p (a c) -> p a c", a=2)
        pickf = gbuf[:, 1, 0:NH]
        rw = gbuf[:, 1, NH:NH + KT * NE].rearrange("p (k e) -> p k e", k=KT)
        wk_rep = tbuf[0:CD].rearrange("p a c -> p (a c)")
        wv = ubuf[0:CD, 0, 0:D]
        khi = hhi
        sigf = sig[:, :, :].rearrange("p t c -> p (t c)")
        xh = (xh0[:, :, :], sigf[:, 0:KT * HC].bitcast(F16).rearrange("p (k q) -> p k q", k=2 * KT))
        cmp = sigf[:, KT * HC:2 * KT * HC].rearrange("p (t e f) -> p t e f", t=HT, e=NE)
        scT = sigf[0:NE, KT * HC:KT * HC + HC]
        qst = simwork[:, :, :, :].rearrange("p a t c -> p (a t c)").bitcast(F16).rearrange("p (h q) -> p h q", h=NH)
        pT = sigf[:, 2 * HC:4 * HC].rearrange("p (k q) -> p k q", k=2)
        xTa = xh0[:, :, :].rearrange("p k q -> p (k q)").bitcast(F32).rearrange("p (k q) -> p k q", k=KT)
        wq_rep = stage2[:, :, :].rearrange("p a c -> p (a c)")[:, 0:KT * 4 * D].rearrange("p (k c) -> p k c", k=KT)
        qhi = stage2[:, :, :].rearrange("p a c -> p (a c)")[:, KT * 4 * D:KT * 4 * D + HC].bitcast(F16).rearrange("p (k c) -> p k c", k=2)
        nmx = stage2[:, :, :].rearrange("p a c -> p (a c)")[0:NH, KT * 4 * D + HC:KT * 4 * D + 2 * HC]
        g = [gbuf[:, i] for i in range(2)]
        tt = [tbuf[:, i] for i in range(2)]
        u = [ubuf[:, i] for i in range(2)]
        ao = ctx3[:, 0].rearrange("p (b c) -> p b c", b=NB)
        aoT = ctx3[:, 1].rearrange("p (k q) -> p k q", k=KT)
        nm = ctx3[:, 2, KT * D:KT * D + HC // 2].bitcast(F16)
        wout = ctx3[:, 2, 0:KT * D].rearrange("p (k c) -> p k c", k=KT)
        w32 = w16[:, :, :].rearrange("p e c -> p (e c)").bitcast(F32)
        place = [0]

        def carve(*shape):
            n = 1
            for v in shape:
                n *= v
            out = w32[:, place[0]:place[0] + n]
            place[0] += n
            if len(shape) == 2:
                return out.rearrange("p (a c) -> p a c", a=shape[0])
            return out

        d1, d2, aggw, bcw, gatew = carve(KT, HID), carve(HID // P, D), carve(KT, D), carve(KT, D), carve(KT, D)
        rows, cols = carve(4, D), carve(32)
        brow, gsum, yA, yB = carve(NB, D), carve(HT, D), carve(HT, D), carve(HT, D)
        zt = [carve(HT, D), carve(HT, D)]
        yl, cen, sq, nrm, th, act8 = carve(KT, NB), carve(KT, NB), carve(KT, NB), carve(KT, NB), carve(KT, NB), carve(HID // P, NB)
        cvar, crs, chalf, mean4 = carve(NB), carve(NB), carve(NB), carve(P)

        in_ctx, in_x, in_gam, in_const = sem("in_ctx"), sem("in_x"), sem("in_gam"), sem("in_const")
        in_w = [sem(f"in_w{q}") for q in range(4)]
        const_ready, gam_ready = sem("const_ready"), sem("gam_ready")
        l0_proj, l0_qk, sim_ready, sim_copied, sig_ready = (sem(n) for n in ("l0_proj", "l0_qk", "sim_ready", "sim_copied", "sig_ready"))
        top_ready, top_removed, masked, mask_t, sym_done, x1_done = (sem(n) for n in ("top_ready", "top_removed", "masked", "mask_t", "sym_done", "x1_done"))
        ln_x0 = sem("ln_x0")
        dve_step, chain_step = sem("dve_step"), sem("chain_step")
        vare_ready, rstd_ready, xn_ready = sem("vare_ready"), sem("rstd_ready"), sem("xn_ready")
        w_scaled, w_hi, w_lo = sem("w_scaled"), sem("w_hi"), sem("w_lo")
        t_ready, xhi_ready, xlo_ready = sem("t_ready"), sem("xhi_ready"), sem("xlo_ready")
        logit_ready, rdiff_ready, rexp_ready, sc_ready, scT_mm, scT_ready, bias_mm = (sem(n) for n in (
            "logit_ready", "rdiff_ready", "rexp_ready", "sc_ready", "scT_mm", "scT_ready", "bias_mm"))
        gu_ready, g_done, u_raw, u_done, tanh_done, glu_done, h_done, hhi_done, hlo_done, dn_ready, acc_done = (sem(n) for n in (
            "gu_ready", "g_done", "u_raw", "u_done", "tanh_done", "glu_done", "h_done", "hhi_done", "hlo_done", "dn_ready", "acc_done"))
        kwt_ready, kpsum, khi_ready, kcorr, kst_ready, vpsum, v_ready = (sem(n) for n in (
            "kwt_ready", "kpsum", "khi_ready", "kcorr", "kst_ready", "vpsum", "v_ready"))
        zero_ready, in_attn, xTa_ready, qpsum, qhi_ready, qcorr, q_ready = (sem(n) for n in (
            "zero_ready", "in_attn", "xTa_ready", "qpsum", "qhi_ready", "qcorr", "q_ready"))
        s_ready, mx_done, mxT_ready, nmx_ready, nm_ready, st_ready, exp_done, pv_done, rs_done, o_done = (sem(n) for n in (
            "s_ready", "mx_done", "mxT_ready", "nmx_ready", "nm_ready", "st_ready", "exp_done", "pv_done", "rs_done", "o_done"))
        aoT_psum, aoT_ready, wo_ready, x3_done = sem("aoT_psum"), sem("aoT_ready"), sem("wo_ready"), sem("x3_done")
        in_ffn, c_mm, c_v, c_var, c_rstd, c_gelu = (sem(n) for n in ("in_ffn", "c_mm", "c_v", "c_var", "c_rstd", "c_gelu"))
        brow_ready, gate_mm, z_ready, gate_ready, fin_ready = (sem(n) for n in ("brow_ready", "gate_mm", "z_ready", "gate_ready", "fin_ready"))
        out_done = sem("out_done")

        dstep = [0]

        def link(dve, ins):
            dstep[0] += 1
            ins.then_inc(dve_step, 1)
            dve.wait_ge(dve_step, dstep[0])

        block = ctx.enter_context(nc.Block())
        NCONST = 11
        NCV = 5
        FFN = ((d1, "d1"), (d2, "d2"), (aggw, "aggw"), (bcw, "bcw"), (gatew, "gatew"), (rows, "rows"), (cols, "cols"))
        NFFN = 16 * len(FFN)
        ADDS = HT * (NE + 1)

        @block.sync
        def _(sp):
            sp.dma_start(ctxT[:, :], a["ctxT"]).then_inc(in_ctx, 16)
            sp.dma_start(wqk0[:, :], a["wqk0"]).then_inc(in_ctx, 16)
            sp.dma_start(x[:, :, :], a["x"]).then_inc(in_x, 16)
            for dst, n in ((gam[:, 0:1], "gamma"), (mhalf[:, :], "mhalf")):
                sp.dma_start(dst, a[n]).then_inc(in_gam, 16)
            for dst, n in ((wk_rep, "wk_rep"), (wv, "wv"), (ident[:, :], "ident"), (maskf, "masks"), (negf, "neg"),
                           (pickf, "pick"), (rbias[:, :], "rbias"), (gub[:, :, :], "gub"), (tri[:, :], "tri"), (rw, "rw"),
                           (bdown[:, :], "bdown")):
                sp.dma_start(dst, a[n]).then_inc(in_const, 16)
            for q in range(4):
                sp.dma_start(stage[:, q, :], a["w_exp"][q // 2, :, (q % 2) * WP:(q % 2 + 1) * WP]).then_inc(in_w[q], 16)
            with sp.Fori(1, NE // 2) as i:
                for q in range(4):
                    sp.wait_ge(w_lo, 4 * i + q - 3)
                    sp.dma_start(stage[:, q, :], a["w_exp"][bass.ds(2 * i + q // 2, 1), :, (q % 2) * WP:(q % 2 + 1) * WP]
                                 .rearrange("e p c -> p (e c)")).then_inc(in_w[q], 16)
            sp.wait_ge(w_lo, 2 * NE)
            sp.dma_start(wq_rep, a["wq_rep"]).then_inc(in_attn, 16)
            sp.wait_ge(sim_ready, NT)
            sp.dma_start(wout, a["wout"]).then_inc(in_attn, 16)
            sp.wait_ge(dn_ready, 2 * (NE + 8))
            for dst, n in FFN:
                sp.dma_start(dst, a[n]).then_inc(in_ffn, 16)
            sp.wait_ge(fin_ready, 2 * HT)
            sp.dma_start(a["out"], x[:, :, :]).then_inc(out_done, 16)
            sp.wait_ge(out_done, 16)

        @block.tensor
        def _(pe):
            pe.wait_ge(in_ctx, 32)
            for j in range(2):
                for w in range(2):
                    pe.matmul(psum[2 * w + j][0:CD, :], wqk0[:, w * CD:(w + 1) * CD], ctxT[:, j * 512:(j + 1) * 512],
                              start=True, stop=True).then_inc(l0_proj, 1)
            for b in range(NB):
                pe.wait_ge(l0_qk, 4 * (b // 2) // 2 + 2)
                for half in range(2):
                    t, r = half * HT + b, 1 - half
                    pe.matmul(psum[4 + t // 2][:, (t % 2) * SEQ:(t % 2 + 1) * SEQ],
                              qT0[:, b * SEQ + r * P:b * SEQ + (r + 1) * P], kT0[:, b * SEQ:(b + 1) * SEQ],
                              start=True, stop=True).then_inc(sim_ready, 1)
            pe.wait_ge(in_const, 16 * NCONST)
            for m in range(4):
                if m >= 2:
                    pe.wait_ge(v_ready, m - 1)
                for c in range(2):
                    t = 2 * m + c
                    mm = pe.matmul(psum[2 + m % 2][:, c * D:(c + 1) * D], ctxT[:, t * P:(t + 1) * P], wv, start=True, stop=True)
                mm.then_inc(vpsum, 1)
            pe.wait_ge(kwt_ready, 1)
            for i in range(NH // 2):
                for j in range(2):
                    if i:
                        pe.wait_ge(kst_ready, 2 * i + j - 1)
                    pe.matmul(psum[j][:, :], wk_rep[:, i * P:(i + 1) * P], ctxT[:, j * 512:(j + 1) * 512],
                              start=True, stop=True).then_inc(kpsum, 1)
                if i == 0:
                    pe.wait_ge(const_ready, 1)
                for j in range(2):
                    pe.wait_ge(khi_ready, 2 * i + j + 1)
                    pe.matmul(psum[j][:, :], neg[:, 1, :], khi[:, j, :], start=False, stop=True,
                              skip_group_check=True).then_inc(kcorr, 1)
            pe.wait_ge(masked, NT)
            pe.wait_ge(kst_ready, NH)
            pe.wait_ge(v_ready, 4)
            for m in range(NT // 2):
                for t in (2 * m, 2 * m + 1):
                    b, r = t % HT, 1 - t // HT
                    for kc in range(2):
                        src = (1 - kc) * HT + b
                        mm = pe.transpose(psum[m][:, (t % 2) * SEQ + kc * P:(t % 2) * SEQ + (kc + 1) * P],
                                          work[:, src, r * P:(r + 1) * P], ident[:, :])
                mm.then_inc(mask_t, 1)

            def turn_xn(n):
                src = {3: yA, 5: yB}.get(n, xn)
                pe.wait_ge(xn_ready, HT * (n + 1))
                for kt in range(KT):
                    for j in range(HT):
                        mm = pe.transpose(psum[6 + kt][:, j * P:(j + 1) * P], src[:, j, kt * P:(kt + 1) * P], ident[:, :])
                    mm.then_inc(t_ready, 1)

            def logits(half):
                for j in range(HT):
                    n = 0
                    for kt in range(KT):
                        for xpart, wpart in ((0, 0), (0, 1), (KT, 0)):
                            mm = pe.matmul(psum[7][:, j * NE:(j + 1) * NE], xh[half][:, xpart + kt, j * P:(j + 1) * P], rw16[:, wpart, kt, :],
                                           start=(n == 0), stop=(n == 5))
                            n += 1
                mm.then_inc(logit_ready, 1)

            def gate_up(half, e, d, first=False):
                gi = half * NE + e
                for which, bank, read in ((0, psum[d], g_done), (1, psum[2 + d], u_raw)):
                    if not first:
                        pe.wait_ge(read, 2 * gi + d - 1)
                    n = 0
                    for kt in range(KT):
                        for wpart, xpart in ((0, 0), (0, KT), (1, 0)):
                            c0 = wpart * WC + kt * 2 * D + which * D + d * P
                            mm = pe.matmul(bank[:, :], w16[:, bass.ds(e, 1), c0:c0 + P].rearrange("p a c -> p (a c)"),
                                           xh[half][:, xpart + kt, :], start=(n == 0), stop=(n == 5))
                            n += 1
                    mm.then_inc(gu_ready, 1)

            def down(half, e, k):
                if k == 0:
                    pe.wait_ge(hlo_done, 2 * (half * NE + e) + 2)
                pe.wait_ge(acc_done, ADDS * half + 4 * e + 2 * k + 2)
                for j in (2 * k, 2 * k + 1):
                    n = 0
                    for d in range(2):
                        for hpart, wpart in ((hhi, 0), (hhi, 1), (hlo, 0)):
                            c0 = wpart * WC + KT * 2 * D + d * D
                            mm = pe.matmul(psum[4 + k][:, (j % 2) * D:(j % 2 + 1) * D], hpart[:, d, j * P:(j + 1) * P],
                                           w16[:, bass.ds(e, 1), c0:c0 + D].rearrange("p a c -> p (a c)"),
                                           start=(n == 0), stop=(n == 5))
                            n += 1
                mm.then_inc(dn_ready, 1)

            def weighed_biases(half):
                pe.wait_ge(sc_ready, half + 1)
                for j in range(HT):
                    mm = pe.transpose(psum[6][0:NE, j * P:(j + 1) * P], sc[:, j, :], ident[:, :])
                mm.then_inc(scT_mm, 1)
                pe.wait_ge(scT_ready, half + 1)
                for j in range(HT):
                    mm = pe.matmul(psum[6 + j // 2][:, (j % 2) * D:(j % 2 + 1) * D], scT[:, j * P:(j + 1) * P], bdown[:, :],
                                   start=True, stop=True)
                    if j % 2:
                        mm.then_inc(bias_mm, 1)

            def expert(half, e, before=None, middle=None, between=None, inside=None):
                for d, extra in ((0, before), (1, middle)):
                    if extra:
                        extra()
                    gate_up(half, e, d)
                if between:
                    between()
                down(half, e - 1, 0)
                if inside:
                    inside()
                down(half, e - 1, 1)

            def project_q(half):
                pe.wait_ge(in_attn, 32)
                pe.wait_ge(xTa_ready, KT * (1 + 2 * half))
                for i in range(NH // 2 + 1):
                    n = 8 * half + i
                    if i < NH // 2:
                        if i >= 2:
                            pe.wait_ge(q_ready, 2 * (n - 1))
                        for kt in range(KT):
                            mm = pe.matmul(psum[6 + i % 2][:, :], wq_rep[:, kt, i * P:(i + 1) * P], xTa[:, kt, :],
                                           start=(kt == 0), stop=(kt == KT - 1))
                        mm.then_inc(qpsum, 1)
                    if i:
                        pe.wait_ge(qhi_ready, n)
                        pe.matmul(psum[6 + (i - 1) % 2][:, :], neg[:, 0, :], qhi[:, (i - 1) % 2, :], start=False, stop=True,
                                  skip_group_check=True).then_inc(qcorr, 1)

            def scores(half, i, hh):
                n = NH * half + 2 * i + hh
                width = SEQ if half == 0 else P
                for k in range(2):
                    pe.wait_ge(mx_done, 2 * n + k + 1)
                    for c in range(2):
                        b = 2 * k + c
                        pe.matmul(psum[6 + k][:, c * width:(c + 1) * width],
                                  qst[:, bass.ds(2 * i + hh, 1), b * P:(b + 1) * P].rearrange("p a c -> p (a c)"),
                                  kst[:, bass.ds(i, 1), b * SEQ:b * SEQ + width].rearrange("p a c -> p (a c)"), start=True, stop=False)
                        mm = pe.matmul(psum[6 + k][:, (c + 1) * width - P:(c + 1) * width], identb[:, :], maskb[:, 0, :],
                                       start=False, stop=True)
                    mm.then_inc(s_ready, 1)

            def turn_maxima(half):
                pe.wait_ge(mx_done, 2 * NH * (half + 1) + 2)
                for b in range(NB):
                    mm = pe.transpose(psum[6][0:NH, b * P:(b + 1) * P], mx[:, b, :], ident[:, :])
                mm.then_inc(mxT_ready, 1)

            def scores_t(half, i, hh, kt, bank):
                diagonal = kt == 1 or half == 1
                pe.matmul(bank[:, :], pick[:, bass.ds(2 * i + hh, 1)].broadcast_to([P, P]), nm, start=True, stop=False)
                if diagonal:
                    pe.matmul(bank[:, :], identb[:, :], maskb[:, 1, :].unsqueeze(1).broadcast_to([P, NB, P]), start=False, stop=False)
                for b in range(NB):
                    mm = pe.matmul(bank[:, b * P:(b + 1) * P],
                                   kst[:, bass.ds(i, 1), b * SEQ + kt * P:b * SEQ + (kt + 1) * P].rearrange("p a c -> p (a c)"),
                                   qst[:, bass.ds(2 * i + hh, 1), b * P:(b + 1) * P].rearrange("p a c -> p (a c)"),
                                   start=False, stop=(b == NB - 1))
                mm.then_inc(st_ready, 1)

            def weigh(i, hh, kts, slots, bank):
                for b in range(NB):
                    for kt, slot in zip(kts, slots):
                        mm = pe.matmul(bank[:, b * VW:(b + 1) * VW], pT[:, slot, b * P:(b + 1) * P],
                                       vals[:, 2 * b + kt, bass.ds((2 * i + hh) * VW, VW)],
                                       start=(kt == 0), stop=(kt == kts[-1]))
                mm.then_inc(pv_done, 1)

            def scores_t0(i, hh):
                pe.wait_ge(o_done, 2 * i + hh + 2)
                for kt in range(2):
                    scores_t(0, i, hh, kt, psum[6 + kt])

            def weigh0(i, hh):
                pe.wait_ge(exp_done, 4 * i + 2 * hh + 2)
                weigh(i, hh, (0, 1), (0, 1), psum[6])

            def project_out(half):
                pe.wait_ge(o_done, NH * (half + 1) + 2)
                for kt in range(KT):
                    for b in range(NB):
                        mm = pe.transpose(psum[6 + kt][:, b * P:(b + 1) * P], ao[:, b, kt * P:(kt + 1) * P], ident[:, :])
                    mm.then_inc(aoT_psum, 1)
                pe.wait_ge(aoT_ready, 2 * (half + 1))
                for j in range(HT):
                    for kt in range(KT):
                        mm = pe.matmul(psum[6 + j // 2][:, (j % 2) * D:(j % 2 + 1) * D], aoT[:, kt, j * P:(j + 1) * P], wout[:, kt, :],
                                       start=(kt == 0), stop=(kt == KT - 1))
                    if j % 2:
                        mm.then_inc(wo_ready, 1)

            turn_xn(0)
            pe.wait_ge(xhi_ready, KT)
            pe.wait_ge(xlo_ready, KT)
            pe.wait_ge(w_lo, 4)
            gate_up(0, 0, 0, first=True)
            gate_up(0, 0, 1, first=True)
            logits(0)
            gate_up(0, 1, 0)
            gate_up(0, 1, 1)
            weighed_biases(0)
            down(0, 0, 0)
            down(0, 0, 1)
            with pe.Fori(1, 4) as m:
                for s in range(2):
                    pe.wait_ge(w_lo, 4 * m + 2 * s + 2)
                    expert(0, 2 * m + s)
            turn_xn(1)
            with pe.Fori(4, NE // 2) as m:
                for s in range(2):
                    pe.wait_ge(w_lo, 4 * m + 2 * s + 2)
                    expert(0, 2 * m + s)

            pe.wait_ge(xhi_ready, 2 * KT)
            pe.wait_ge(xlo_ready, 2 * KT)
            gate_up(1, 0, 0)
            gate_up(1, 0, 1)
            down(0, NE - 1, 0)
            down(0, NE - 1, 1)
            logits(1)
            gate_up(1, 1, 0)
            gate_up(1, 1, 1)
            weighed_biases(1)
            down(1, 0, 0)
            down(1, 0, 1)
            pe.wait_ge(acc_done, ADDS + HT)
            turn_xn(2)
            project_q(0)
            pe.wait_ge(q_ready, NH)
            with pe.Fori(1, 3) as m:
                for s in range(2):
                    i = 4 * m + 2 * s - 4
                    expert(1, 2 * m + s, lambda: scores(0, i, 0), lambda: scores(0, i, 1),
                           lambda: scores(0, i + 1, 0), lambda: scores(0, i + 1, 1))
            turn_maxima(0)
            for e in (6, 7):
                expert(1, e)
            pe.wait_ge(nm_ready, 2)
            with pe.Fori(4, NE // 2) as m:
                for s in range(2):
                    i = 2 * m + s - 8
                    expert(1, 2 * m + s, lambda: scores_t0(i, 0), lambda: weigh0(i, 0),
                           lambda: scores_t0(i, 1), lambda: weigh0(i, 1))
            down(1, NE - 1, 0)
            down(1, NE - 1, 1)
            project_out(0)

            cbank = psum[5]
            pe.wait_ge(in_ffn, NFFN)

            def column_sum(src, c):
                pe.wait_ge(c_v, c)
                for kt in range(KT):
                    mm = pe.matmul(cbank[:, 0:NB], mean4, src[:, kt, :], start=(kt == 0), stop=(kt == KT - 1))
                mm.then_inc(c_mm, 1)

            def column_mm(w, src, kts, ms, c):
                pe.wait_ge(c_v, c)
                for m in range(ms):
                    for kt in range(kts):
                        mm = pe.matmul(cbank[:, m * NB:(m + 1) * NB], w[:, kt, m * P:(m + 1) * P], src[:, kt, :],
                                       start=(kt == 0), stop=(kt == kts - 1))
                mm.then_inc(c_mm, 1)

            def gates(half):
                pe.wait_ge(xTa_ready, KT * (2 + 2 * half))
                for j in range(HT):
                    for kt in range(KT):
                        mm = pe.matmul(psum[2 + j // 2][:, (j % 2) * D:(j % 2 + 1) * D], xTa[:, kt, j * P:(j + 1) * P], gatew[:, kt, :],
                                       start=(kt == 0), stop=(kt == KT - 1))
                    if j % 2:
                        mm.then_inc(gate_mm, 1)

            turn_xn(3)
            column_sum(yl, 1)
            gates(0)
            column_sum(sq, 2)
            turn_xn(4)
            column_mm(aggw, nrm, KT, KT, 3)
            project_q(1)
            pe.wait_ge(q_ready, 2 * NH)
            with pe.Fori(0, NH // 2) as i:
                for hh in range(2):
                    scores(1, i, hh)
            turn_maxima(1)
            pe.wait_ge(nm_ready, 4)

            def scores_t1(i, k):
                for hh in range(2):
                    pe.wait_ge(o_done, NH + 2 * i + hh + 1)
                    scores_t(1, i, hh, 0, psum[6 + hh])

            def weigh1(i):
                for hh in range(2):
                    pe.wait_ge(exp_done, 2 * NH + 2 * i + hh + 1)
                    weigh(i, hh, (0,), (hh,), psum[6 + hh])

            with pe.Fori(0, STEPS) as k:
                column_sum(th, 4 * k + 4)
                scores_t1(2 * k, k)
                column_sum(sq, 4 * k + 5)
                weigh1(2 * k)
                column_mm(d1, nrm, KT, HID // P, 4 * k + 6)
                scores_t1(2 * k + 1, k)
                column_mm(d2, act8, HID // P, KT, 4 * k + 7)
                weigh1(2 * k + 1)
            project_out(1)
            pe.wait_ge(c_v, 4 * STEPS + 4)
            for b in range(NB):
                for kt in range(KT):
                    mm = pe.matmul(psum[b // 2][:, (b % 2) * D:(b % 2 + 1) * D], th[:, kt, b:b + 1].broadcast_to([P, P]), bcw[:, kt, :],
                                   start=(kt == 0), stop=(kt == KT - 1))
            mm.then_inc(c_mm, 1)
            turn_xn(5)
            gates(1)

        @block.scalar
        def _(act):
            for n in range(4):
                act.wait_ge(l0_proj, n + 1)
                j, w = n // 2, n % 2
                dst = (qT0, kT0)[w]
                act.activation(dst[:, j * 512:(j + 1) * 512], psum[2 * w + j][0:CD, :], ACT.Copy).then_inc(l0_qk, 1)
            act.wait_ge(in_gam, 32)
            act.activation(gam[:, 1:2], gam[:, 0:1], ACT.Tanh, scale=0.5).then_inc(gam_ready, 1)
            for dst in (work, sim):
                for bank, need in ((0, 3), (2, 4), (1, 7), (3, 8)):
                    act.wait_ge(sim_ready, need)
                    act.activation(dst[:, 2 * bank:2 * bank + 2, :], psum[4 + bank][:, :].rearrange("p (a c) -> p a c", a=2),
                                   ACT.Copy).then_inc(sim_copied, 1)
            act.wait_ge(ln_x0, 2)
            for t in range(NT):
                act.activation(x[:, t, :], x[:, t, :], ACT.Identity, bias=lnc[:, t:t + 1], scale=lna[:, t:t + 1]).then_inc(ln_x0, 1)
            act.wait_ge(sim_copied, 8)
            for m in range(4):
                act.activation(sig[:, 2 * m:2 * m + 2, :], sim[:, 2 * m:2 * m + 2, :], ACT.Tanh, scale=1 / 32).then_inc(sig_ready, 1)
            for m in range(4):
                act.wait_ge(sig_ready, m + 1)
                act.activation(sig[:, 2 * m:2 * m + 2, :], sig[:, 2 * m:2 * m + 2, :], ACT.Copy, bias=1.0).then_inc(sig_ready, 1)
            act.wait_ge(zero_ready, 1)
            for m in range(4):
                act.wait_ge(vpsum, m + 1)
                act.activation(vals[:, 2 * m:2 * m + 2, :].rearrange("p t (h v) -> p t h v", v=VW)[:, :, :, 0:HD],
                               psum[2 + m % 2][:, :].rearrange("p (t h v) -> p t h v", t=2, h=NH), ACT.Copy).then_inc(v_ready, 1)
            act.activation(wk_rep, wk_rep, ACT.Copy, scale=KS).then_inc(kwt_ready, 1)

            def split_part(i, q):
                act.wait_ge(in_w[q], 16 * i + 16)
                act.activation(w16[:, bass.ds(2 * i + q // 2, 1), (q % 2) * WP:(q % 2 + 1) * WP].rearrange("p a c -> p (a c)"),
                               stage[:, q, :], ACT.Copy, scale=WS).then_inc(w_hi, 1)
                act.activation(stage[:, q, :], stage[:, q, :], ACT.Copy, scale=WS).then_inc(w_scaled, 1)

            def key_part(i, q):
                j = q % 2
                if q < 2:
                    act.wait_ge(kpsum, 2 * i + j + 1)
                    act.activation(khi[:, j, :], psum[j][:, :], ACT.Copy).then_inc(khi_ready, 1)
                else:
                    act.wait_ge(kcorr, 2 * i + j + 1)
                    act.activation(kst[:, bass.ds(i, 1), j * 512:(j + 1) * 512].rearrange("p a c -> p (a c)"), psum[j][:, :],
                                   ACT.Copy).then_inc(kst_ready, 1)

            with act.Fori(0, NCV) as i:
                for q in range(4):
                    split_part(i, q)
                    key_part(i, q)
            with act.Fori(NCV, NE // 2) as i:
                for q in range(4):
                    key_part(i, q)

            def high_parts(half):
                for kt in range(KT):
                    act.wait_ge(t_ready, KT * half + kt + 1)
                    act.activation(xh[half][:, kt, :], psum[6 + kt][:, :], ACT.Copy).then_inc(xhi_ready, 1)

            def ups(half, e, d, first=False):
                gi = half * NE + e
                act.wait_ge(gu_ready, 4 * gi + 2 * d + 2)
                if not first:
                    act.wait_ge(hlo_done, 2 * gi + d - 1)
                act.activation(u[d], psum[2 + d][:, :], ACT.Identity, scale=1 / WS,
                               bias=ub1[:, bass.ds(e, 1), d:d + 1].rearrange("p a c -> p (a c)")).then_inc(u_raw, 1)
                act.wait_ge(g_done, 2 * gi + d + 1)
                act.activation(tt[d], g[d], ACT.Tanh, scale=ALPHA / 2 / WS).then_inc(tanh_done, 1)

            def highs(half, e, d, first=False):
                gi = half * NE + e
                if not first:
                    act.wait_ge(dn_ready, 2 * gi)
                act.wait_ge(h_done, 2 * gi + d + 1)
                act.activation(hhi[:, d, :], u[d], ACT.Copy).then_inc(hhi_done, 1)

            def expert(half, e, first=False, before=None, between=None):
                if before:
                    before()
                for d in range(2):
                    ups(half, e, d, first)
                if between:
                    between()
                for d in range(2):
                    highs(half, e, d, first)

            def scores_out(half):
                act.wait_ge(rdiff_ready, half + 1)
                act.activation(rex[:, :, :], rex[:, :, :], ACT.Exp).then_inc(rexp_ready, 1)
                act.wait_ge(scT_mm, half + 1)
                act.activation(scT, psum[6][0:NE, :], ACT.Copy).then_inc(scT_ready, 1)

            def copy_turned(n):
                for kt in range(KT):
                    act.wait_ge(t_ready, KT * n + kt + 1)
                    act.activation(xTa[:, kt, :], psum[6 + kt][:, :], ACT.Copy).then_inc(xTa_ready, 1)

            def queries(half):
                for i in range(NH // 2 + 1):
                    n = 8 * half + i
                    if i < NH // 2:
                        act.wait_ge(qpsum, n + 1)
                        act.activation(qhi[:, i % 2, :], psum[6 + i % 2][:, :], ACT.Copy).then_inc(qhi_ready, 1)
                    if i:
                        act.wait_ge(qcorr, n)
                        for hh in range(2):
                            r = slice(hh * 64, hh * 64 + 64)
                            act.activation(qst[r, 2 * i - 2 + hh, :], psum[6 + (i - 1) % 2][r, :], ACT.Copy).then_inc(q_ready, 1)

            def maxima_out(half):
                act.wait_ge(mxT_ready, half + 1)
                act.activation(nm[0:NH, :], psum[6][0:NH, :], ACT.Copy, scale=-1.0).then_inc(nm_ready, 1)
                act.activation(nmx, psum[6][0:NH, :], ACT.Copy, scale=-1.0).then_inc(nmx_ready, 1)

            def exps(half, i, hh):
                for kt in range(2 - half):
                    n = (4 * i + 2 * hh + kt) if half == 0 else (2 * NH + 2 * i + hh)
                    slot = hh if half else kt
                    act.wait_ge(st_ready, n + 1)
                    act.activation(pT[:, slot, :], psum[6 + slot][:, :], ACT.Exp, scale=HD ** -0.5 / KS).then_inc(exp_done, 1)

            def turned_out(half):
                for kt in range(KT):
                    act.wait_ge(aoT_psum, 2 * half + kt + 1)
                    act.activation(aoT[:, kt, :], psum[6 + kt][:, :], ACT.Copy).then_inc(aoT_ready, 1)

            high_parts(0)
            expert(0, 0, first=True)
            scores_out(0)
            expert(0, 1)
            with act.Fori(1, 4) as m:
                for s in range(2):
                    expert(0, 2 * m + s)
                    for q in (2 * s, 2 * s + 1):
                        split_part(m + NCV - 1, q)
            high_parts(1)
            with act.Fori(4, NE // 2) as m:
                for s in range(2):
                    expert(0, 2 * m + s)

            expert(1, 0)
            scores_out(1)
            expert(1, 1)
            act.wait_ge(zero_ready, 3)
            copy_turned(2)
            queries(0)
            with act.Fori(1, 3) as m:
                for s in range(2):
                    expert(1, 2 * m + s)
            maxima_out(0)
            for e in (6, 7):
                expert(1, e)
            with act.Fori(4, NE // 2) as m:
                for s in range(2):
                    i = 2 * m + s - 8
                    expert(1, 2 * m + s, before=lambda: exps(0, i, 0), between=lambda: exps(0, i, 1))
            turned_out(0)

            def gate_tanh(half):
                for m in range(2):
                    act.wait_ge(z_ready, 2 * half + m + 1)
                    two = slice(2 * m, 2 * m + 2)
                    act.activation(zt[half][:, two, :], zt[half][:, two, :], ACT.Tanh, scale=0.5).then_inc(gate_ready, 1)

            copy_turned(3)
            gate_tanh(0)
            act.wait_ge(c_v, 1)
            copy_turned(4)
            queries(1)
            maxima_out(1)
            with act.Fori(0, STEPS) as k:
                for hh in range(2):
                    exps(1, 2 * k, hh)
                act.wait_ge(c_gelu, k + 1)
                act.activation(act8[:, :, :], act8[:, :, :], ACT.Gelu).then_inc(c_v, 1)
                for hh in range(2):
                    exps(1, 2 * k + 1, hh)
            turned_out(1)
            copy_turned(5)
            gate_tanh(1)

        @block.gpsimd
        def _(pool):
            def power(n, sl):
                pool.wait_ge(vare_ready, n)
                pool.tensor_tensor(rstd[:, sl], vare[:, sl], mhalf[:, sl], ALU.pow).then_inc(rstd_ready, 1)

            pool.memset(vals[:, :, :].rearrange("p t (h v) -> p t h v", v=VW)[:, :, :, HD:VW], 1.0).then_inc(zero_ready, 1)
            pool.wait_ge(in_gam, 32)
            power(1, slice(0, NT))
            def split_part(i, q):
                pool.wait_ge(w_scaled, 4 * i + q + 1)
                e, c0 = bass.ds(2 * i + q // 2, 1), (q % 2) * WP
                pool.tensor_tensor(w16[:, e, WC + c0:WC + c0 + WP].rearrange("p a c -> p (a c)"), stage[:, q, :],
                                   w16[:, e, c0:c0 + WP].rearrange("p a c -> p (a c)"), ALU.subtract).then_inc(w_lo, 1)

            def lows(gi):
                for d in range(2):
                    pool.wait_ge(hhi_done, 2 * gi + d + 1)
                    pool.tensor_tensor(hlo[:, d, :], u[d], hhi[:, d, :], ALU.subtract).then_inc(hlo_done, 1)

            with pool.Fori(0, NCV) as i:
                for q in range(4):
                    split_part(i, q)
            pool.wait_ge(x1_done, 4)
            power(2, slice(0, HT))
            pool.memset(ctx3[:, 2, KT * D:KT * D + HC // 2], 0.0).then_inc(zero_ready, 1)
            pool.memset(simwork[:, :, :, :].rearrange("p a t c -> p (a t c)"), 0.0).then_inc(zero_ready, 1)
            lows(0)
            lows(1)
            with pool.Fori(1, 4) as m:
                for s in range(2):
                    lows(2 * m + s)
                    for q in (2 * s, 2 * s + 1):
                        split_part(m + NCV - 1, q)
            power(3, slice(0, HT))
            with pool.Fori(4, NE // 2) as m:
                for s in range(2):
                    lows(2 * m + s)
            lows(NE)
            lows(NE + 1)
            power(4, slice(0, HT))
            with pool.Fori(1, NE // 2) as m:
                for s in range(2):
                    lows(2 * m + s + NE)
            power(5, slice(0, HT))

            def chain_power(n):
                pool.wait_ge(c_var, n)
                pool.tensor_tensor(crs, cvar, chalf, ALU.pow).then_inc(c_rstd, 1)

            chain_power(1)
            power(6, slice(0, HT))
            with pool.Fori(0, STEPS) as k:
                chain_power(k + 2)
            for n in (7, 8, 9):
                power(n, slice(0, HT))

        @block.vector
        def _(dve):
            def stats(src, k, n, eps):
                for j in range(k):
                    ins = dve.bn_stats(bn[:, j, :], src[:, j, :])
                link(dve, ins)
                for j in range(k):
                    ins = dve.bn_aggr(mv[:, j, :], bn[:, j, :])
                link(dve, ins)
                dve.tensor_scalar(vare[:, 0:k], mv[:, 0:k, 1], eps, None, ALU.add).then_inc(vare_ready, 1)
                dve.wait_ge(rstd_ready, n)

            dve.wait_ge(in_x, 16)
            dve.sem_inc(mx_done, 2)
            dve.sem_inc(o_done, 2)
            stats(x, NT, 1, 1e-5)
            dve.wait_ge(gam_ready, 1)
            link(dve, dve.tensor_scalar(gam[:, 2:3], gam[:, 1:2], -0.5, 0.5, ALU.mult, ALU.add))
            dve.tensor_scalar(gam[:, 3:4], gam[:, 1:2], 0.125, 0.125, ALU.mult, ALU.add)
            dve.tensor_scalar(lna[:, :], rstd[:, :], gam[:, 2:3], 1.0, ALU.mult, ALU.add).then_inc(ln_x0, 1)
            link(dve, dve.scalar_tensor_tensor(lnc[:, :], mv[:, :, 0], gam[:, 2:3], rstd[:, :], ALU.mult, ALU.mult))
            dve.tensor_scalar(lnc[:, :], lnc[:, :], -1.0, None, ALU.mult).then_inc(ln_x0, 1)
            order = (0, 1, 4, 5, 2, 3, 6, 7)
            for n, t in enumerate(order):
                dve.wait_ge(sim_copied, n // 2 + 1)
                dve.max(top[:, t, :], work[:, t, :]).then_inc(top_ready, 1)
            dve.wait_ge(in_const, 16 * NCONST)
            dve.tensor_copy(identb[:, :], ident[:, :])
            dve.tensor_copy(maskb[:, :, :], maskf)
            dve.tensor_copy(neg[:, :, :], negf)
            dve.tensor_copy(pick[:, :], pickf)
            link(dve, dve.tensor_scalar(rw16[:, 0], rw, WS, None, ALU.mult))
            dve.scalar_tensor_tensor(rw16[:, 1], rw, WS, rw16[:, 0], ALU.mult, ALU.subtract)
            dve.tensor_scalar(gub64[:, :, :], gub[:, :, 0:2], WS, None, ALU.mult)
            dve.tensor_scalar(ub1[:, :, :], gub[:, :, 2:4], 1.0, None, ALU.add).then_inc(const_ready, 1)
            for i in range(TOPK // 8):
                for n, t in enumerate(order):
                    dve.wait_ge(top_ready, NT * i + n + 1)
                    dve.match_replace(work[:, t, :], top[:, t, :], work[:, t, :], -3e38).then_inc(top_removed, 1)
                for n, t in enumerate(order):
                    dve.wait_ge(top_removed, NT * i + n + 1)
                    dve.max(top[:, t, :], work[:, t, :]).then_inc(top_ready, 1)
            kth = TOPK % 8 - 1
            dve.wait_ge(top_ready, NT * (TOPK // 8 + 1))
            dve.wait_ge(sig_ready, 8)
            for t in range(NT):
                dve.scalar_tensor_tensor(work[:, t, :], sim[:, t, :], top[:, t, kth:kth + 1], sig[:, t, :],
                                         ALU.is_ge, ALU.mult).then_inc(masked, 1)
            dve.wait_ge(masked, NT)
            dve.wait_ge(ln_x0, 2 + NT)
            for m in range(NT // 2):
                dve.wait_ge(mask_t, m + 1)
                dve.tensor_tensor(sim[:, 2 * m:2 * m + 2, :], work[:, 2 * m:2 * m + 2, :],
                                  psum[m][:, :].rearrange("p (a c) -> p a c", a=2), ALU.add).then_inc(sym_done, 1)
            for m in range(NT // 2):
                dve.wait_ge(sym_done, m + 1)
                dve.scalar_tensor_tensor(x[:, 2 * m:2 * m + 2, :], sim[:, 2 * m:2 * m + 2, :], gam[:, 3:4],
                                         x[:, 2 * m:2 * m + 2, :], ALU.mult, ALU.add).then_inc(x1_done, 1)
            def normalise(half, n, dst=None):
                stats(x[:, half * HT:(half + 1) * HT], HT, len(rounds) + 2, 1e-5)
                rounds.append(n)
                dst = xn if dst is None else dst
                if n:
                    dve.wait_ge(t_ready, KT * n)
                for j in range(HT):
                    dve.tensor_scalar(dst[:, j, :], x[:, half * HT + j, :], mv[:, j, 0:1], rstd[:, j:j + 1],
                                      ALU.subtract, ALU.mult).then_inc(xn_ready, 1)

            def low_parts(half):
                for kt in range(KT):
                    dve.wait_ge(xhi_ready, KT * half + kt + 1)
                    dve.tensor_tensor(xh[half][:, KT + kt, :], psum[6 + kt][:, :], xh[half][:, kt, :], ALU.subtract).then_inc(xlo_ready, 1)

            def router(half):
                dve.wait_ge(logit_ready, half + 1)
                link(dve, dve.scalar_tensor_tensor(lg[:, :, :], psum[7][:, 0:HT * NE].rearrange("p (t e) -> p t e", t=HT), 1 / WS,
                                                   rbias[:, :].unsqueeze(1).broadcast_to([P, HT, NE]), ALU.mult, ALU.add))
                link(dve, dve.tensor_reduce(rmx[:, :], lg[:, :, :], AXX, ALU.max))
                dve.tensor_tensor(rex[:, :, :], lg[:, :, :], rmx[:, :].unsqueeze(2).broadcast_to([P, HT, NE]),
                                  ALU.subtract).then_inc(rdiff_ready, 1)
                mine = lg[:, :, :].unsqueeze(3).broadcast_to([P, HT, NE, NE])
                other = lg[:, :, :].unsqueeze(2).broadcast_to([P, HT, NE, NE])
                cmpf = cmp.rearrange("p t e f -> p t (e f)")
                link(dve, dve.tensor_tensor(cmp, other, mine, ALU.is_equal))
                link(dve, dve.tensor_tensor(cmpf, cmpf, tri[:, :].unsqueeze(1).broadcast_to([P, HT, NE * NE]), ALU.mult))
                link(dve, dve.tensor_reduce(sc[:, :, :], cmp, AXX, ALU.add))
                link(dve, dve.tensor_tensor(cmp, other, mine, ALU.is_gt))
                link(dve, dve.tensor_reduce(rank[:, :, :], cmp, AXX, ALU.add))
                link(dve, dve.tensor_tensor(rank[:, :, :], rank[:, :, :], sc[:, :, :], ALU.add))
                dve.wait_ge(rexp_ready, half + 1)
                link(dve, dve.scalar_tensor_tensor(rex[:, :, :], rank[:, :, :], float(NTOP), rex[:, :, :], ALU.is_lt, ALU.mult))
                link(dve, dve.tensor_reduce(rsm[:, :], rex[:, :, :], AXX, ALU.add))
                link(dve, dve.reciprocal(rsm[:, :], rsm[:, :]))
                dve.tensor_tensor(sc[:, :, :], rex[:, :, :], rsm[:, :].unsqueeze(2).broadcast_to([P, HT, NE]),
                                  ALU.mult).then_inc(sc_ready, 1)
                dve.wait_ge(sc_ready, half + 1)
                link(dve, dve.tensor_scalar(sc64[:, :, :], sc[:, :, :], 1 / WS, None, ALU.mult))

            def act_fn(half, e, d):
                gi = half * NE + e
                dve.wait_ge(gu_ready, 4 * gi + 2 * d + 1)
                dve.tensor_scalar(g[d], psum[d][:, :], gub64[:, bass.ds(e, 1), d:d + 1].rearrange("p a c -> p (a c)"),
                                  GLIM * WS, ALU.add, ALU.min).then_inc(g_done, 1)
                dve.wait_ge(u_raw, 2 * gi + d + 1)
                dve.tensor_scalar(u[d], u[d], GLIM + 1, 1 - GLIM, ALU.min, ALU.max).then_inc(u_done, 1)
                dve.wait_ge(tanh_done, 2 * gi + d + 1)
                dve.scalar_tensor_tensor(tt[d], tt[d], 1.0, g[d], ALU.add, ALU.mult).then_inc(glu_done, 1)
                dve.wait_ge(glu_done, 2 * gi + d + 1)
                dve.wait_ge(u_done, 2 * gi + d + 1)
                dve.scalar_tensor_tensor(u[d], tt[d], 0.5 / WS, u[d], ALU.mult, ALU.mult).then_inc(h_done, 1)

            def add_out(half, e, k):
                gi = half * NE + e
                for j in (2 * k, 2 * k + 1):
                    t = half * HT + j
                    dve.wait_ge(dn_ready, 2 * gi + k + 1)
                    dve.scalar_tensor_tensor(x[:, t, :], psum[4 + k][:, (j % 2) * D:(j % 2 + 1) * D],
                                             sc64[:, j, bass.ds(e, 1)], x[:, t, :], ALU.mult, ALU.add).then_inc(acc_done, 1)

            def add_biases(half):
                for j in range(HT):
                    t = half * HT + j
                    dve.wait_ge(bias_mm, 2 * half + j // 2 + 1)
                    dve.tensor_tensor(x[:, t, :], x[:, t, :], psum[6 + j // 2][:, (j % 2) * D:(j % 2 + 1) * D], ALU.add).then_inc(acc_done, 1)
                dve.wait_ge(acc_done, ADDS * half + HT)

            def expert(half, e, before=None, middle=None, between=None, inside=None):
                for d, extra in ((0, before), (1, middle)):
                    if extra:
                        extra()
                    act_fn(half, e, d)
                if between:
                    between()
                add_out(half, e - 1, 0)
                if inside:
                    inside()
                add_out(half, e - 1, 1)

            def maxima(half, i, hh):
                n = NH * half + 2 * i + hh
                width = SEQ if half == 0 else P
                for k in range(2):
                    dve.wait_ge(s_ready, 2 * n + k + 1)
                    dve.tensor_reduce(mx[:, 2 * k:2 * k + 2, bass.ds(2 * i + hh, 1)],
                                      psum[6 + k][:, 0:2 * width].rearrange("p (b c) -> p b c", b=2), AXX, ALU.max).then_inc(mx_done, 1)

            def maxima_low(half):
                dve.wait_ge(nmx_ready, half + 1)
                dve.tensor_tensor(nm[32:32 + NH, :], nmx, nm[0:NH, :], ALU.subtract).then_inc(nm_ready, 1)

            def outputs(half, i, hh):
                n = NH * half + 2 * i + hh
                o = psum[6 + (hh if half else 0)][:, 0:NB * VW].rearrange("p (b v) -> p b v", v=VW)
                dve.wait_ge(pv_done, n + 1)
                dve.reciprocal(rs[:, hh, :], o[:, :, HD]).then_inc(rs_done, 1)
                dve.wait_ge(rs_done, n + 1)
                dve.tensor_tensor(ao[:, :, bass.ds((2 * i + hh) * HD, HD)], o[:, :, 0:HD],
                                  rs[:, hh, :].unsqueeze(2).broadcast_to([P, NB, HD]), ALU.mult).then_inc(o_done, 1)

            def add_attention(half):
                for j in range(HT):
                    t = half * HT + j
                    dve.wait_ge(wo_ready, 2 * half + j // 2 + 1)
                    dve.tensor_tensor(x[:, t, :], x[:, t, :], psum[6 + j // 2][:, (j % 2) * D:(j % 2 + 1) * D], ALU.add).then_inc(x3_done, 1)

            rounds = []
            dve.wait_ge(x1_done, 4)
            normalise(0, 0)
            low_parts(0)
            act_fn(0, 0, 0)
            act_fn(0, 0, 1)
            router(0)
            act_fn(0, 1, 0)
            act_fn(0, 1, 1)
            add_biases(0)
            add_out(0, 0, 0)
            add_out(0, 0, 1)
            with dve.Fori(1, 4) as m:
                for s in range(2):
                    expert(0, 2 * m + s)
            normalise(1, 1)
            low_parts(1)
            with dve.Fori(4, NE // 2) as m:
                for s in range(2):
                    expert(0, 2 * m + s)

            act_fn(1, 0, 0)
            act_fn(1, 0, 1)
            add_out(0, NE - 1, 0)
            add_out(0, NE - 1, 1)
            router(1)
            act_fn(1, 1, 0)
            act_fn(1, 1, 1)
            add_biases(1)
            add_out(1, 0, 0)
            add_out(1, 0, 1)
            normalise(0, 2)
            with dve.Fori(1, 3) as m:
                for s in range(2):
                    i = 4 * m + 2 * s - 4
                    expert(1, 2 * m + s, lambda: maxima(0, i, 0), lambda: maxima(0, i, 1),
                           lambda: maxima(0, i + 1, 0), lambda: maxima(0, i + 1, 1))
            maxima_low(0)
            for e in (6, 7):
                expert(1, e)
            with dve.Fori(4, NE // 2) as m:
                for s in range(2):
                    i = 2 * m + s - 8
                    expert(1, 2 * m + s, None, lambda: outputs(0, i, 0), None, lambda: outputs(0, i, 1))
            add_out(1, NE - 1, 0)
            add_out(1, NE - 1, 1)
            add_attention(0)

            def column(c, n=KT):
                return cols[:, c:c + n].unsqueeze(2).broadcast_to([P, n, NB])

            def pairs(v):
                return v.rearrange("p (a c) -> p a c", c=NB)

            def product(c, n=NB):
                dve.wait_ge(c_mm, c)
                return psum[5][:, 0:n]

            def centre(src, c):
                mean = product(c).unsqueeze(1).broadcast_to([P, KT, NB])
                dve.tensor_tensor(cen[:, :, :], src[:, :, :], mean, ALU.subtract).then_inc(chain_step, 1)
                dve.wait_ge(chain_step, c)
                dve.tensor_tensor(sq[:, :, :], cen[:, :, :], cen[:, :, :], ALU.mult).then_inc(c_v, 1)

            def scale_columns(c, ln, gcol, bcol):
                dve.tensor_scalar(cvar, product(c), 1e-6, None, ALU.add).then_inc(c_var, 1)
                dve.wait_ge(c_rstd, ln)
                dve.tensor_tensor(nrm[:, :, :], cen[:, :, :], crs.unsqueeze(1).broadcast_to([P, KT, NB]), ALU.mult).then_inc(chain_step, 1)
                dve.wait_ge(chain_step, c)
                dve.tensor_tensor(nrm[:, :, :], nrm[:, :, :], column(gcol), ALU.mult).then_inc(chain_step, 1)
                dve.wait_ge(chain_step, c + 1)
                dve.tensor_tensor(nrm[:, :, :], nrm[:, :, :], column(bcol), ALU.add).then_inc(c_v, 1)

            def gate_sums(half):
                for m in range(2):
                    dve.wait_ge(gate_mm, 2 * half + m + 1)
                    dve.tensor_tensor(zt[half][:, 2 * m:2 * m + 2, :], psum[2 + m][:, :].rearrange("p (b c) -> p b c", b=2),
                                      rows[:, 0:1, :].broadcast_to([P, 2, D]), ALU.add).then_inc(z_ready, 1)

            dve.wait_ge(x3_done, HT)
            normalise(0, 3, yA)
            dve.memset(mean4, 1.0 / D)
            dve.memset(chalf, -0.5)
            dve.wait_ge(in_ffn, NFFN)
            dve.wait_ge(xTa_ready, KT * 2)
            dve.tensor_copy(yl[:, :, :], xTa.rearrange("p k (b q) -> p k b q", b=NB)[:, :, :, P - 1]).then_inc(c_v, 1)
            centre(yl, 1)
            gate_sums(0)
            scale_columns(2, 1, 0, 2)
            normalise(1, 4)
            dve.tensor_tensor(th[:, :, :], pairs(product(3, KT * NB)), column(4), ALU.add).then_inc(c_v, 1)
            with dve.Fori(0, NH // 2) as i:
                for hh in range(2):
                    maxima(1, i, hh)
            maxima_low(1)
            with dve.Fori(0, STEPS) as k:
                centre(th, 4 * k + 4)
                scale_columns(4 * k + 5, k + 2, 6, 8)
                outputs(1, 2 * k, 0)
                outputs(1, 2 * k, 1)
                dve.tensor_tensor(act8[:, :, :], pairs(product(4 * k + 6, HID // P * NB)), column(12, HID // P), ALU.add).then_inc(c_gelu, 1)
                dve.tensor_tensor(th[:, :, :], th[:, :, :], column(10), ALU.add).then_inc(chain_step, 1)
                dve.wait_ge(chain_step, 4 * k + 7)
                dve.tensor_tensor(th[:, :, :], th[:, :, :], pairs(product(4 * k + 7, KT * NB)), ALU.add).then_inc(c_v, 1)
                outputs(1, 2 * k + 1, 0)
                outputs(1, 2 * k + 1, 1)
            add_attention(1)

            product(4 * STEPS + 4)
            for m in range(2):
                ins = dve.tensor_tensor(brow[:, 2 * m:2 * m + 2, :], psum[m][:, :].rearrange("p (b c) -> p b c", b=2),
                                        rows[:, 3:4, :].broadcast_to([P, 2, D]), ALU.add)
            link(dve, ins)
            dve.wait_ge(x3_done, 2 * HT)
            normalise(1, 5, yB)
            for half in range(2):
                y = (yA, yB)[half]
                if half:
                    gate_sums(1)
                for m in range(2):
                    two = slice(2 * m, 2 * m + 2)
                    dve.wait_ge(gate_ready, 2 * half + m + 1)
                    link(dve, dve.scalar_tensor_tensor(gsum[:, two, :], zt[half][:, two, :], 1.0, brow[:, two, :], ALU.add, ALU.mult))
                    link(dve, dve.scalar_tensor_tensor(gsum[:, two, :], gsum[:, two, :], 0.5, y[:, two, :], ALU.mult, ALU.add))
                stats(gsum, HT, len(rounds) + 2, 1e-6)
                rounds.append("out")
                for j in range(HT):
                    t = half * HT + j
                    link(dve, dve.tensor_scalar(gsum[:, j, :], gsum[:, j, :], mv[:, j, 0:1], rstd[:, j:j + 1], ALU.subtract, ALU.mult))
                    dve.tensor_tensor(x[:, t, :], x[:, t, :], rows[:, 2, :], ALU.add)
                    link(dve, dve.tensor_tensor(gsum[:, j, :], gsum[:, j, :], rows[:, 1, :], ALU.mult))
                    dve.tensor_tensor(x[:, t, :], x[:, t, :], gsum[:, j, :], ALU.add).then_inc(fin_ready, 1)


def kernel(**inputs):
    import numpy as np
    import concourse.bacc as bacc
    from concourse.bass_utils import run_bass_kernel_spmd as run

    I = {k: np.asarray(v) for k, v in inputs.items()}
    f = np.float32

    def tiles(w):
        return np.ascontiguousarray(w.reshape(-1, P, w.shape[-1]).transpose(1, 0, 2))

    def spread(v):
        return np.ascontiguousarray(np.broadcast_to(v.reshape(1, -1), (P, v.size)))

    def column(v):
        return v.reshape(-1, P).T

    xs = I["x"].reshape(NB, 2, P, D)[:, ::-1].transpose(2, 1, 0, 3).reshape(P, NT, D)
    gu = I["L0_ffn_gate_up_proj"].reshape(NE, KT, P, D, 2).transpose(0, 2, 1, 4, 3).reshape(NE, P, KT * 2 * D)
    dn = I["L0_ffn_down_proj"].reshape(NE, KT, P, D).transpose(0, 2, 1, 3).reshape(NE, P, KT * D)
    gb = I["L0_ffn_gate_up_proj_bias"].reshape(NE, 2, P, 2).transpose(2, 0, 3, 1).reshape(P, NE, 4)
    i = np.arange(P)
    up = np.where(i[None, :] > i[:, None], f(NEG), f(0))
    e = np.arange(NE)
    group = i // HD % 4
    neg = np.stack([-np.diag((group == c).astype(f)) for c in (1, 2)], 1).astype(f)
    pick = np.where(i[:, None] % 32 == e[None, :], f(1), f(0)) * (i[:, None] < 64)
    pick = pick.astype(f)

    def stacked(w, copies):
        w = w.reshape(-1, NH, 1, HD)
        none = np.zeros((w.shape[0], NH, 4 - copies, HD), f)
        return np.concatenate([w] * copies + [none], 2).reshape(w.shape[0], NH * 64)

    wk_rep = stacked(I["L1_xattn_Wkv_expand"][:D].T, 3)
    wq_rep = tiles(stacked(I["L1_xattn_Wq"].T, 3))
    arrays = {
        "x": xs, "ctxT": I["ctx_512"].reshape(-1, CD).T,
        "wqk0": np.concatenate([I["L0_xattn_Wq"].T, I["L0_xattn_Wk"].T], 1),
        "gamma": np.broadcast_to(I["L0_xattn_gamma_raw"].reshape(1, 1), (P, 1)),
        "ident": np.eye(P, dtype=f), "masks": np.stack([up, up.T], 1).astype(f),
        "mhalf": np.full((P, NT), -0.5, f),
        "neg": neg, "pick": pick, "wk_rep": wk_rep, "wq_rep": wq_rep,
        "wv": I["L1_xattn_Wkv_expand"][D:].T, "wout": tiles(I["L1_xattn_Wout"].T),
        "d1": tiles(I["L1_ffn_d1_w"]), "d2": tiles(I["L1_ffn_d2_w"]), "aggw": tiles(I["L1_ffn_agg_w"]),
        "bcw": tiles(I["L1_ffn_bc_w"]), "gatew": tiles(I["L1_ffn_gate_w"]),
        "rows": np.stack([spread(I[n]) for n in ("L1_ffn_gate_b", "L1_ffn_out_gamma", "L1_ffn_out_beta", "L1_ffn_bc_b")], 1),
        "cols": np.concatenate([column(I["L1_ffn_" + n]) for n in ("in_gamma", "in_beta", "agg_b", "pn_gamma", "pn_beta", "d2_b", "d1_b")]
                               + [np.zeros((P, 32 - 20), f)], 1),
        "rbias": spread(I["L0_ffn_router_bias"]), "gub": gb,
        "tri": spread((e[None, :] < e[:, None]).astype(f)),
        "rw": tiles(I["L0_ffn_router_weight"].T), "bdown": I["L0_ffn_down_proj_bias"],
        "w_exp": np.concatenate([gu, dn], 2),
    }
    arrays = {k: np.ascontiguousarray(v) for k, v in arrays.items()}
    nc = bacc.Bacc("TRN2", target_bir_lowering=False, num_devices=1)
    args = {k: nc.dram_tensor(f"in_{k}", v.shape, mybir.dt.from_np(v.dtype), kind="ExternalInput").ap() for k, v in arrays.items()}
    args["out"] = nc.dram_tensor("out_x", (P, NT, D), F32, kind="ExternalOutput").ap()
    chip_program(nc, args)
    r = run(nc, [{f"in_{k}": v for k, v in arrays.items()}], core_ids=[0])
    out = r.results[0]["out_x"]
    return np.ascontiguousarray(out.reshape(P, 2, NB, D).transpose(2, 1, 0, 3)[:, ::-1].reshape(NB, SEQ, D))
```

```python
import math
from contextlib import ExitStack

import concourse.bass as bass
from concourse import mybir

F32 = mybir.dt.float32
F16 = mybir.dt.float16
BF16 = mybir.dt.bfloat16
ALU = mybir.AluOpType
ACT = mybir.ActivationFunctionType
AXX = mybir.AxisListType.X

P = 128
NB = 4
SEQ = 256
D = 256
KT = D // P
NT = NB * SEQ // P
HT = NT // 2
HC = HT * P
CD = 64
TOPK = max(1, int(SEQ * 0.3))
NE = 16
NTOP = 4
NH = 16
HD = D // NH
VW = HD + 1
WC = KT * 2 * D + KT * D
WP = WC // 2
WS = 64.0
GLIM = 7.0
US = 0.5 / WS
POOL_FROM = 10
ALPHA = 1.702
KS = 16.0
PS = 1024.0
HID = 4 * D
STEPS = 4
NEG = -1e30


def chip_program(nc, a):
    with ExitStack() as ctx:
        def sb(name, shape, dt=F32):
            return ctx.enter_context(nc.sbuf_tensor(name, shape, dt))

        def sem(name):
            return ctx.enter_context(nc.semaphore(name))

        psum = [ctx.enter_context(nc.psum_tensor(f"bank{i}", [P, 512], F32)) for i in range(8)]

        x = sb("x", [P, NT, D])
        xn = sb("xn", [P, HT, D])
        ctx3 = sb("ctx3", [P, 3, NB * SEQ])
        ctxT, qT0, kT0 = (ctx3[0:CD, i] for i in range(3))
        wqk0 = sb("wqk0", [CD, 2 * CD])
        simwork = sb("simwork", [P, 2, NT, SEQ])
        sim, work = simwork[:, 0], simwork[:, 1]
        sig = sb("sig", [P, NT, SEQ])
        top = sb("top", [P, NT, 8])
        bn = sb("bn", [P, NT, 6])
        mv = sb("mv", [P, NT, 2])
        vare = sb("vare", [P, NT])
        rstd = sb("rstd", [P, NT])
        mhalf = sb("mhalf", [P, NT])
        gam = sb("gam", [P, 4])
        lna = sb("lna", [P, NT])
        lnc = sb("lnc", [P, NT])
        ident = sb("ident", [P, P])
        identb = sb("identb", [P, P], BF16)
        maskb = sb("maskb", [P, 2, P], BF16)
        pick = sb("pick", [P, NH], F16)
        rbias = sb("rbias", [P, NE])
        gub = sb("gub", [P, NE, 4])
        gub64 = sb("gub64", [P, NE, 2])
        ub1 = sb("ub1", [P, NE, 2])
        tri = sb("tri", [P, NE * NE])
        rw16 = sb("rw16", [P, 2, KT, NE], F16)
        bdown = sb("bdown", [NE, D])
        stage2 = sb("stage2", [P, 2, WC])
        stage = stage2[:, :, :].rearrange("p a c -> p (a c)").rearrange("p (q c) -> p q c", q=4)
        w16 = sb("w16", [P, NE, 2 * WC], F16)
        xh0 = sb("xh0", [P, 2 * KT, HC], F16)
        lg = sb("lg", [P, HT, NE])
        rank = sb("rank", [P, HT, NE])
        rex = sb("rex", [P, HT, NE])
        rmx = sb("rmx", [P, HT])
        rsm = sb("rsm", [P, HT])
        sc = sb("sc", [P, HT, NE])
        sc64 = sb("sc64", [P, 2, HT, NE])
        gbuf = sb("gbuf", [P, 2, HC])
        tbuf = sb("tbuf", [P, 2, HC])
        ubuf = sb("ubuf", [P, 2, HC])
        hhi = sb("hhi", [P, 2, HC], F16)
        hlo = sb("hlo", [P, 2, HC], F16)
        kst = sb("kst", [P, NH // 2, NB * SEQ], F16)
        vals = sb("vals", [P, 2, 2 * NB, NH * VW], F16)
        pbias = sb("pbias", [P, 1])
        mx = sb("mx", [P, NB, NH])
        rs = sb("rs", [P, 2, NB])
        consts = gbuf[:, 0, :]
        maskf = gbuf[:, 0, 0:2 * P].rearrange("p (a c) -> p a c", a=2)
        pickf = gbuf[:, 1, 0:NH]
        rw = gbuf[:, 1, NH:NH + KT * NE].rearrange("p (k e) -> p k e", k=KT)
        wk = tbuf[0:CD, 0, 0:D]
        wv = ubuf[0:CD, 0, 0:D]
        sigf = sig[:, :, :].rearrange("p t c -> p (t c)")
        xh = (xh0[:, :, :], sigf[:, 0:KT * HC].bitcast(F16).rearrange("p (k q) -> p k q", k=2 * KT))
        cmp = sigf[:, KT * HC:2 * KT * HC].rearrange("p (t e f) -> p t e f", t=HT, e=NE)
        scT = sigf[0:NE, KT * HC:KT * HC + HC]
        qst = simwork[:, :, :, :].rearrange("p a t c -> p (a t c)").bitcast(F16).rearrange("p (h q) -> p h q", h=NH)
        pT = sigf.rearrange("p (k q) -> p k q", k=4)
        xTa = xh0[:, :, :].rearrange("p k q -> p (k q)").bitcast(F32).rearrange("p (k q) -> p k q", k=KT)
        stagef = stage2[:, :, :].rearrange("p a c -> p (a c)")
        wq = stagef[:, 0:KT * D].rearrange("p (k c) -> p k c", k=KT)
        selectf = stagef[:, 2 * D:6 * D]
        select = stagef[:, 6 * D:8 * D].bitcast(F16).rearrange("p (a i c) -> p a i c", a=2, i=NH // 4)
        p16 = stagef[:, 2 * D:6 * D].bitcast(F16).rearrange("p (s a q) -> p s a q", s=2, a=2)
        qhi, qlo = (stagef[:, n * 2 * D:(n + 1) * 2 * D].bitcast(F16).rearrange("p (k c) -> p k c", k=2) for n in (4, 5))
        nmx = stagef[0:NH, 10 * D:12 * D]
        g = [gbuf[:, i] for i in range(2)]
        tt = [tbuf[:, i] for i in range(2)]
        u = [ubuf[:, i] for i in range(2)]
        ao = ctx3[:, 0].rearrange("p (b c) -> p b c", b=NB)
        aoT = ctx3[:, 1].rearrange("p (k q) -> p k q", k=KT)
        nm = ctx3[:, 2, KT * D:KT * D + HC // 2].bitcast(F16)
        wout = ctx3[:, 2, 0:KT * D].rearrange("p (k c) -> p k c", k=KT)
        w32 = w16[:, :, :].rearrange("p e c -> p (e c)").bitcast(F32)
        late = w32[:, NE // 2 * WC:]
        key = late[:, 0:2 * NB * SEQ].rearrange("p (m q) -> p m q", m=2)
        khi, klo = (late[:, n * NB * SEQ:(n + 1) * NB * SEQ].bitcast(F16).rearrange("p (m q) -> p m q", m=2) for n in (2, 3))
        val = late[:, 5 * NB * SEQ + 2 * D:7 * NB * SEQ + 2 * D].rearrange("p (t c) -> p t c", t=2 * NB)
        kselectf = late[:, 4 * NB * SEQ:4 * NB * SEQ + 4 * D]
        kselect = late[:, 5 * NB * SEQ:5 * NB * SEQ + 2 * D].bitcast(F16).rearrange("p (a i c) -> p a i c", a=2, i=NH // 4)
        place = [0]

        def carve(*shape):
            n = 1
            for v in shape:
                n *= v
            out = w32[:, place[0]:place[0] + n]
            place[0] += n
            if len(shape) == 2:
                return out.rearrange("p (a c) -> p a c", a=shape[0])
            return out

        d1, d2, aggw, bcw, gatew = carve(KT, HID), carve(HID // P, D), carve(KT, D), carve(KT, D), carve(KT, D)
        rows, cols = carve(4, D), carve(32)
        d12 = w32[:, 0:2 * KT * HID]
        QD = KT * HID // 2
        d12s = carve(2 * KT * HID).bitcast(F16).rearrange("p (a c) -> p a c", a=2)
        d1s = d12s[:, :, 0:KT * HID].rearrange("p a (k c) -> p a k c", k=KT)
        d2s = d12s[:, :, KT * HID:2 * KT * HID].rearrange("p a (k c) -> p a k c", k=HID // P)
        brow, gsum, yA, yB = carve(NB, D), carve(HT, D), carve(HT, D), carve(HT, D)
        gsumA = carve(HT, D)
        zt = [carve(HT, D), carve(HT, D)]
        yl, cen, sq, nrm, th, act8 = carve(KT, NB), carve(KT, NB), carve(KT, NB), carve(KT, NB), carve(KT, NB), carve(HID // P, NB)
        nrm16, act16 = (carve(k * NB).bitcast(F16).rearrange("p (a k c) -> p a k c", a=2, k=k) for k in (KT, HID // P))
        cvar, crs, chalf, mean4 = carve(NB), carve(NB), carve(NB), carve(P)
        xTb = carve(KT, HC)
        nshift = carve(HT)
        p16b = carve(8 * HC).bitcast(F16).rearrange("p (s a q) -> p s a q", s=8, a=2)
        pTb = [pT[:, c, :] for c in range(4)] + [gbuf[:, 0], gbuf[:, 1], tbuf[:, 0], tbuf[:, 1]]

        in_ctx, in_x, in_gam, in_const = sem("in_ctx"), sem("in_x"), sem("in_gam"), sem("in_const")
        in_w = [sem(f"in_w{q}") for q in range(4)]
        const_ready, gam_ready = sem("const_ready"), sem("gam_ready")
        l0_proj, l0_qk, sim_ready, sim_copied, sig_ready = (sem(n) for n in ("l0_proj", "l0_qk", "sim_ready", "sim_copied", "sig_ready"))
        top_ready, top_removed, masked, mask_t, sym_done, x1_done = (sem(n) for n in ("top_ready", "top_removed", "masked", "mask_t", "sym_done", "x1_done"))
        ln_x0 = sem("ln_x0")
        dve_step, chain_step, pool_step = sem("dve_step"), sem("chain_step"), sem("pool_step")
        vare_ready, rstd_ready, xn_ready = sem("vare_ready"), sem("rstd_ready"), sem("xn_ready")
        w_scaled, w_hi, w_lo = sem("w_scaled"), sem("w_hi"), sem("w_lo")
        t_ready, xhi_ready, xlo_ready = sem("t_ready"), sem("xhi_ready"), sem("xlo_ready")
        logit_ready, rdiff_ready, rexp_ready, sc_ready, scT_mm, scT_ready, bias_mm = (sem(n) for n in (
            "logit_ready", "rdiff_ready", "rexp_ready", "sc_ready", "scT_mm", "scT_ready", "bias_mm"))
        gu_ready, g_done, u_raw, u_done, tanh_done, glu_done, h_done, hhi_done, hlo_done, dn_ready, acc_done = (sem(n) for n in (
            "gu_ready", "g_done", "u_raw", "u_done", "tanh_done", "glu_done", "h_done", "hhi_done", "hlo_done", "dn_ready", "acc_done"))
        kpsum, khi_ready, klo_ready, kselect_ready, kstacked, kst_ready, vpsum, v_ready = (sem(n) for n in (
            "kpsum", "khi_ready", "klo_ready", "kselect_ready", "kstacked", "kst_ready", "vpsum", "v_ready"))
        zero_ready, in_attn, xTa_ready, qpsum, qhi_ready, qlo_ready, qstacked, q_ready = (sem(n) for n in (
            "zero_ready", "in_attn", "xTa_ready", "qpsum", "qhi_ready", "qlo_ready", "qstacked", "q_ready"))
        plo_ready, vlo_ready = sem("plo_ready"), sem("vlo_ready")
        dhi_ready, dlo_ready = sem("dhi_ready"), sem("dlo_ready")
        bias_added, select_ready = sem("bias_added"), sem("select_ready")
        s_ready, mx_done, mxT_ready, nmx_ready, nm_ready, st_ready, exp_done, pv_done, rs_done, o_done = (sem(n) for n in (
            "s_ready", "mx_done", "mxT_ready", "nmx_ready", "nm_ready", "st_ready", "exp_done", "pv_done", "rs_done", "o_done"))
        aoT_psum, aoT_ready, wo_ready, x3_done = sem("aoT_psum"), sem("aoT_ready"), sem("wo_ready"), sem("x3_done")
        in_ffn, c_mm, c_v, c_var, c_rstd, c_gelu = (sem(n) for n in ("in_ffn", "c_mm", "c_v", "c_var", "c_rstd", "c_gelu"))
        gelu_done = sem("gelu_done")
        nshift_ready, endA_ready, cT_ready, xB_turned = (sem(n) for n in ("nshift_ready", "endA_ready", "cT_ready", "xB_turned"))
        centred_ready = sem("centred_ready")
        brow_ready, gate_mm, z_ready, gate_ready = (sem(n) for n in ("brow_ready", "gate_mm", "z_ready", "gate_ready"))
        fin_ready = [sem(f"fin_ready{half}") for half in range(2)]
        out_done = sem("out_done")

        dstep = [0]

        def link(dve, ins):
            dstep[0] += 1
            ins.then_inc(dve_step, 1)
            dve.wait_ge(dve_step, dstep[0])

        block = ctx.enter_context(nc.Block())
        BANKS = (6, 7, 0, 1)
        LANES = (6, 7, 0, 1, 4, 5, 2, 3)
        LEAD = 3
        NCONST = 11
        NCV = 4
        FFN = ((d1, "d1"), (d2, "d2"), (aggw, "aggw"), (bcw, "bcw"), (gatew, "gatew"), (rows, "rows"), (cols, "cols"))
        NFFN = 16 * len(FFN)
        ADDS = HT * NE

        @block.sync
        def _(sp):
            sp.dma_start(ctxT[:, :], a["ctxT"]).then_inc(in_ctx, 16)
            sp.dma_start(wqk0[:, :], a["wqk0"]).then_inc(in_ctx, 16)
            sp.dma_start(x[:, :, :], a["x"]).then_inc(in_x, 16)
            for dst, n in ((gam[:, 0:1], "gamma"), (mhalf[:, :], "mhalf")):
                sp.dma_start(dst, a[n]).then_inc(in_gam, 16)
            for dst, n in ((wk, "wk"), (wv, "wv"), (ident[:, :], "ident"), (maskf, "masks"), (kselectf, "kselect"),
                           (pickf, "pick"), (rbias[:, :], "rbias"), (gub[:, :, :], "gub"), (tri[:, :], "tri"), (rw, "rw"),
                           (bdown[:, :], "bdown")):
                sp.dma_start(dst, a[n]).then_inc(in_const, 16)
            for q in range(4):
                sp.dma_start(stage[:, q, :], a["w_exp"][q // 2, :, (q % 2) * WP:(q % 2 + 1) * WP]).then_inc(in_w[q], 16)
            with sp.Fori(1, NE // 2) as i:
                for q in range(4):
                    sp.wait_ge(w_lo, 4 * i + q - 3)
                    sp.dma_start(stage[:, q, :], a["w_exp"][bass.ds(2 * i + q // 2, 1), :, (q % 2) * WP:(q % 2 + 1) * WP]
                                 .rearrange("e p c -> p (e c)")).then_inc(in_w[q], 16)
            sp.wait_ge(w_lo, 2 * NE)
            sp.dma_start(wq, a["wq"]).then_inc(in_attn, 16)
            sp.dma_start(selectf, a["select"]).then_inc(in_attn, 16)
            sp.wait_ge(sim_ready, NT)
            sp.dma_start(wout, a["wout"]).then_inc(in_attn, 16)
            sp.wait_ge(dn_ready, 2 * (NE + 8))
            for dst, n in FFN:
                sp.dma_start(dst, a[n]).then_inc(in_ffn, 16)
            for half in range(2):
                sp.wait_ge(fin_ready[half], HT)
                sp.dma_start(a["out"][:, half * HT:(half + 1) * HT], x[:, half * HT:(half + 1) * HT, :]).then_inc(out_done, 16)
            sp.wait_ge(out_done, 32)

        @block.tensor
        def _(pe):
            pe.wait_ge(in_ctx, 32)
            def project_0(j, w):
                pe.matmul(psum[2 * w + j][0:CD, :], wqk0[:, w * CD:(w + 1) * CD], ctxT[:, j * 512:(j + 1) * 512],
                          start=True, stop=True).then_inc(l0_proj, 1)

            def sims(b):
                pe.wait_ge(l0_qk, 2 * (b // 2) + 2)
                for half in range(2):
                    t, r = half * HT + b, 1 - half
                    pe.matmul(psum[4 + t // 2][:, (t % 2) * SEQ:(t % 2 + 1) * SEQ],
                              qT0[:, b * SEQ + r * P:b * SEQ + (r + 1) * P], kT0[:, b * SEQ:(b + 1) * SEQ],
                              start=True, stop=True).then_inc(sim_ready, 1)

            project_0(0, 0)
            project_0(0, 1)
            project_0(1, 0)
            sims(0)
            sims(1)
            project_0(1, 1)
            sims(2)
            sims(3)
            pe.wait_ge(in_const, 16 * NCONST)
            for m in range(4):
                if m >= 2:
                    pe.wait_ge(v_ready, m - 1)
                for c in range(2):
                    t = 2 * m + c
                    mm = pe.matmul(psum[2 + m % 2][:, c * D:(c + 1) * D], ctxT[:, t * P:(t + 1) * P], wv, start=True, stop=True)
                mm.then_inc(vpsum, 1)
            for n in range(4):
                m, j = n // 2, n % 2
                if n >= 2:
                    pe.wait_ge(khi_ready, 2 * (n - 1))
                pe.matmul(psum[j][:, :], wk[:, m * P:(m + 1) * P], ctxT[:, j * 512:(j + 1) * 512],
                          start=True, stop=True).then_inc(kpsum, 1)
            pe.wait_ge(kselect_ready, 1)
            pe.wait_ge(khi_ready, 8)
            for i in range(NH // 2):
                for j in range(2):
                    pe.wait_ge(klo_ready, 2 * (i // 4) + j + 1)
                    if i:
                        pe.wait_ge(kst_ready, 2 * i + j - 1)
                    for part, k in ((0, khi), (1, klo)):
                        mm = pe.matmul(psum[j][:, :], kselect[:, part, i % 4, :], k[:, i // 4, j * 512:(j + 1) * 512],
                                       start=(part == 0), stop=(part == 1))
                    mm.then_inc(kstacked, 1)
            pe.wait_ge(v_ready, 4)
            pe.wait_ge(sim_copied, 8)
            for m in (0, 1, 2, 3):
                pe.wait_ge(masked, NT if m % 2 else HT)
                for t in (2 * m, 2 * m + 1):
                    b, r = t % HT, 1 - t // HT
                    for kc in range(2):
                        src = (1 - kc) * HT + b
                        mm = pe.transpose(psum[2 + m][:, (t % 2) * SEQ + kc * P:(t % 2) * SEQ + (kc + 1) * P],
                                          work[:, src, r * P:(r + 1) * P], ident[:, :])
                mm.then_inc(mask_t, 1)
            pe.wait_ge(kst_ready, NH)

            def turn_xn(n, src=xn, bank=6):
                pe.wait_ge(xn_ready, HT * (n + 1))
                for kt in range(KT):
                    for j in range(HT):
                        mm = pe.transpose(psum[bank + kt][:, j * P:(j + 1) * P], src[:, j, kt * P:(kt + 1) * P], ident[:, :])
                    mm.then_inc(t_ready, 1)

            def logits(half):
                for j in range(HT):
                    n = 0
                    for kt in range(KT):
                        for xpart, wpart in ((0, 0), (0, 1), (KT, 0)):
                            mm = pe.matmul(psum[7][:, j * NE:(j + 1) * NE], xh[half][:, xpart + kt, j * P:(j + 1) * P], rw16[:, wpart, kt, :],
                                           start=(n == 0), stop=(n == 5))
                            n += 1
                mm.then_inc(logit_ready, 1)

            def gate_up(half, e, d, first=False):
                gi = half * NE + e
                for which, bank, read in ((0, psum[d], g_done), (1, psum[2 + d], u_raw)):
                    if not first:
                        pe.wait_ge(read, 2 * gi + d - 1)
                    n = 0
                    for kt in range(KT):
                        for wpart, xpart in ((0, 0), (0, KT), (1, 0)):
                            c0 = wpart * WC + kt * 2 * D + which * D + d * P
                            mm = pe.matmul(bank[:, :], w16[:, bass.ds(e, 1), c0:c0 + P].rearrange("p a c -> p (a c)"),
                                           xh[half][:, xpart + kt, :], start=(n == 0), stop=(n == 5))
                            n += 1
                    mm.then_inc(gu_ready, 1)

            def down(half, e, k):
                if k == 0:
                    pe.wait_ge(hlo_done, 2 * (half * NE + e) + 2)
                if not (isinstance(e, int) and half == 0 and e == 0):
                    pe.wait_ge(acc_done, ADDS * half + 4 * e + 2 * k - 2)
                for j in (2 * k, 2 * k + 1):
                    n = 0
                    for d in range(2):
                        for hpart, wpart in ((hhi, 0), (hhi, 1), (hlo, 0)):
                            c0 = wpart * WC + KT * 2 * D + d * D
                            mm = pe.matmul(psum[4 + k][:, (j % 2) * D:(j % 2 + 1) * D], hpart[:, d, j * P:(j + 1) * P],
                                           w16[:, bass.ds(e, 1), c0:c0 + D].rearrange("p a c -> p (a c)"),
                                           start=(n == 0), stop=(n == 5))
                            n += 1
                mm.then_inc(dn_ready, 1)

            def turn_scores(half):
                pe.wait_ge(sc_ready, half + 1)
                for j in range(HT):
                    mm = pe.transpose(psum[6][0:NE, j * P:(j + 1) * P], sc[:, j, :], ident[:, :])
                mm.then_inc(scT_mm, 1)

            def weighed_biases(half):
                pe.wait_ge(scT_ready, half + 1)
                for j in range(HT):
                    mm = pe.matmul(psum[6 + j // 2][:, (j % 2) * D:(j % 2 + 1) * D], scT[:, j * P:(j + 1) * P], bdown[:, :],
                                   start=True, stop=True)
                    if j % 2:
                        mm.then_inc(bias_mm, 1)

            def expert(half, e, before=None, middle=None, between=None, inside=None, after=None):
                for d, extra in ((0, before), (1, middle)):
                    if extra:
                        extra()
                    gate_up(half, e, d)
                if between:
                    between()
                down(half, e - 1, 0)
                if inside:
                    inside()
                down(half, e - 1, 1)
                if after:
                    after()

            def project_q(half, bank, ms=(0, 1)):
                pe.wait_ge(in_attn, 48)
                pe.wait_ge(xTa_ready, KT * (2 * half + 1))
                for m in ms:
                    for kt in range(KT):
                        mm = pe.matmul(psum[bank + m][:, :], wq[:, kt, m * P:(m + 1) * P], xTa[:, kt, :],
                                       start=(kt == 0), stop=(kt == KT - 1))
                    mm.then_inc(qpsum, 1)

            def stack_q(half, i, banks):
                n = 8 * half + i
                if i == 0:
                    pe.wait_ge(select_ready, 1)
                    pe.wait_ge(qlo_ready, 2 * half + 2)
                if i >= len(banks):
                    pe.wait_ge(q_ready, 2 * (n - len(banks) + 1))
                for part, q in ((0, qhi), (1, qlo)):
                    mm = pe.matmul(psum[banks[i % len(banks)]][:, :], select[:, part, i % 4, :], q[:, i // 4, :],
                                   start=(part == 0), stop=(part == 1))
                mm.then_inc(qstacked, 1)

            def scores(i, hh):
                for k in range(2):
                    pe.wait_ge(mx_done, 4 * i + 2 * hh + k + 1)
                    for c in range(2):
                        b = 2 * k + c
                        pe.matmul(psum[6 + k][:, c * SEQ:(c + 1) * SEQ],
                                  qst[:, bass.ds(2 * i + hh, 1), b * P:(b + 1) * P].rearrange("p a c -> p (a c)"),
                                  kst[:, bass.ds(i, 1), b * SEQ:(b + 1) * SEQ].rearrange("p a c -> p (a c)"), start=True, stop=False)
                        mm = pe.matmul(psum[6 + k][:, (c + 1) * SEQ - P:(c + 1) * SEQ], identb[:, :], maskb[:, 0, :],
                                       start=False, stop=True)
                    mm.then_inc(s_ready, 1)

            def scores1(i, hh, c):
                pe.wait_ge(mx_done, 2 * NH + 2 * i + hh - 1)
                bank = psum[BANKS[c]]
                for b in range(NB):
                    pe.matmul(bank[:, b * P:(b + 1) * P],
                              qst[:, bass.ds(2 * i + hh, 1), b * P:(b + 1) * P].rearrange("p a c -> p (a c)"),
                              kst[:, bass.ds(i, 1), b * SEQ:b * SEQ + P].rearrange("p a c -> p (a c)"), start=(b == 0), stop=False)
                mm = pe.matmul(bank[:, :], identb[:, :], maskb[:, 0, :].unsqueeze(1).broadcast_to([P, NB, P]), start=False, stop=True)
                mm.then_inc(s_ready, 1)

            def turn_maxima(half):
                pe.wait_ge(mx_done, NH * (half + 2) + 2)
                for b in range(NB):
                    mm = pe.transpose(psum[6][0:NH, b * P:(b + 1) * P], mx[:, b, :], ident[:, :])
                mm.then_inc(mxT_ready, 1)

            def scores_t(half, i, hh, kt, bank):
                diagonal = kt == 1 or half == 1
                pe.matmul(bank[:, :], pick[:, bass.ds(2 * i + hh, 1)].broadcast_to([P, P]), nm, start=True, stop=False)
                if diagonal:
                    pe.matmul(bank[:, :], identb[:, :], maskb[:, 1, :].unsqueeze(1).broadcast_to([P, NB, P]), start=False, stop=False)
                for b in range(NB):
                    mm = pe.matmul(bank[:, b * P:(b + 1) * P],
                                   kst[:, bass.ds(i, 1), b * SEQ + kt * P:b * SEQ + (kt + 1) * P].rearrange("p a c -> p (a c)"),
                                   qst[:, bass.ds(2 * i + hh, 1), b * P:(b + 1) * P].rearrange("p a c -> p (a c)"),
                                   start=False, stop=(b == NB - 1))
                mm.then_inc(st_ready, 1)

            def weigh(i, hh, kts, parts, bank):
                for b in range(NB):
                    n = 0
                    for kt in kts:
                        for ppart, vpart in ((0, 0), (0, 1), (1, 0)):
                            mm = pe.matmul(bank[:, b * VW:(b + 1) * VW], parts[kt][:, ppart, b * P:(b + 1) * P],
                                           vals[:, vpart, 2 * b + kt, bass.ds((2 * i + hh) * VW, VW)],
                                           start=(n == 0), stop=(n == 3 * len(kts) - 1))
                            n += 1
                mm.then_inc(pv_done, 1)

            def scores_t0(i, hh):
                scores_t(0, i, hh, 1, psum[7])
                pe.wait_ge(o_done, 2 * i + hh + 2)
                scores_t(0, i, hh, 0, psum[6])

            def weigh0(i, hh):
                pe.wait_ge(plo_ready, 4 * i + 2 * hh + 2)
                weigh(i, hh, (0, 1), (p16[:, 0], p16[:, 1]), psum[6])

            def weigh_and_next(i, hh, last=False):
                weigh0(i, hh)
                if not last:
                    scores_t0(i + hh, 1 - hh)

            def project_out(half):
                pe.wait_ge(o_done, NH * (half + 1) + 2)
                for kt in range(KT):
                    for b in range(NB):
                        mm = pe.transpose(psum[6 + kt][:, b * P:(b + 1) * P], ao[:, b, kt * P:(kt + 1) * P], ident[:, :])
                    mm.then_inc(aoT_psum, 1)
                pe.wait_ge(aoT_ready, 2 * (half + 1))
                for j in range(HT):
                    for kt in range(KT):
                        mm = pe.matmul(psum[6 + j // 2][:, (j % 2) * D:(j % 2 + 1) * D], aoT[:, kt, j * P:(j + 1) * P], wout[:, kt, :],
                                       start=(kt == 0), stop=(kt == KT - 1))
                    if j % 2:
                        mm.then_inc(wo_ready, 1)

            turn_xn(0)
            pe.wait_ge(xhi_ready, KT)
            pe.wait_ge(xlo_ready, KT)
            pe.wait_ge(w_lo, 4)
            gate_up(0, 0, 0, first=True)
            gate_up(0, 0, 1, first=True)
            logits(0)
            gate_up(0, 1, 0)
            gate_up(0, 1, 1)
            down(0, 0, 0)
            down(0, 0, 1)
            pe.wait_ge(w_lo, 4 + 2)
            expert(0, 2, between=lambda: turn_scores(0))
            pe.wait_ge(w_lo, 4 + 4)
            expert(0, 3, middle=lambda: weighed_biases(0))
            with pe.Fori(2, 4) as m:
                for s in range(2):
                    pe.wait_ge(w_lo, 4 * m + 2 * s + 2)
                    expert(0, 2 * m + s)

            def logits_1():
                pe.wait_ge(xhi_ready, 2 * KT)
                pe.wait_ge(xlo_ready, 2 * KT)
                logits(1)

            pe.wait_ge(w_lo, 2 * 9)
            expert(0, 8)
            pe.wait_ge(w_lo, 2 * 10)
            expert(0, 9, after=lambda: turn_xn(1))
            pe.wait_ge(w_lo, 2 * 11)
            expert(0, 10)
            pe.wait_ge(w_lo, 2 * 12)
            expert(0, 11, middle=logits_1)
            pe.wait_ge(w_lo, 2 * NE)
            expert(0, 12)
            expert(0, 13)
            expert(0, 14)
            expert(0, NE - 1, between=lambda: turn_scores(1))

            gate_up(1, 0, 0)
            gate_up(1, 0, 1)
            weighed_biases(1)
            down(0, NE - 1, 0)
            down(0, NE - 1, 1)
            pe.wait_ge(bias_added, 2 * HT)
            expert(1, 1, after=lambda: turn_xn(2))
            expert(1, 2, middle=lambda: project_q(0, 6), inside=lambda: stack_q(0, 0, (6, 7)), after=lambda: stack_q(0, 1, (6, 7)))
            expert(1, 3, *(lambda i=i: stack_q(0, i, (6, 7)) for i in range(2, 7)))
            stack_q(0, 7, (6, 7))
            pe.wait_ge(q_ready, NH)
            with pe.Fori(2, 4) as m:
                for s in range(2):
                    i = 4 * m + 2 * s - 8
                    expert(1, 2 * m + s, lambda: scores(i, 0), lambda: scores(i, 1),
                           lambda: scores(i + 1, 0), lambda: scores(i + 1, 1))
            turn_maxima(0)
            pe.wait_ge(nm_ready, 2)
            pe.wait_ge(vlo_ready, 4)
            scores_t0(0, 0)
            with pe.Fori(8, NE - 1) as e:
                i = e - 8
                expert(1, e, middle=lambda: weigh_and_next(i, 0), inside=lambda: weigh_and_next(i, 1))
            i = NH // 2 - 1
            expert(1, NE - 1, middle=lambda: weigh_and_next(i, 0), inside=lambda: weigh_and_next(i, 1, last=True))
            project_out(0)
            down(1, NE - 1, 0)
            down(1, NE - 1, 1)

            cbank = psum[5]

            def column_sum(src, c):
                pe.wait_ge(c_v, c)
                for kt in range(KT):
                    mm = pe.matmul(cbank[:, 0:NB], mean4, src[:, kt, :], start=(kt == 0), stop=(kt == KT - 1))
                mm.then_inc(c_mm, 1)

            def column_mm(w, src, kts, ms, c):
                pe.wait_ge(c_v, c)
                for m in range(ms):
                    for kt in range(kts):
                        mm = pe.matmul(cbank[:, m * NB:(m + 1) * NB], w[:, kt, m * P:(m + 1) * P], src[:, kt, :],
                                       start=(kt == 0), stop=(kt == kts - 1))
                mm.then_inc(c_mm, 1)

            def split_mm(w, src, kts, ms, c):
                pe.wait_ge(c_v, c)
                for m in range(ms):
                    n = 0
                    for kt in range(kts):
                        for wpart, part in ((0, 0), (0, 1), (1, 0)):
                            mm = pe.matmul(cbank[:, m * NB:(m + 1) * NB], w[:, wpart, kt, m * P:(m + 1) * P], src[:, part, kt, :],
                                           start=(n == 0), stop=(n == 3 * kts - 1))
                            n += 1
                mm.then_inc(c_mm, 1)

            def gates(half, bank, tiles=range(HT)):
                pe.wait_ge(xTa_ready, KT * 2)
                for j in tiles:
                    for kt in range(KT):
                        mm = pe.matmul(psum[bank + j // 2][:, (j % 2) * D:(j % 2 + 1) * D], xTb[:, kt, j * P:(j + 1) * P], gatew[:, kt, :],
                                       start=(kt == 0), stop=(kt == KT - 1))
                    if j % 2:
                        mm.then_inc(gate_mm, 1)

            turn_xn(3, yA)
            pe.wait_ge(in_ffn, NFFN)
            column_sum(yl, 1)
            column_sum(sq, 2)
            turn_xn(4, bank=0)
            column_mm(aggw, nrm, KT, KT, 3)

            def thought(k, scaling=None, gelu=None, after=None):
                column_sum(th, 4 * k + 4)
                column_sum(sq, 4 * k + 5)
                if scaling:
                    scaling()
                split_mm(d1s, nrm16, KT, HID // P, 4 * k + 6)
                if gelu:
                    gelu()
                split_mm(d2s, act16, HID // P, KT, 4 * k + 7)
                if after:
                    after()

            def stack_more(first, last):
                for i in range(first, last):
                    stack_q(1, i, BANKS)

            def more_scores(first, last):
                for c in range(first, last):
                    scores1(4 * k + c // 2 - 8, c % 2, c % 4)

            pe.wait_ge(dlo_ready, 4)
            thought(0, lambda: project_q(1, 6, (0,)), lambda: project_q(1, 6, (1,)), lambda: gates(0, 2, (0, 1)))
            thought(1, lambda: stack_more(0, 4), lambda: stack_more(4, 5), lambda: (stack_more(5, NH // 2), gates(0, 2, (2, 3))))
            pe.wait_ge(q_ready, 2 * NH)
            with pe.Fori(2, STEPS) as k:
                thought(k, lambda: more_scores(0, 4), lambda: more_scores(4, 6), lambda: more_scores(6, 8))
            turn_maxima(1)
            pe.wait_ge(z_ready, 2)
            pe.wait_ge(c_v, 4 * STEPS + 4)
            for b in range(NB):
                for kt in range(KT):
                    mm = pe.matmul(psum[2 + b // 2][:, (b % 2) * D:(b % 2 + 1) * D], th[:, kt, b:b + 1].broadcast_to([P, P]), bcw[:, kt, :],
                                   start=(kt == 0), stop=(kt == KT - 1))
            mm.then_inc(c_mm, 1)
            pe.wait_ge(nm_ready, 4)
            for n in range(NH + LEAD):
                if n < NH:
                    if n >= len(LANES):
                        pe.wait_ge(o_done, NH + n - len(LANES) + 3)
                    if n == 6:
                        pe.wait_ge(brow_ready, 2)
                    scores_t(1, n // 2, n % 2, 0, psum[LANES[n % 8]])
                if n >= LEAD:
                    h = n - LEAD
                    pe.wait_ge(plo_ready, 2 * NH + h + 1)
                    weigh(h // 2, h % 2, (0,), (p16b[:, h % 8],), psum[LANES[h % 8]])
            project_out(1)
            for c in range(2):
                pe.wait_ge(xn_ready, HT * 5 + 2 * c + 2)
                for kt in range(KT):
                    for j in range(2):
                        mm = pe.transpose(psum[6 + c][:, (2 * kt + j) * P:(2 * kt + j + 1) * P], yB[:, 2 * c + j, kt * P:(kt + 1) * P], ident[:, :])
                mm.then_inc(cT_ready, 1)
            for c in range(2):
                pe.wait_ge(xB_turned, c + 1)
                gates(1, 0, (2 * c, 2 * c + 1))

        @block.scalar
        def _(act):
            for n in range(4):
                act.wait_ge(l0_proj, n + 1)
                j, w = n // 2, n % 2
                dst = (qT0, kT0)[w]
                act.activation(dst[:, j * 512:(j + 1) * 512], psum[2 * w + j][0:CD, :], ACT.Copy).then_inc(l0_qk, 1)
            act.wait_ge(in_gam, 32)
            act.activation(gam[:, 1:2], gam[:, 0:1], ACT.Tanh, scale=0.5).then_inc(gam_ready, 1)
            for dst in (work, sim):
                for bank, need in ((0, 3), (2, 4), (1, 7), (3, 8)):
                    act.wait_ge(sim_ready, need)
                    act.activation(dst[:, 2 * bank:2 * bank + 2, :], psum[4 + bank][:, :].rearrange("p (a c) -> p a c", a=2),
                                   ACT.Copy).then_inc(sim_copied, 1)
            act.wait_ge(ln_x0, 2)
            for t in range(NT):
                act.activation(x[:, t, :], x[:, t, :], ACT.Identity, bias=lnc[:, t:t + 1], scale=lna[:, t:t + 1]).then_inc(ln_x0, 1)
            act.wait_ge(sim_copied, 8)
            for m in range(4):
                act.activation(sig[:, 2 * m:2 * m + 2, :], sim[:, 2 * m:2 * m + 2, :], ACT.Tanh, scale=1 / 32).then_inc(sig_ready, 1)
            for m in range(4):
                act.wait_ge(sig_ready, m + 1)
                act.activation(sig[:, 2 * m:2 * m + 2, :], sig[:, 2 * m:2 * m + 2, :], ACT.Copy, bias=1.0).then_inc(sig_ready, 1)
            act.wait_ge(zero_ready, 1)
            for m in range(4):
                act.wait_ge(vpsum, m + 1)
                act.activation(val[:, 2 * m:2 * m + 2, :], psum[2 + m % 2][:, :].rearrange("p (t c) -> p t c", t=2), ACT.Copy, scale=WS)
                act.activation(vals[:, 0, 2 * m:2 * m + 2, :].rearrange("p t (h v) -> p t h v", v=VW)[:, :, :, 0:HD],
                               psum[2 + m % 2][:, :].rearrange("p (t h v) -> p t h v", t=2, h=NH), ACT.Copy, scale=WS).then_inc(v_ready, 1)
            for n in range(4):
                m, j = n // 2, n % 2
                act.wait_ge(kpsum, n + 1)
                act.activation(key[:, m, j * 512:(j + 1) * 512], psum[j][:, :], ACT.Copy, scale=KS).then_inc(khi_ready, 1)
                act.activation(khi[:, m, j * 512:(j + 1) * 512], psum[j][:, :], ACT.Copy, scale=KS).then_inc(khi_ready, 1)

            def split_part(i, q):
                act.wait_ge(in_w[q], 16 * i + 16)
                act.activation(w16[:, bass.ds(2 * i + q // 2, 1), (q % 2) * WP:(q % 2 + 1) * WP].rearrange("p a c -> p (a c)"),
                               stage[:, q, :], ACT.Copy, scale=WS).then_inc(w_hi, 1)
                act.activation(stage[:, q, :], stage[:, q, :], ACT.Copy, scale=WS).then_inc(w_scaled, 1)

            with act.Fori(0, NCV) as i:
                for q in range(4):
                    split_part(i, q)
                    act.wait_ge(kstacked, 4 * i + q + 1)
                    act.activation(kst[:, bass.ds(2 * i + q // 2, 1), (q % 2) * 512:(q % 2 + 1) * 512].rearrange("p a c -> p (a c)"),
                                   psum[q % 2][:, :], ACT.Copy).then_inc(kst_ready, 1)

            def high_parts(half):
                for kt in range(KT):
                    act.wait_ge(t_ready, KT * half + kt + 1)
                    act.activation(xh[half][:, kt, :], psum[6 + kt][:, :], ACT.Copy).then_inc(xhi_ready, 1)

            def ups(half, e, d, first=False):
                gi = half * NE + e
                act.wait_ge(gu_ready, 4 * gi + 2 * d + 2)
                if not first:
                    act.wait_ge(hlo_done, 2 * gi + d - 1)
                act.activation(u[d], psum[2 + d][:, :], ACT.Identity, scale=US / WS,
                               bias=ub1[:, bass.ds(e, 1), d:d + 1].rearrange("p a c -> p (a c)")).then_inc(u_raw, 1)
                act.wait_ge(g_done, 2 * gi + d + 1)
                act.activation(tt[d], g[d], ACT.Tanh, scale=ALPHA / 2 / WS).then_inc(tanh_done, 1)

            def highs(half, e, d, first=False):
                gi = half * NE + e
                if not first:
                    act.wait_ge(dn_ready, 2 * gi)
                act.wait_ge(h_done, 2 * gi + d + 1)
                act.activation(hhi[:, d, :], u[d], ACT.Copy).then_inc(hhi_done, 1)

            def expert(half, e, first=False, before=None, middle=None, between=None, inside=None):
                for d, extra in ((0, before), (1, middle)):
                    if extra:
                        extra()
                    ups(half, e, d, first)
                for d, extra in ((0, between), (1, inside)):
                    if extra:
                        extra()
                    highs(half, e, d, first)

            def exp_logits(half):
                act.wait_ge(rdiff_ready, half + 1)
                act.activation(rex[:, :, :], rex[:, :, :], ACT.Exp).then_inc(rexp_ready, 1)

            def turn_scores_out(half):
                act.wait_ge(scT_mm, half + 1)
                act.activation(scT, psum[6][0:NE, :], ACT.Copy).then_inc(scT_ready, 1)

            def copy_turned(n, dst=xTa, bank=6):
                for kt in range(KT):
                    act.wait_ge(t_ready, KT * n + kt + 1)
                    act.activation(dst[:, kt, :], psum[bank + kt][:, :], ACT.Copy).then_inc(xTa_ready, 1)

            def high_queries(half, bank, ms=(0, 1)):
                for m in ms:
                    act.wait_ge(qpsum, 2 * half + m + 1)
                    act.activation(qhi[:, m, :], psum[bank + m][:, :], ACT.Copy).then_inc(qhi_ready, 1)

            def queries(half, i, banks):
                act.wait_ge(qstacked, 8 * half + i + 1)
                for hh in range(2):
                    r = slice(hh * 64, hh * 64 + 64)
                    act.activation(qst[r, 2 * i + hh, :], psum[banks[i % len(banks)]][r, :], ACT.Copy).then_inc(q_ready, 1)

            def maxima_out(half):
                act.wait_ge(mxT_ready, half + 1)
                act.activation(nm[0:NH, :], psum[6][0:NH, :], ACT.Copy, scale=-1.0).then_inc(nm_ready, 1)
                act.activation(nmx, psum[6][0:NH, :], ACT.Copy, scale=-1.0).then_inc(nmx_ready, 1)

            def exps0(i, hh):
                for k, kt in enumerate((1, 0)):
                    act.wait_ge(st_ready, 4 * i + 2 * hh + k + 1)
                    for dst in (p16[:, kt, 0], pT[:, 2 + kt, :]):
                        act.activation(dst, psum[6 + kt][:, :], ACT.Exp, scale=HD ** -0.5 / KS, bias=pbias[:, :]).then_inc(exp_done, 1)

            def turned_out(half):
                for kt in range(KT):
                    act.wait_ge(aoT_psum, 2 * half + kt + 1)
                    act.activation(aoT[:, kt, :], psum[6 + kt][:, :], ACT.Copy).then_inc(aoT_ready, 1)

            high_parts(0)
            expert(0, 0, first=True)
            expert(0, 1, between=lambda: exp_logits(0))

            def expert_and_split(e, i, s, between=None):
                def second():
                    if between:
                        between()
                    split_part(i, 2 * s + 1)

                expert(0, e, middle=lambda: split_part(i, 2 * s), between=second)

            expert_and_split(2, NCV, 0, between=lambda: turn_scores_out(0))
            expert_and_split(3, NCV, 1)
            with act.Fori(2, 4) as m:
                for s in range(2):
                    expert_and_split(2 * m + s, m + NCV - 1, s)
            expert_and_split(8, NE // 2 - 1, 0)
            expert_and_split(9, NE // 2 - 1, 1)
            expert(0, 10, before=lambda: high_parts(1))
            expert(0, 11)
            expert(0, 12, between=lambda: exp_logits(1))
            expert(0, 13)
            expert(0, 14)
            expert(0, NE - 1, between=lambda: turn_scores_out(1))

            expert(1, 0)
            expert(1, 1)
            copy_turned(2)
            act.wait_ge(in_attn, 48)
            act.activation(select.rearrange("p a i c -> p (a i c)"), selectf, ACT.Copy).then_inc(select_ready, 1)
            act.wait_ge(zero_ready, 3)
            expert(1, 2, middle=lambda: high_queries(0, 6))
            for i in (0, 1):
                queries(0, i, (6, 7))
            expert(1, 3, False, *(lambda i=i: queries(0, i, (6, 7)) for i in range(2, 6)))
            for i in (6, 7):
                queries(0, i, (6, 7))
            with act.Fori(2, 4) as m:
                for s in range(2):
                    expert(1, 2 * m + s)
            maxima_out(0)
            act.wait_ge(zero_ready, 4)
            exps0(0, 0)
            with act.Fori(8, 11) as e:
                i = e - 8
                expert(1, e, middle=lambda: exps0(i, 1), between=lambda: exps0(i + 1, 0))
            act.wait_ge(in_ffn, NFFN)

            def split_quarter(e):
                quarter = bass.ds((e - 11) * QD, QD)
                act.activation(d12s[:, 0, quarter], d12[:, quarter], ACT.Copy, scale=WS).then_inc(dhi_ready, 1)
                act.activation(d12[:, quarter], d12[:, quarter], ACT.Copy, scale=WS).then_inc(dhi_ready, 1)

            with act.Fori(11, NE - 1) as e:
                i = e - 8
                expert(1, e, middle=lambda: exps0(i, 1), between=lambda: exps0(i + 1, 0))
                split_quarter(e)
            expert(1, NE - 1, middle=lambda: exps0(NH // 2 - 1, 1))
            turned_out(0)
            def gate_tanh(half):
                for m in range(2):
                    act.wait_ge(z_ready, 2 * half + m + 1)
                    two = slice(2 * m, 2 * m + 2)
                    act.activation(zt[half][:, two, :], zt[half][:, two, :], ACT.Tanh, scale=0.5).then_inc(gate_ready, 1)

            copy_turned(3, xTb)
            copy_turned(4, bank=0)
            high_queries(1, 6, (0,))

            def gelu(k):
                act.wait_ge(c_gelu, k + 1)
                act.activation(act16[:, 0], act8[:, :, :], ACT.Gelu).then_inc(gelu_done, 1)
                act.activation(act8[:, :, :], act8[:, :, :], ACT.Gelu).then_inc(gelu_done, 1)

            gelu(0)
            high_queries(1, 6, (1,))
            for i in range(4):
                queries(1, i, BANKS)
            gelu(1)
            for i in range(4, NH // 2):
                queries(1, i, BANKS)
            with act.Fori(2, STEPS) as k:
                gelu(k)
            maxima_out(1)
            gate_tanh(0)
            for n in range(NH):
                act.wait_ge(st_ready, 2 * NH + n + 1)
                for dst in (p16b[:, n % 8, 0], pTb[n % 8]):
                    act.activation(dst, psum[LANES[n % 8]][:, :], ACT.Exp, scale=HD ** -0.5 / KS, bias=pbias[:, :]).then_inc(exp_done, 1)
            turned_out(1)
            act.wait_ge(nshift_ready, 2)
            for j in range(HT):
                act.activation(gsumA[:, j, :], gsumA[:, j, :], ACT.Identity, bias=nshift[:, j:j + 1],
                               scale=rstd[:, HT + j:HT + j + 1]).then_inc(endA_ready, 1)
            for c in range(2):
                act.wait_ge(cT_ready, c + 1)
                act.activation(xTb[:, :, 2 * c * P:(2 * c + 2) * P], psum[6 + c][:, :].rearrange("p (k q) -> p k q", k=KT),
                               ACT.Copy).then_inc(xB_turned, 1)
            gate_tanh(1)

        @block.gpsimd
        def _(pool):
            def power(n, sl):
                pool.wait_ge(vare_ready, n)
                pool.tensor_tensor(rstd[:, sl], vare[:, sl], mhalf[:, sl], ALU.pow).then_inc(rstd_ready, 1)

            vcols = vals[:, :, :, :].rearrange("p a t (h v) -> p a t h v", v=VW)
            pool.memset(vcols[:, 0, :, :, HD:VW], WS)
            pool.memset(vcols[:, 1, :, :, HD:VW], 0.0).then_inc(zero_ready, 1)
            pool.wait_ge(in_gam, 32)
            power(1, slice(0, NT))
            for m in range(4):
                two = slice(2 * m, 2 * m + 2)
                pool.wait_ge(v_ready, m + 1)
                pool.tensor_tensor(vcols[:, 1, two, :, 0:HD], val[:, two].rearrange("p t (h v) -> p t h v", h=NH),
                                   vcols[:, 0, two, :, 0:HD], ALU.subtract).then_inc(vlo_ready, 1)
            pool.wait_ge(in_const, 16 * NCONST)
            pool.tensor_copy(kselect.rearrange("p a i c -> p (a i c)"), kselectf).then_inc(kselect_ready, 1)
            for n in range(4):
                m, j = n // 2, slice(n % 2 * 512, (n % 2 + 1) * 512)
                pool.wait_ge(khi_ready, 2 * n + 2)
                pool.tensor_tensor(klo[:, m, j], key[:, m, j], khi[:, m, j], ALU.subtract).then_inc(klo_ready, 1)

            def split_part(i, q):
                pool.wait_ge(w_scaled, 4 * i + q + 1)
                e, c0 = bass.ds(2 * i + q // 2, 1), (q % 2) * WP
                pool.tensor_tensor(w16[:, e, WC + c0:WC + c0 + WP].rearrange("p a c -> p (a c)"), stage[:, q, :],
                                   w16[:, e, c0:c0 + WP].rearrange("p a c -> p (a c)"), ALU.subtract).then_inc(w_lo, 1)

            def lows(gi):
                for d in range(2):
                    pool.wait_ge(hhi_done, 2 * gi + d + 1)
                    pool.tensor_tensor(hlo[:, d, :], u[d], hhi[:, d, :], ALU.subtract).then_inc(hlo_done, 1)

            with pool.Fori(0, NCV) as i:
                for q in range(4):
                    split_part(i, q)
            power(2, slice(0, HT))
            pool.wait_ge(x1_done, 4)
            pool.memset(ctx3[:, 2, KT * D:KT * D + HC // 2], 0.0).then_inc(zero_ready, 1)
            pool.memset(simwork[:, :, :, :].rearrange("p a t c -> p (a t c)"), 0.0).then_inc(zero_ready, 1)
            pool.memset(pbias[:, :], math.log(PS)).then_inc(zero_ready, 1)
            lows(0)
            lows(1)
            with pool.Fori(1, 4) as m:
                for s in range(2):
                    split_part(m + NCV - 1, 2 * s)
                    lows(2 * m + s)
                    split_part(m + NCV - 1, 2 * s + 1)
            for e in (8, 9):
                split_part(NE // 2 - 1, 2 * (e % 2))
                lows(e)
                if e == 8:
                    power(3, slice(0, HT))
                split_part(NE // 2 - 1, 2 * (e % 2) + 1)
            def product(gi, d):
                pool.wait_ge(glu_done, 2 * gi + d + 1)
                pool.wait_ge(u_done, 2 * gi + d + 1)
                pool.tensor_tensor(u[d], tt[d], u[d], ALU.mult).then_inc(h_done, 1)

            def products_lows(gi):
                for d in range(2):
                    product(gi, d)
                lows(gi)

            with pool.Fori(POOL_FROM, NE) as e:
                products_lows(e)
            product(NE, 0)
            product(NE, 1)
            power(4, slice(0, HT))
            lows(NE)
            with pool.Fori(1, 8) as e:
                products_lows(e + NE)

            def low_probabilities(i, hh):
                for k, kt in enumerate((1, 0)):
                    pool.wait_ge(exp_done, 8 * i + 4 * hh + 2 * k + 2)
                    pool.tensor_tensor(p16[:, kt, 1], pT[:, 2 + kt, :], p16[:, kt, 0], ALU.subtract).then_inc(plo_ready, 1)

            def low_quarter(e):
                quarter = bass.ds((e - 11) * QD, QD)
                pool.wait_ge(dhi_ready, 2 * e - 20)
                pool.tensor_tensor(d12s[:, 1, quarter], d12[:, quarter], d12s[:, 0, quarter], ALU.subtract).then_inc(dlo_ready, 1)

            low_probabilities(0, 0)
            for first, last in ((8, 11), (11, NE - 1)):
                with pool.Fori(first, last) as e:
                    product(e + NE, 0)
                    low_probabilities(e - 8, 1)
                    product(e + NE, 1)
                    low_probabilities(e - 7, 0)
                    lows(e + NE)
                    if first == 11:
                        low_quarter(e)
            product(2 * NE - 1, 0)
            low_probabilities(NH // 2 - 1, 1)
            product(2 * NE - 1, 1)
            lows(2 * NE - 1)
            power(5, slice(0, HT))
            power(6, slice(0, HT))
            def chain_power(n):
                pool.wait_ge(c_var, n)
                pool.tensor_tensor(crs, cvar, chalf, ALU.pow).then_inc(c_rstd, 1)

            chain_power(1)
            pool.wait_ge(xn_ready, HT * 4)
            for j in range(HT):
                pool.tensor_tensor(x[:, j, :], x[:, j, :], rows[:, 2, :], ALU.add).then_inc(pool_step, 1)
            with pool.Fori(0, STEPS) as k:
                chain_power(k + 2)
            for n in range(NH):
                pool.wait_ge(exp_done, 4 * NH + 2 * n + 2)
                pool.tensor_tensor(p16b[:, n % 8, 1], pTb[n % 8], p16b[:, n % 8, 0], ALU.subtract).then_inc(plo_ready, 1)
            power(7, slice(HT, NT))
            pool.wait_ge(rstd_ready, 7)
            pool.tensor_tensor(nshift[:, :], mv[:, HT:NT, 0], rstd[:, HT:NT], ALU.mult).then_inc(nshift_ready, 1)
            pool.wait_ge(nshift_ready, 1)
            pool.tensor_scalar(nshift[:, :], nshift[:, :], -1.0, None, ALU.mult).then_inc(nshift_ready, 1)

            def end_of_tile(j):
                pool.wait_ge(endA_ready, j + 1)
                pool.tensor_tensor(gsumA[:, j, :], gsumA[:, j, :], rows[:, 1, :], ALU.mult).then_inc(pool_step, 1)
                pool.wait_ge(pool_step, HT + j + 1)
                pool.tensor_tensor(x[:, j, :], x[:, j, :], gsumA[:, j, :], ALU.add).then_inc(fin_ready[0], 1)

            end_of_tile(0)
            end_of_tile(1)
            power(8, slice(0, HT))
            end_of_tile(2)
            end_of_tile(3)
            power(9, slice(0, HT))

        @block.vector
        def _(dve):
            def stats(src, k, n, eps, o=0):
                for j in range(k):
                    ins = dve.bn_stats(bn[:, o + j, :], src[:, j, :])
                link(dve, ins)
                for j in range(k):
                    ins = dve.bn_aggr(mv[:, o + j, :], bn[:, o + j, :])
                link(dve, ins)
                dve.tensor_scalar(vare[:, o:o + k], mv[:, o:o + k, 1], eps, None, ALU.add).then_inc(vare_ready, 1)
                if n is not None:
                    dve.wait_ge(rstd_ready, n)

            dve.wait_ge(in_x, 16)
            dve.sem_inc(mx_done, 2)
            dve.sem_inc(o_done, 2)
            stats(x, NT, 1, 1e-5)
            dve.wait_ge(gam_ready, 1)
            link(dve, dve.tensor_scalar(gam[:, 2:3], gam[:, 1:2], -0.5, 0.5, ALU.mult, ALU.add))
            dve.tensor_scalar(gam[:, 3:4], gam[:, 1:2], 0.125, 0.125, ALU.mult, ALU.add)
            dve.tensor_scalar(lna[:, :], rstd[:, :], gam[:, 2:3], 1.0, ALU.mult, ALU.add).then_inc(ln_x0, 1)
            link(dve, dve.scalar_tensor_tensor(lnc[:, :], mv[:, :, 0], gam[:, 2:3], rstd[:, :], ALU.mult, ALU.mult))
            dve.tensor_scalar(lnc[:, :], lnc[:, :], -1.0, None, ALU.mult).then_inc(ln_x0, 1)
            order = (0, 1, 4, 5, 2, 3, 6, 7)
            for n, t in enumerate(order):
                dve.wait_ge(sim_copied, n // 2 + 1)
                dve.max(top[:, t, :], work[:, t, :]).then_inc(top_ready, 1)
            dve.wait_ge(in_const, 16 * NCONST)
            dve.tensor_copy(identb[:, :], ident[:, :])
            dve.tensor_copy(maskb[:, :, :], maskf)
            dve.tensor_copy(pick[:, :], pickf)
            link(dve, dve.tensor_scalar(rw16[:, 0], rw, WS, None, ALU.mult))
            dve.scalar_tensor_tensor(rw16[:, 1], rw, WS, rw16[:, 0], ALU.mult, ALU.subtract)
            dve.tensor_scalar(gub64[:, :, :], gub[:, :, 0:2], WS, None, ALU.mult)
            dve.tensor_scalar(ub1[:, :, :], gub[:, :, 2:4], 1.0, US, ALU.add, ALU.mult).then_inc(const_ready, 1)
            for i in range(TOPK // 8):
                for n, t in enumerate(order):
                    dve.wait_ge(top_ready, NT * i + n + 1)
                    dve.match_replace(work[:, t, :], top[:, t, :], work[:, t, :], -3e38).then_inc(top_removed, 1)
                for n, t in enumerate(order):
                    dve.wait_ge(top_removed, NT * i + n + 1)
                    dve.max(top[:, t, :], work[:, t, :]).then_inc(top_ready, 1)
            kth = TOPK % 8 - 1
            dve.wait_ge(top_ready, NT * (TOPK // 8 + 1))
            dve.wait_ge(sig_ready, 8)
            for t in (0, 4, 1, 5, 2, 6, 3, 7):
                dve.scalar_tensor_tensor(work[:, t, :], sim[:, t, :], top[:, t, kth:kth + 1], sig[:, t, :],
                                         ALU.is_ge, ALU.mult).then_inc(masked, 1)
            dve.wait_ge(masked, NT)
            dve.wait_ge(ln_x0, 2 + NT)

            def symmetrised(half):
                for m in (2 * half, 2 * half + 1):
                    dve.wait_ge(mask_t, m + 1)
                    dve.tensor_tensor(sim[:, 2 * m:2 * m + 2, :], work[:, 2 * m:2 * m + 2, :],
                                      psum[2 + m][:, :].rearrange("p (a c) -> p a c", a=2), ALU.add).then_inc(sym_done, 1)
                for m in (2 * half, 2 * half + 1):
                    dve.wait_ge(sym_done, m + 1)
                    dve.scalar_tensor_tensor(x[:, 2 * m:2 * m + 2, :], sim[:, 2 * m:2 * m + 2, :], gam[:, 3:4],
                                             x[:, 2 * m:2 * m + 2, :], ALU.mult, ALU.add).then_inc(x1_done, 1)

            def statistics(half, n):
                rounds.append(n)
                stats(x[:, half * HT:(half + 1) * HT], HT, None, 1e-5)

            def normalised(half, n, dst=None):
                dve.wait_ge(rstd_ready, len(rounds) + 1)
                dst = xn if dst is None else dst
                if n:
                    dve.wait_ge(t_ready, KT * n)
                for j in range(HT):
                    dve.tensor_scalar(dst[:, j, :], x[:, half * HT + j, :], mv[:, j, 0:1], rstd[:, j:j + 1],
                                      ALU.subtract, ALU.mult).then_inc(xn_ready, 1)

            def normalise(half, n, dst=None, between=None):
                statistics(half, n)
                if between:
                    between()
                normalised(half, n, dst)

            def low_part(half, kt):
                dve.wait_ge(xhi_ready, KT * half + kt + 1)
                dve.tensor_tensor(xh[half][:, KT + kt, :], psum[6 + kt][:, :], xh[half][:, kt, :], ALU.subtract).then_inc(xlo_ready, 1)

            mine = lg[:, :, :].unsqueeze(3).broadcast_to([P, HT, NE, NE])
            other = lg[:, :, :].unsqueeze(2).broadcast_to([P, HT, NE, NE])
            cmpf = cmp.rearrange("p t e f -> p t (e f)")

            def take_logits(half):
                dve.wait_ge(logit_ready, half + 1)
                link(dve, dve.scalar_tensor_tensor(lg[:, :, :], psum[7][:, 0:HT * NE].rearrange("p (t e) -> p t e", t=HT), 1 / WS,
                                                   rbias[:, :].unsqueeze(1).broadcast_to([P, HT, NE]), ALU.mult, ALU.add))
                link(dve, dve.tensor_reduce(rmx[:, :], lg[:, :, :], AXX, ALU.max))
                dve.tensor_tensor(rex[:, :, :], lg[:, :, :], rmx[:, :].unsqueeze(2).broadcast_to([P, HT, NE]),
                                  ALU.subtract).then_inc(rdiff_ready, 1)

            def equal_logits():
                link(dve, dve.tensor_tensor(cmp, other, mine, ALU.is_equal))

            def equal_before():
                link(dve, dve.tensor_tensor(cmpf, cmpf, tri[:, :].unsqueeze(1).broadcast_to([P, HT, NE * NE]), ALU.mult))

            def count_equal():
                link(dve, dve.tensor_reduce(sc[:, :, :], cmp, AXX, ALU.add))

            def larger_logits():
                link(dve, dve.tensor_tensor(cmp, other, mine, ALU.is_gt))

            def count_larger():
                link(dve, dve.tensor_reduce(rank[:, :, :], cmp, AXX, ALU.add))
                link(dve, dve.tensor_tensor(rank[:, :, :], rank[:, :, :], sc[:, :, :], ALU.add))

            def weigh_scores(half):
                dve.wait_ge(rexp_ready, half + 1)
                link(dve, dve.scalar_tensor_tensor(rex[:, :, :], rank[:, :, :], float(NTOP), rex[:, :, :], ALU.is_lt, ALU.mult))
                link(dve, dve.tensor_reduce(rsm[:, :], rex[:, :, :], AXX, ALU.add))
                link(dve, dve.reciprocal(rsm[:, :], rsm[:, :]))
                dve.tensor_tensor(sc[:, :, :], rex[:, :, :], rsm[:, :].unsqueeze(2).broadcast_to([P, HT, NE]),
                                  ALU.mult).then_inc(sc_ready, 1)
                dve.wait_ge(sc_ready, half + 1)
                link(dve, dve.tensor_scalar(sc64[:, half], sc[:, :, :], 1 / WS, None, ALU.mult))

            def act_fn(half, e, d, after_g=None, after_t=None, early=False):
                gi = half * NE + e
                dve.wait_ge(gu_ready, 4 * gi + 2 * d + 1)
                dve.tensor_scalar(g[d], psum[d][:, :], gub64[:, bass.ds(e, 1), d:d + 1].rearrange("p a c -> p (a c)"),
                                  GLIM * WS, ALU.add, ALU.min).then_inc(g_done, 1)
                if after_g:
                    after_g()
                dve.wait_ge(u_raw, 2 * gi + d + 1)
                dve.tensor_scalar(u[d], u[d], US * (GLIM + 1), US * (1 - GLIM), ALU.min, ALU.max).then_inc(u_done, 1)
                dve.wait_ge(tanh_done, 2 * gi + d + 1)
                dve.scalar_tensor_tensor(tt[d], tt[d], 1.0, g[d], ALU.add, ALU.mult).then_inc(glu_done, 1)
                if after_t:
                    after_t()
                if early or half == 0 and e < POOL_FROM:
                    dve.wait_ge(glu_done, 2 * gi + d + 1)
                    dve.wait_ge(u_done, 2 * gi + d + 1)
                    dve.tensor_tensor(u[d], tt[d], u[d], ALU.mult).then_inc(h_done, 1)

            def add_out(half, e, k):
                gi = half * NE + e
                for j in (2 * k, 2 * k + 1):
                    t = half * HT + j
                    dve.wait_ge(dn_ready, 2 * gi + k + 1)
                    dve.scalar_tensor_tensor(x[:, t, :], psum[4 + k][:, (j % 2) * D:(j % 2 + 1) * D],
                                             sc64[:, half, j, bass.ds(e, 1)], x[:, t, :], ALU.mult, ALU.add).then_inc(acc_done, 1)

            def add_biases(half, k):
                for j in (2 * k, 2 * k + 1):
                    t = half * HT + j
                    dve.wait_ge(bias_mm, 2 * half + j // 2 + 1)
                    dve.tensor_tensor(x[:, t, :], x[:, t, :], psum[6 + j // 2][:, (j % 2) * D:(j % 2 + 1) * D], ALU.add).then_inc(bias_added, 1)
                dve.wait_ge(bias_added, HT * half + 2 * k + 2)

            def expert(half, e, *work, early=False):
                for d in range(2):
                    act_fn(half, e, d, early=early)
                    if d < len(work) and work[d]:
                        work[d]()
                add_out(half, e - 1, 0)
                add_out(half, e - 1, 1)

            def maxima(i, hh):
                for k in range(2):
                    dve.wait_ge(s_ready, 4 * i + 2 * hh + k + 1)
                    dve.tensor_reduce(mx[:, 2 * k:2 * k + 2, bass.ds(2 * i + hh, 1)],
                                      psum[6 + k][:, :].rearrange("p (b c) -> p b c", b=2), AXX, ALU.max).then_inc(mx_done, 1)

            def maxima1(i, hh, c):
                dve.wait_ge(s_ready, 2 * NH + 2 * i + hh + 1)
                dve.tensor_reduce(mx[:, :, bass.ds(2 * i + hh, 1)], psum[BANKS[c]][:, :].rearrange("p (b c) -> p b c", b=NB),
                                  AXX, ALU.max).then_inc(mx_done, 1)

            def maxima_low(half):
                dve.wait_ge(nmx_ready, half + 1)
                dve.tensor_tensor(nm[32:32 + NH, :], nmx, nm[0:NH, :], ALU.subtract).then_inc(nm_ready, 1)

            def outputs(half, i, hh, bank=6):
                n = NH * half + 2 * i + hh
                o = psum[bank][:, 0:NB * VW].rearrange("p (b v) -> p b v", v=VW)
                dve.wait_ge(pv_done, n + 1)
                dve.reciprocal(rs[:, hh, :], o[:, :, HD]).then_inc(rs_done, 1)
                dve.wait_ge(rs_done, n + 1)
                dve.tensor_tensor(ao[:, :, bass.ds((2 * i + hh) * HD, HD)], o[:, :, 0:HD],
                                  rs[:, hh, :].unsqueeze(2).broadcast_to([P, NB, HD]), ALU.mult).then_inc(o_done, 1)

            def add_attention(half):
                for j in range(HT):
                    t = half * HT + j
                    dve.wait_ge(wo_ready, 2 * half + j // 2 + 1)
                    dve.tensor_tensor(x[:, t, :], x[:, t, :], psum[6 + j // 2][:, (j % 2) * D:(j % 2 + 1) * D], ALU.add).then_inc(x3_done, 1)

            rounds = []
            symmetrised(0)
            dve.wait_ge(x1_done, 2)
            normalise(0, 0)
            symmetrised(1)
            low_part(0, 0)
            low_part(0, 1)
            act_fn(0, 0, 0)
            act_fn(0, 0, 1)
            take_logits(0)
            equal_logits()
            act_fn(0, 1, 0)
            equal_before()
            count_equal()
            act_fn(0, 1, 1)
            larger_logits()
            count_larger()
            weigh_scores(0)
            add_out(0, 0, 0)
            add_out(0, 0, 1)
            expert(0, 2)
            expert(0, 3, lambda: add_biases(0, 0), lambda: add_biases(0, 1))
            with dve.Fori(2, 4) as m:
                for s in range(2):
                    expert(0, 2 * m + s, early=True)
            dve.wait_ge(x1_done, 4)
            expert(0, 8, None, lambda: statistics(1, 1))
            expert(0, 9, lambda: normalised(1, 1))
            expert(0, 10, lambda: low_part(1, 0), lambda: low_part(1, 1))
            expert(0, 11, None, lambda: take_logits(1))
            expert(0, 12, equal_logits, equal_before)
            expert(0, 13, count_equal, larger_logits)
            expert(0, 14, count_larger, lambda: weigh_scores(1))
            expert(0, NE - 1)

            def low_queries(half, bank, ms=(0, 1)):
                for m in ms:
                    dve.wait_ge(qhi_ready, 2 * half + m + 1)
                    dve.tensor_tensor(qlo[:, m, :], psum[bank + m][:, :], qhi[:, m, :], ALU.subtract).then_inc(qlo_ready, 1)

            act_fn(1, 0, 0)
            act_fn(1, 0, 1)
            add_biases(1, 0)
            add_biases(1, 1)
            add_out(0, NE - 1, 0)
            add_out(0, NE - 1, 1)
            dve.wait_ge(acc_done, ADDS)
            statistics(0, 2)
            expert(1, 1, lambda: normalised(0, 2))
            expert(1, 2, None, lambda: low_queries(0, 6))
            expert(1, 3)
            with dve.Fori(2, 4) as m:
                for s in range(2):
                    i = 4 * m + 2 * s - 8
                    e = 2 * m + s
                    maxima(i, 0)
                    act_fn(1, e, 0, after_g=lambda: maxima(i, 1))
                    act_fn(1, e, 1, after_g=lambda: maxima(i + 1, 0), after_t=lambda: maxima(i + 1, 1))
                    add_out(1, e - 1, 0)
                    add_out(1, e - 1, 1)
            maxima_low(0)
            with dve.Fori(8, NE) as e:
                act_fn(1, e, 0, after_g=lambda: outputs(0, e - 8, 0))
                act_fn(1, e, 1, after_t=lambda: outputs(0, e - 8, 1))
                add_out(1, e - 1, 0)
                add_out(1, e - 1, 1)
            add_attention(0)

            def column(c, n=KT):
                return cols[:, c:c + n].unsqueeze(2).broadcast_to([P, n, NB])

            def pairs(v):
                return v.rearrange("p (a c) -> p a c", c=NB)

            def product(c, n=NB):
                dve.wait_ge(c_mm, c)
                return psum[5][:, 0:n]

            def centre(src, c, step):
                mean = product(c).unsqueeze(1).broadcast_to([P, KT, NB])
                dve.tensor_tensor(cen[:, :, :], src[:, :, :], mean, ALU.subtract).then_inc(chain_step, 1)
                dve.wait_ge(chain_step, step)
                dve.tensor_tensor(sq[:, :, :], cen[:, :, :], cen[:, :, :], ALU.mult).then_inc(c_v, 1)

            def variance(c):
                dve.tensor_scalar(cvar, product(c), 1e-6, None, ALU.add).then_inc(c_var, 1)

            def scale_columns(ln, step, gcol, bcol, parts=None):
                dve.tensor_tensor(cen[:, :, :], cen[:, :, :], column(gcol), ALU.mult).then_inc(chain_step, 1)
                dve.wait_ge(chain_step, step)
                dve.wait_ge(c_rstd, ln)
                dve.tensor_tensor(nrm[:, :, :], cen[:, :, :], crs.unsqueeze(1).broadcast_to([P, KT, NB]), ALU.mult).then_inc(chain_step, 1)
                dve.wait_ge(chain_step, step + 1)
                if parts is not None:
                    dve.tensor_tensor(parts[:, 0], nrm[:, :, :], column(bcol), ALU.add).then_inc(chain_step, 1)
                dve.tensor_tensor(nrm[:, :, :], nrm[:, :, :], column(bcol), ALU.add).then_inc(c_v if parts is None else chain_step, 1)

            def low_vector(src, parts):
                dve.tensor_tensor(parts[:, 1], src[:, :, :], parts[:, 0], ALU.subtract).then_inc(c_v, 1)

            def gate_sums(half, bank):
                for m in range(2):
                    dve.wait_ge(gate_mm, 2 * half + m + 1)
                    dve.tensor_tensor(zt[half][:, 2 * m:2 * m + 2, :], psum[bank + m][:, :].rearrange("p (b c) -> p b c", b=2),
                                      rows[:, 0:1, :].broadcast_to([P, 2, D]), ALU.add).then_inc(z_ready, 1)

            def first_centred():
                dve.memset(mean4, 1.0 / D)
                dve.memset(chalf, -0.5)
                dve.wait_ge(in_ffn, NFFN)
                dve.wait_ge(xTa_ready, KT * 2)
                dve.tensor_copy(yl[:, :, :], xTb.rearrange("p k (b q) -> p k b q", b=NB)[:, :, :, P - 1]).then_inc(c_v, 1)
                centre(yl, 1, 1)
                variance(2)

            def last_outputs():
                add_out(1, NE - 1, 0)
                add_out(1, NE - 1, 1)

            dve.wait_ge(x3_done, HT)
            normalise(0, 3, yA, last_outputs)
            dve.wait_ge(acc_done, 2 * ADDS)
            normalise(1, 4, None, first_centred)
            scale_columns(1, 2, 0, 2)
            dve.tensor_tensor(th[:, :, :], pairs(product(3, KT * NB)), column(4), ALU.add).then_inc(c_v, 1)

            def thought(k, scaling=None, first=None, gelu=None, second=None, after=None):
                centre(th, 4 * k + 4, 6 * k + 4)
                variance(4 * k + 5)
                if scaling:
                    scaling()
                scale_columns(k + 2, 6 * k + 5, 6, 8, nrm16)
                dve.wait_ge(chain_step, 6 * k + 8)
                low_vector(nrm, nrm16)
                if first:
                    first()
                dve.scalar_tensor_tensor(act8[:, :, :], pairs(product(4 * k + 6, HID // P * NB)), 1 / WS, column(12, HID // P),
                                         ALU.mult, ALU.add).then_inc(c_gelu, 1)
                dve.tensor_tensor(th[:, :, :], th[:, :, :], column(10), ALU.add).then_inc(chain_step, 1)
                if gelu:
                    gelu()
                dve.wait_ge(gelu_done, 2 * k + 2)
                dve.wait_ge(chain_step, 6 * k + 9)
                low_vector(act8, act16)
                if second:
                    second()
                dve.scalar_tensor_tensor(th[:, :, :], pairs(product(4 * k + 7, KT * NB)), 1 / WS, th[:, :, :],
                                         ALU.mult, ALU.add).then_inc(c_v, 1)
                if after:
                    after()

            def more_maxima(first, last):
                for c in range(first, last):
                    maxima1(4 * k + c // 2 - 8, c % 2, c % 4)

            thought(0, first=lambda: low_queries(1, 6, (0,)), second=lambda: low_queries(1, 6, (1,)))
            thought(1, after=lambda: gate_sums(0, 2))
            with dve.Fori(2, STEPS) as k:
                thought(k, lambda: more_maxima(0, 2), lambda: more_maxima(2, 4), None, lambda: more_maxima(4, 6),
                        lambda: more_maxima(6, 8))
            maxima_low(1)
            product(4 * STEPS + 4)
            for m in range(2):
                dve.tensor_tensor(brow[:, 2 * m:2 * m + 2, :], psum[2 + m][:, :].rearrange("p (b c) -> p b c", b=2),
                                  rows[:, 3:4, :].broadcast_to([P, 2, D]), ALU.add).then_inc(brow_ready, 1)
            def gated(half, y, dst, m, op):
                two = slice(2 * m, 2 * m + 2)
                if op == 0:
                    dve.wait_ge(gate_ready, 2 * half + m + 1)
                    link(dve, dve.scalar_tensor_tensor(dst[:, two, :], zt[half][:, two, :], 1.0, brow[:, two, :], ALU.add, ALU.mult))
                else:
                    link(dve, dve.scalar_tensor_tensor(dst[:, two, :], dst[:, two, :], 0.5, y[:, two, :], ALU.mult, ALU.add))

            def tile_stats(src, j, o=0):
                return dve.bn_stats(bn[:, o + j, :], src[:, j, :])

            def stats_end(o, eps):
                for j in range(HT):
                    ins = dve.bn_aggr(mv[:, o + j, :], bn[:, o + j, :])
                link(dve, ins)
                dve.tensor_scalar(vare[:, o:o + HT], mv[:, o:o + HT, 1], eps, None, ALU.add).then_inc(vare_ready, 1)

            dve.wait_ge(brow_ready, 2)
            for n in range(NH):
                outputs(1, n // 2, n % 2, LANES[n % 8])
                if 2 <= n < 6:
                    gated(0, yA, gsumA, (n - 2) // 2, n % 2)
                if 6 <= n < 10:
                    ins = tile_stats(gsumA, n - 6, HT)
                if n == 9:
                    link(dve, ins)
                    stats_end(HT, 1e-6)
            for m in range(2):
                for j in (2 * m, 2 * m + 1):
                    t = HT + j
                    dve.wait_ge(wo_ready, 2 + m + 1)
                    dve.tensor_tensor(x[:, t, :], x[:, t, :], psum[6 + m][:, (j % 2) * D:(j % 2 + 1) * D], ALU.add).then_inc(x3_done, 1)
                for j in (2 * m, 2 * m + 1):
                    dve.wait_ge(x3_done, HT + j + 1)
                    ins = tile_stats(x[:, HT:NT], j)
            link(dve, ins)
            stats_end(0, 1e-5)
            dve.wait_ge(rstd_ready, 8)
            for j in range(HT):
                dve.tensor_scalar(yB[:, j, :], x[:, HT + j, :], mv[:, j, 0:1], rstd[:, j:j + 1], ALU.subtract, ALU.mult).then_inc(xn_ready, 1)
            dve.wait_ge(xn_ready, HT * 6)
            for j in range(HT):
                ins = dve.tensor_tensor(x[:, HT + j, :], x[:, HT + j, :], rows[:, 2, :], ALU.add)
            link(dve, ins)
            def gate_sum(m):
                dve.wait_ge(gate_mm, 2 + m + 1)
                dve.tensor_tensor(zt[1][:, 2 * m:2 * m + 2, :], psum[m][:, :].rearrange("p (b c) -> p b c", b=2),
                                  rows[:, 0:1, :].broadcast_to([P, 2, D]), ALU.add).then_inc(z_ready, 1)

            gate_sum(0)
            gated(1, yB, gsum, 0, 0)
            gate_sum(1)
            gated(1, yB, gsum, 0, 1)
            for j in (0, 1):
                tile_stats(gsum, j)
            gated(1, yB, gsum, 1, 0)
            gated(1, yB, gsum, 1, 1)
            for j in (2, 3):
                ins = tile_stats(gsum, j)
            link(dve, ins)
            stats_end(0, 1e-6)
            dve.wait_ge(rstd_ready, 9)
            for j in range(HT + 1):
                if j < HT:
                    dve.scalar_tensor_tensor(gsum[:, j, :], gsum[:, j, :], mv[:, j, 0:1], rows[:, 1, :],
                                             ALU.subtract, ALU.mult).then_inc(centred_ready, 1)
                if j:
                    t = HT + j - 1
                    dve.wait_ge(centred_ready, j)
                    dve.scalar_tensor_tensor(x[:, t, :], gsum[:, j - 1, :], rstd[:, j - 1:j], x[:, t, :], ALU.mult, ALU.add).then_inc(fin_ready[1], 1)


def kernel(**inputs):
    import numpy as np
    import concourse.bacc as bacc
    from concourse.bass_utils import run_bass_kernel_spmd as run

    I = {k: np.asarray(v) for k, v in inputs.items()}
    f = np.float32

    def tiles(w):
        return np.ascontiguousarray(w.reshape(-1, P, w.shape[-1]).transpose(1, 0, 2))

    def spread(v):
        return np.ascontiguousarray(np.broadcast_to(v.reshape(1, -1), (P, v.size)))

    def column(v):
        return v.reshape(-1, P).T

    xs = I["x"].reshape(NB, 2, P, D)[:, ::-1].transpose(2, 1, 0, 3).reshape(P, NT, D)
    gu = I["L0_ffn_gate_up_proj"].reshape(NE, KT, P, D, 2).transpose(0, 2, 1, 4, 3).reshape(NE, P, KT * 2 * D)
    dn = I["L0_ffn_down_proj"].reshape(NE, KT, P, D).transpose(0, 2, 1, 3).reshape(NE, P, KT * D)
    gb = I["L0_ffn_gate_up_proj_bias"].reshape(NE, 2, P, 2).transpose(2, 0, 3, 1).reshape(P, NE, 4)
    i = np.arange(P)
    up = np.where(i[None, :] > i[:, None], f(NEG), f(0))
    e = np.arange(NE)
    group = i // HD % 4
    pair = np.arange(NH // 4)
    head = 2 * pair[:, None] + i[None, :] // 64
    row = head * HD + i[None, :] % HD
    qselect, kselect = (np.stack([(i[:, None, None] == row[None]) * (np.isin(group, groups)) for groups in parts], 1)
                        .astype(f).reshape(P, -1) for parts in (((0, 2), (1,)), ((0, 1), (2,))))
    pick = np.where(i[:, None] % 32 == e[None, :], f(1), f(0)) * (i[:, None] < 64)
    pick = pick.astype(f)

    arrays = {
        "x": xs, "ctxT": I["ctx_512"].reshape(-1, CD).T,
        "wqk0": np.concatenate([I["L0_xattn_Wq"].T, I["L0_xattn_Wk"].T], 1),
        "gamma": np.broadcast_to(I["L0_xattn_gamma_raw"].reshape(1, 1), (P, 1)),
        "ident": np.eye(P, dtype=f), "masks": np.stack([up, up.T], 1).astype(f),
        "mhalf": np.full((P, NT), -0.5, f),
        "pick": pick, "wk": I["L1_xattn_Wkv_expand"][:D].T, "kselect": kselect, "wq": tiles(I["L1_xattn_Wq"].T),
        "select": qselect,
        "wv": I["L1_xattn_Wkv_expand"][D:].T, "wout": tiles(I["L1_xattn_Wout"].T),
        "d1": tiles(I["L1_ffn_d1_w"]), "d2": tiles(I["L1_ffn_d2_w"]), "aggw": tiles(I["L1_ffn_agg_w"]),
        "bcw": tiles(I["L1_ffn_bc_w"]), "gatew": tiles(I["L1_ffn_gate_w"]),
        "rows": np.stack([spread(I[n]) for n in ("L1_ffn_gate_b", "L1_ffn_out_gamma", "L1_ffn_out_beta", "L1_ffn_bc_b")], 1),
        "cols": np.concatenate([column(I["L1_ffn_" + n]) for n in ("in_gamma", "in_beta", "agg_b", "pn_gamma", "pn_beta", "d2_b", "d1_b")]
                               + [np.zeros((P, 32 - 20), f)], 1),
        "rbias": spread(I["L0_ffn_router_bias"]), "gub": gb,
        "tri": spread((e[None, :] < e[:, None]).astype(f)),
        "rw": tiles(I["L0_ffn_router_weight"].T), "bdown": I["L0_ffn_down_proj_bias"],
        "w_exp": np.concatenate([gu, dn], 2),
    }
    arrays = {k: np.ascontiguousarray(v) for k, v in arrays.items()}
    nc = bacc.Bacc("TRN2", target_bir_lowering=False, num_devices=1)
    args = {k: nc.dram_tensor(f"in_{k}", v.shape, mybir.dt.from_np(v.dtype), kind="ExternalInput").ap() for k, v in arrays.items()}
    args["out"] = nc.dram_tensor("out_x", (P, NT, D), F32, kind="ExternalOutput").ap()
    chip_program(nc, args)
    r = run(nc, [{f"in_{k}": v for k, v in arrays.items()}], core_ids=[0])
    out = r.results[0]["out_x"]
    return np.ascontiguousarray(out.reshape(P, 2, NB, D).transpose(2, 1, 0, 3)[:, ::-1].reshape(NB, SEQ, D))
```
